# Optimizing a Trainium2 kernel written in Bass

```python
import numpy as np
import jax
import jax.numpy as jnp

def _softmax(x, axis=-1):
    return jax.nn.softmax(x, axis=axis)

def _gelu(x):
    return jax.nn.gelu(x, approximate=True)

def _silu(x):
    return jax.nn.silu(x)

def _sigmoid(x):
    return jax.nn.sigmoid(x)

def _layernorm(x, axis=-1, eps=1e-05):
    m = jnp.mean(x, axis=axis, keepdims=True)
    v = jnp.var(x, axis=axis, keepdims=True)
    return (x - m) / jnp.sqrt(v + eps)

def _scatter_add(tgt, idx, src, axis=0):
    return tgt.at[idx].add(src)

def _segment_sum(src, seg, n):
    return jax.ops.segment_sum(src, seg, n)
kernel_name = 'mk_xattn_seq_d2_seqx_r8_c1c2a3'

def setup_inputs(seed: int=0):
    np.random.seed(seed)
    _w = jnp.asarray

    def _rec_inputs():
        import jax
        import jax.numpy as jnp
        _rk = jax.random.key(seed)
        x = -0.0001108 + 0.9999 * jax.random.normal(jax.random.fold_in(_rk, 1), (128, 64, 160), jnp.float32)
        _lenS = 64 - jax.random.randint(jax.random.fold_in(_rk, 7), (128,), 0, max(1, 64 // 4) + 1, jnp.int32)
        _lenS2 = 64 - jax.random.randint(jax.random.fold_in(_rk, 8), (128,), 0, max(1, 64 // 4) + 1, jnp.int32)
        _ctx_2048P = jax.random.normal(jax.random.fold_in(_rk, 11), (128, 16, 256), jnp.float32)
        _ctx_2048c = jax.random.dirichlet(jax.random.fold_in(_rk, 511), 0.3 * jnp.ones((16,), jnp.float32), (128, 64))
        _ctx_2048t = jnp.einsum('bsk,bkd->bsd', _ctx_2048c, _ctx_2048P)
        _ctx_2048t = _ctx_2048t * jax.lax.rsqrt(jnp.mean(jnp.square(_ctx_2048t)) + 1e-12) * 0.953939
        ctx_2048 = -0.000395056 + 1.00006 * (_ctx_2048t + 0.3 * jax.random.normal(jax.random.fold_in(_rk, 611), (128, 64, 256), jnp.float32))
        return (x, ctx_2048)
    x, ctx_2048 = _rec_inputs()

    def _L0_xattn_setup():
        import jax, jax.numpy as jnp
        import numpy as np
        NUM_HEADS = 20
        TEXT_LEN = 77
        IP_SCALE = 1.0

        def _attend(q, k, v, sm_scale):
            scores = jnp.einsum('bhsd,bhld->bhsl', q, k) * sm_scale
            probs = jax.nn.softmax(scores, axis=-1)
            return jnp.einsum('bhsl,bhld->bhsd', probs, v)

        def _split_heads(x, h):
            b, s, c = x.shape
            return x.reshape(b, s, h, c // h).transpose(0, 2, 1, 3)

        def _merge_heads(x):
            b, h, s, d = x.shape
            return x.transpose(0, 2, 1, 3).reshape(b, s, h * d)
        key = jax.random.key(seed)
        ks = jax.random.split(key, 8)
        B, S, C, CC, L = (8, 512, 160, 256, TEXT_LEN + 4)
        sd_q = 1.0 / np.sqrt(C)
        sd_kv = 1.0 / np.sqrt(CC)
        return {'hidden_states': jax.random.normal(ks[0], (B, S, C), jnp.float32), 'encoder_hidden_states': jax.random.normal(ks[1], (B, L, CC), jnp.float32), 'Wq': jax.random.normal(ks[2], (C, C), jnp.float32) * sd_q, 'Wk': jax.random.normal(ks[3], (C, CC), jnp.float32) * sd_kv, 'Wv': jax.random.normal(ks[4], (C, CC), jnp.float32) * sd_kv, 'Wk_ip': jax.random.normal(ks[5], (C, CC), jnp.float32) * sd_kv, 'Wv_ip': jax.random.normal(ks[6], (C, CC), jnp.float32) * sd_kv, 'Wo': jax.random.normal(ks[7], (C, C), jnp.float32) * sd_q, 'bo': jnp.zeros((C,), jnp.float32)}
    _L0_xattn_all = _L0_xattn_setup()
    _L0_xattn_in = {k: v for k, v in _L0_xattn_all.items() if k in ('Wq', 'Wk', 'Wv', 'Wk_ip', 'Wv_ip', 'Wo', 'bo')}
    del _L0_xattn_all

    def _L1_xattn_setup():
        import jax, jax.numpy as jnp
        import numpy as np
        DIM = 160
        HEADS = 20
        DHEAD = 64
        CTX_DIM = 256
        INNER = HEADS * DHEAD
        FF_INNER = 4 * DIM
        SCALE = DHEAD ** (-0.5)
        EPS = 1e-05

        def _layer_norm(x, g, b):
            m = jnp.mean(x, axis=-1, keepdims=True)
            v = jnp.mean(jnp.square(x - m), axis=-1, keepdims=True)
            return (x - m) * jax.lax.rsqrt(v + EPS) * g + b

        def _attention(x, ctx, wq, wk, wv, wo, bo):
            B, N, _ = x.shape
            M = ctx.shape[1]
            q = (x @ wq).reshape(B, N, HEADS, DHEAD).transpose(0, 2, 1, 3)
            k = (ctx @ wk).reshape(B, M, HEADS, DHEAD).transpose(0, 2, 1, 3)
            v = (ctx @ wv).reshape(B, M, HEADS, DHEAD).transpose(0, 2, 1, 3)
            sim = jnp.einsum('bhid,bhjd->bhij', q, k) * SCALE
            attn = jax.nn.softmax(sim, axis=-1)
            out = jnp.einsum('bhij,bhjd->bhid', attn, v)
            out = out.transpose(0, 2, 1, 3).reshape(B, N, INNER)
            return out @ wo + bo

        def _geglu_ff(x, w1, b1, w2, b2):
            h = x @ w1 + b1
            a, gate = jnp.split(h, 2, axis=-1)
            return a * jax.nn.gelu(gate, approximate=False) @ w2 + b2
        key = jax.random.key(seed)
        ks = jax.random.split(key, 16)
        s = 0.02
        d = {'x': jax.random.normal(ks[0], (2, 256, DIM), jnp.float32), 'context': jax.random.normal(ks[1], (2, 77, CTX_DIM), jnp.float32), 'a1_wq': jax.random.normal(ks[2], (DIM, INNER), jnp.float32) * s, 'a1_wk': jax.random.normal(ks[3], (DIM, INNER), jnp.float32) * s, 'a1_wv': jax.random.normal(ks[4], (DIM, INNER), jnp.float32) * s, 'a1_wo': jax.random.normal(ks[5], (INNER, DIM), jnp.float32) * s, 'a1_bo': jnp.zeros((DIM,), jnp.float32), 'a2_wq': jax.random.normal(ks[6], (DIM, INNER), jnp.float32) * s, 'a2_wk': jax.random.normal(ks[7], (CTX_DIM, INNER), jnp.float32) * s, 'a2_wv': jax.random.normal(ks[8], (CTX_DIM, INNER), jnp.float32) * s, 'a2_wo': jax.random.normal(ks[9], (INNER, DIM), jnp.float32) * s, 'a2_bo': jnp.zeros((DIM,), jnp.float32), 'ff_w1': jax.random.normal(ks[10], (DIM, 2 * FF_INNER), jnp.float32) * s, 'ff_b1': jnp.zeros((2 * FF_INNER,), jnp.float32), 'ff_w2': jax.random.normal(ks[11], (FF_INNER, DIM), jnp.float32) * s, 'ff_b2': jnp.zeros((DIM,), jnp.float32), 'ln1_g': jnp.ones((DIM,), jnp.float32), 'ln1_b': jnp.zeros((DIM,), jnp.float32), 'ln2_g': jnp.ones((DIM,), jnp.float32), 'ln2_b': jnp.zeros((DIM,), jnp.float32), 'ln3_g': jnp.ones((DIM,), jnp.float32), 'ln3_b': jnp.zeros((DIM,), jnp.float32)}
        return d
    _L1_xattn_all = _L1_xattn_setup()
    _L1_xattn_in = {k: v for k, v in _L1_xattn_all.items() if k in ('a1_wq', 'a1_wk', 'a1_wv', 'a1_wo', 'a1_bo', 'a2_wq', 'a2_wk', 'a2_wv', 'a2_wo', 'a2_bo', 'ff_w1', 'ff_b1', 'ff_w2', 'ff_b2', 'ln1_g', 'ln1_b', 'ln2_g', 'ln2_b', 'ln3_g', 'ln3_b')}
    del _L1_xattn_all
    return {'x': x, 'ctx_2048': ctx_2048, 'L0_xattn_Wq': _L0_xattn_in['Wq'], 'L0_xattn_Wk': _L0_xattn_in['Wk'], 'L0_xattn_Wv': _L0_xattn_in['Wv'], 'L0_xattn_Wk_ip': _L0_xattn_in['Wk_ip'], 'L0_xattn_Wv_ip': _L0_xattn_in['Wv_ip'], 'L0_xattn_Wo': _L0_xattn_in['Wo'], 'L0_xattn_bo': _L0_xattn_in['bo'], 'L1_xattn_a1_wq': _L1_xattn_in['a1_wq'], 'L1_xattn_a1_wk': _L1_xattn_in['a1_wk'], 'L1_xattn_a1_wv': _L1_xattn_in['a1_wv'], 'L1_xattn_a1_wo': _L1_xattn_in['a1_wo'], 'L1_xattn_a1_bo': _L1_xattn_in['a1_bo'], 'L1_xattn_a2_wq': _L1_xattn_in['a2_wq'], 'L1_xattn_a2_wk': _L1_xattn_in['a2_wk'], 'L1_xattn_a2_wv': _L1_xattn_in['a2_wv'], 'L1_xattn_a2_wo': _L1_xattn_in['a2_wo'], 'L1_xattn_a2_bo': _L1_xattn_in['a2_bo'], 'L1_xattn_ff_w1': _L1_xattn_in['ff_w1'], 'L1_xattn_ff_b1': _L1_xattn_in['ff_b1'], 'L1_xattn_ff_w2': _L1_xattn_in['ff_w2'], 'L1_xattn_ff_b2': _L1_xattn_in['ff_b2'], 'L1_xattn_ln1_g': _L1_xattn_in['ln1_g'], 'L1_xattn_ln1_b': _L1_xattn_in['ln1_b'], 'L1_xattn_ln2_g': _L1_xattn_in['ln2_g'], 'L1_xattn_ln2_b': _L1_xattn_in['ln2_b'], 'L1_xattn_ln3_g': _L1_xattn_in['ln3_g'], 'L1_xattn_ln3_b': _L1_xattn_in['ln3_b']}

def reference(x, ctx_2048, L0_xattn_Wq, L0_xattn_Wk, L0_xattn_Wv, L0_xattn_Wk_ip, L0_xattn_Wv_ip, L0_xattn_Wo, L0_xattn_bo, L1_xattn_a1_wq, L1_xattn_a1_wk, L1_xattn_a1_wv, L1_xattn_a1_wo, L1_xattn_a1_bo, L1_xattn_a2_wq, L1_xattn_a2_wk, L1_xattn_a2_wv, L1_xattn_a2_wo, L1_xattn_a2_bo, L1_xattn_ff_w1, L1_xattn_ff_b1, L1_xattn_ff_w2, L1_xattn_ff_b2, L1_xattn_ln1_g, L1_xattn_ln1_b, L1_xattn_ln2_g, L1_xattn_ln2_b, L1_xattn_ln3_g, L1_xattn_ln3_b):
    import jax
    import jax.numpy as jnp

    def _L0_xattn_ref(hidden_states, encoder_hidden_states, Wq, Wk, Wv, Wk_ip, Wv_ip, Wo, bo):
        import jax, jax.numpy as jnp
        import numpy as np
        NUM_HEADS = 20
        TEXT_LEN = 77
        IP_SCALE = 1.0

        def _attend(q, k, v, sm_scale):
            scores = jnp.einsum('bhsd,bhld->bhsl', q, k) * sm_scale
            probs = jax.nn.softmax(scores, axis=-1)
            return jnp.einsum('bhsl,bhld->bhsd', probs, v)

        def _split_heads(x, h):
            b, s, c = x.shape
            return x.reshape(b, s, h, c // h).transpose(0, 2, 1, 3)

        def _merge_heads(x):
            b, h, s, d = x.shape
            return x.transpose(0, 2, 1, 3).reshape(b, s, h * d)
        residual = hidden_states
        B, S, C = hidden_states.shape
        H = NUM_HEADS
        D = C // H
        sm_scale = 1.0 / jnp.sqrt(jnp.asarray(D, hidden_states.dtype))
        text = encoder_hidden_states[:, :TEXT_LEN, :]
        ip = encoder_hidden_states[:, TEXT_LEN:, :]
        q = _split_heads(hidden_states @ Wq.T, H)
        k = _split_heads(text @ Wk.T, H)
        v = _split_heads(text @ Wv.T, H)
        out_text = _merge_heads(_attend(q, k, v, sm_scale))
        k_ip = _split_heads(ip @ Wk_ip.T, H)
        v_ip = _split_heads(ip @ Wv_ip.T, H)
        out_ip = _merge_heads(_attend(q, k_ip, v_ip, sm_scale))
        out = out_text + IP_SCALE * out_ip
        out = out @ Wo.T + bo
        return out + residual

    def _L1_xattn_ref(x, context, a1_wq, a1_wk, a1_wv, a1_wo, a1_bo, a2_wq, a2_wk, a2_wv, a2_wo, a2_bo, ff_w1, ff_b1, ff_w2, ff_b2, ln1_g, ln1_b, ln2_g, ln2_b, ln3_g, ln3_b):
        import jax, jax.numpy as jnp
        import numpy as np
        DIM = 160
        HEADS = 20
        DHEAD = 64
        CTX_DIM = 256
        INNER = HEADS * DHEAD
        FF_INNER = 4 * DIM
        SCALE = DHEAD ** (-0.5)
        EPS = 1e-05

        def _layer_norm(x, g, b):
            m = jnp.mean(x, axis=-1, keepdims=True)
            v = jnp.mean(jnp.square(x - m), axis=-1, keepdims=True)
            return (x - m) * jax.lax.rsqrt(v + EPS) * g + b

        def _attention(x, ctx, wq, wk, wv, wo, bo):
            B, N, _ = x.shape
            M = ctx.shape[1]
            q = (x @ wq).reshape(B, N, HEADS, DHEAD).transpose(0, 2, 1, 3)
            k = (ctx @ wk).reshape(B, M, HEADS, DHEAD).transpose(0, 2, 1, 3)
            v = (ctx @ wv).reshape(B, M, HEADS, DHEAD).transpose(0, 2, 1, 3)
            sim = jnp.einsum('bhid,bhjd->bhij', q, k) * SCALE
            attn = jax.nn.softmax(sim, axis=-1)
            out = jnp.einsum('bhij,bhjd->bhid', attn, v)
            out = out.transpose(0, 2, 1, 3).reshape(B, N, INNER)
            return out @ wo + bo

        def _geglu_ff(x, w1, b1, w2, b2):
            h = x @ w1 + b1
            a, gate = jnp.split(h, 2, axis=-1)
            return a * jax.nn.gelu(gate, approximate=False) @ w2 + b2
        n = _layer_norm(x, ln1_g, ln1_b)
        x = x + _attention(n, n, a1_wq, a1_wk, a1_wv, a1_wo, a1_bo)
        n = _layer_norm(x, ln2_g, ln2_b)
        x = x + _attention(n, context, a2_wq, a2_wk, a2_wv, a2_wo, a2_bo)
        x = _geglu_ff(_layer_norm(x, ln3_g, ln3_b), ff_w1, ff_b1, ff_w2, ff_b2) + x
        return x
    x = _L0_xattn_ref(x, ctx_2048, L0_xattn_Wq, L0_xattn_Wk, L0_xattn_Wv, L0_xattn_Wk_ip, L0_xattn_Wv_ip, L0_xattn_Wo, L0_xattn_bo)
    x = _L1_xattn_ref(x, ctx_2048, L1_xattn_a1_wq, L1_xattn_a1_wk, L1_xattn_a1_wv, L1_xattn_a1_wo, L1_xattn_a1_bo, L1_xattn_a2_wq, L1_xattn_a2_wk, L1_xattn_a2_wv, L1_xattn_a2_wo, L1_xattn_a2_bo, L1_xattn_ff_w1, L1_xattn_ff_b1, L1_xattn_ff_w2, L1_xattn_ff_b2, L1_xattn_ln1_g, L1_xattn_ln1_b, L1_xattn_ln2_g, L1_xattn_ln2_b, L1_xattn_ln3_g, L1_xattn_ln3_b)
    return x

_drawn_inputs = setup_inputs


def setup_inputs(seed=0):
    import zlib

    import numpy as np

    out = dict(_drawn_inputs(seed))
    spreads = {'L0_xattn_bo': (0.0, 0.1),
     'L1_xattn_a1_bo': (0.0, 0.1),
     'L1_xattn_a2_bo': (0.0, 0.1),
     'L1_xattn_ff_b1': (0.0, 0.8),
     'L1_xattn_ff_b2': (0.0, 0.1),
     'L1_xattn_ln1_g': (1.0, 0.6),
     'L1_xattn_ln1_b': (0.0, 0.477),
     'L1_xattn_ln2_g': (1.0, 0.6),
     'L1_xattn_ln2_b': (0.0, 0.8),
     'L1_xattn_ln3_g': (1.0, 0.6),
     'L1_xattn_ln3_b': (0.0, 0.8)}
    factors = {'L1_xattn_a1_wq': 8.0,
     'L1_xattn_a1_wk': 8.0,
     'L1_xattn_a2_wq': 8.0,
     'L1_xattn_a2_wk': 8.0,
     'L1_xattn_ff_w1': 3.279,
     'L1_xattn_ff_w2': 3.234}
    for name, (base, spread) in spreads.items():
        noise = np.random.default_rng([zlib.crc32(name.encode()), seed]).standard_normal(out[name].shape)
        drawn = base * np.exp(spread * noise) if base else spread * noise
        out[name] = jnp.asarray(drawn.astype(out[name].dtype))
    for name, factor in factors.items():
        out[name] = (out[name] * factor).astype(out[name].dtype)
    return out
```

```python
from contextlib import ExitStack

import numpy as np
from concourse import mybir
import concourse.bass as bass

F32 = mybir.dt.float32
F32R = mybir.dt.float32r
ALU = mybir.AluOpType
ACT = mybir.ActivationFunctionType
AX = mybir.AxisListType

P = 128
SEQS, SEQ, DIM, CTX = 128, 64, 160, 256
TOKENS = SEQS * SEQ
TILES = 4
GROUP = TILES * P
GROUPS = TOKENS // GROUP
REM = DIM - P
COPIES = P // REM
HEADS = 20
INNER = HEADS * 64
UNITS = 10
BLOCKS = 8
EPS = 1e-5
FF = 640
FF_CHUNKS = FF // P


def back(g, u, n):
    return (g, u - n) if u >= n else (g - 1, u - n + UNITS)


def real(g):
    return not (isinstance(g, int) and g < 0)


def over_groups(engine, body):
    body(0, True, False, True)
    body(1, True, True, True)
    with engine.Fori(2, GROUPS - 1) as g:
        body(g, True, True, True)
    body(GROUPS - 1, True, True, False)
    body(GROUPS, False, True, False)


class Loads:

    def __init__(self, nc):
        self.staged = [nc.alloc_semaphore(f"w_staged{i}") for i in range(2)]
        self.rounded = nc.alloc_semaphore("w_rounded")
        self.split = nc.alloc_semaphore("w_split")
        self.loaded = nc.alloc_semaphore("w_loaded")
        self.arrivals, self.jobs, self.plain = [0, 0], 0, 0


def split_weights(nc, tag, loads, jobs, plain):
    with ExitStack() as ctx:
        width = max(w for _, w, _, _ in jobs)
        stage = [ctx.enter_context(nc.sbuf_tensor(f"{tag}_stage{i}", [P, width], F32)) for i in range(2)]
        before, arrived = loads.jobs, []
        for n, (_, _, _, lo) in enumerate(jobs):
            loads.arrivals[n % 2] += 16 * (COPIES if lo is None else 1)
            arrived.append(loads.arrivals[n % 2])
        loads.jobs += len(jobs)
        loads.plain += 16 * len(plain)
        block = ctx.enter_context(nc.Block())

        @block.sync
        def _(sp):
            for n, (source, w, hi, lo) in enumerate(jobs):
                if n >= 2:
                    sp.wait_ge(loads.split, before + n - 1)
                if lo is None:
                    for c in range(COPIES):
                        sp.dma_start(stage[n % 2][c * REM:(c + 1) * REM, 0:w], source)\
                          .then_inc(loads.staged[n % 2], 16)
                else:
                    sp.dma_start(stage[n % 2][:, 0:w], source).then_inc(loads.staged[n % 2], 16)

        @block.gpsimd
        def _(pool):
            for tile, source in plain:
                pool.dma_start(tile, source).then_inc(loads.loaded, 16)
            pool.wait_ge(loads.loaded, loads.plain)

        @block.scalar
        def _(act):
            for n, (source, w, hi, lo) in enumerate(jobs):
                act.wait_ge(loads.staged[n % 2], arrived[n])
                act.activation(hi, stage[n % 2][:, 0:w], ACT.Copy).then_inc(loads.rounded, 1)

        @block.vector
        def _(dve):
            for n, (source, w, hi, lo) in enumerate(jobs):
                dve.wait_ge(loads.rounded, before + n + 1)
                if lo is None:
                    for r in (REM, 3 * REM):
                        part = dve.tensor_tensor(hi[r:r + REM, :], stage[n % 2][r:r + REM, 0:w],
                                                 hi[r:r + REM, :].bitcast(F32), ALU.subtract)
                else:
                    part = dve.tensor_tensor(lo, stage[n % 2][:, 0:w], hi.bitcast(F32), ALU.subtract)
                part.then_inc(loads.split, 1)


def row(v):
    return v.rearrange("(a n) -> a n", a=1).broadcast_to([P, v.shape[0]])


class Softmax:

    def __init__(self, nc, ctx, tag):
        def sem(name):
            return nc.alloc_semaphore(f"{tag}_{name}")

        def sb(name, shape):
            return ctx.enter_context(nc.sbuf_tensor(f"{tag}_{name}", shape, F32))

        def pb(name):
            return ctx.enter_context(nc.psum_tensor(f"{tag}_{name}", [P, 512], F32))

        self.scores = [pb(f"scores{i}") for i in range(2)]
        self.turned = [pb(f"turned{i}") for i in range(2)]
        self.out = pb("out")
        self.y = pb("y")
        self.proj = [pb(f"proj{i}") for i in range(2)]
        self.top = sb("top", [P, 2, BLOCKS])
        self.total = sb("total", [P, 2, BLOCKS])
        self.inverse = sb("inverse", [P, 2, BLOCKS])
        self.own = sb("own", [P, 2])
        self.factor = sb("factor", [P, 2, BLOCKS, 2])
        self.e = [sb(f"e{i}", [P, BLOCKS, 64]) for i in range(2)]
        self.prob = [sb(f"prob{i}", [P, BLOCKS, P]) for i in range(2)]
        self.probT = [sb(f"probT{i}", [P, BLOCKS, P]) for i in range(2)]
        self.scored = sem("scored")
        self.topped = sem("topped")
        self.shifted = sem("shifted")
        self.exped = sem("exped")
        self.summed = sem("summed")
        self.inverted = sem("inverted")
        self.factored = sem("factored")
        self.normed = sem("normed")
        self.transposed = sem("transposed")
        self.copied_a = sem("copied_a")
        self.copied_b = sem("copied_b")
        self.valued = sem("valued")
        self.set = sem("set")

    def constants(self, dve):
        for b in range(2):
            for c in range(2):
                dve.memset(self.own[b * 64:(b + 1) * 64, c:c + 1], float(b == c)).then_inc(self.set, 1)
        dve.wait_ge(self.set, 4)

    def maximum_and_shift(self, dve, g, u):
        r, s = u % 2, self.scores[u % 2][:].rearrange("p (k j) -> p k j", j=64)
        g2, u2 = back(g, u, 2)
        dve.wait_ge(self.scored, g * UNITS + u + 1)
        if real(g2):
            dve.wait_ge(self.shifted, g2 * UNITS + u2 + 1)
        dve.tensor_reduce(self.top[:, r, :], s, axis=AX.X, op=ALU.max).then_inc(self.topped, 1)
        dve.wait_ge(self.topped, g * UNITS + u + 1)
        if real(g2):
            dve.wait_ge(self.normed, g2 * UNITS + u2 + 1)
        dve.tensor_tensor(self.e[r][:], s, self.top[:, r, :].unsqueeze(2).broadcast_to([P, BLOCKS, 64]),
                          ALU.subtract).then_inc(self.shifted, 1)

    def sum_and_invert(self, dve, g, u):
        r = u % 2
        g2, u2 = back(g, u, 2)
        dve.wait_ge(self.exped, g * UNITS + u + 1)
        dve.tensor_reduce(self.total[:, r, :], self.e[r][:], axis=AX.X, op=ALU.add).then_inc(self.summed, 1)
        dve.wait_ge(self.summed, g * UNITS + u + 1)
        dve.reciprocal(self.inverse[:, r, :], self.total[:, r, :]).then_inc(self.inverted, 1)
        dve.wait_ge(self.inverted, g * UNITS + u + 1)
        if real(g2):
            dve.wait_ge(self.normed, g2 * UNITS + u2 + 1)
        dve.tensor_tensor(self.factor[:, r, :, :], self.inverse[:, r, :].unsqueeze(2).broadcast_to([P, BLOCKS, 2]),
                          self.own[:].unsqueeze(1).broadcast_to([P, BLOCKS, 2]), ALU.mult).then_inc(self.factored, 1)

    def copy_b(self, dve, g, u):
        g2, u2 = back(g, u, 2)
        dve.wait_ge(self.transposed, 2 * (g * UNITS + u) + 2)
        if real(g2):
            dve.wait_ge(self.valued, g2 * UNITS + u2 + 1)
        dve.tensor_copy(self.probT[u % 2][:, 4:8, :], self.turned[1][:].rearrange("p (k i) -> p k i", i=P))\
           .then_inc(self.copied_b, 1)

    def exponential(self, act, g, u, scale):
        act.wait_ge(self.shifted, g * UNITS + u + 1)
        act.activation(self.e[u % 2][:], self.e[u % 2][:], ACT.Exp, scale=scale).then_inc(self.exped, 1)

    def copy_a(self, act, g, u):
        g2, u2 = back(g, u, 2)
        act.wait_ge(self.transposed, 2 * (g * UNITS + u) + 1)
        if real(g2):
            act.wait_ge(self.valued, g2 * UNITS + u2 + 1)
        act.activation(self.probT[u % 2][:, 0:4, :], self.turned[0][:].rearrange("p (k i) -> p k i", i=P),
                       ACT.Copy).then_inc(self.copied_a, 1)

    def normalise(self, pool, g, u):
        r = u % 2
        g2, u2 = back(g, u, 2)
        pool.wait_ge(self.factored, g * UNITS + u + 1)
        if real(g2):
            pool.wait_ge(self.transposed, 2 * (g2 * UNITS + u2 + 1))
        pool.tensor_tensor(self.prob[r][:].rearrange("p k (b j) -> p k b j", b=2),
                           self.e[r][:].unsqueeze(2).broadcast_to([P, BLOCKS, 2, 64]),
                           self.factor[:, r, :, :].unsqueeze(3).broadcast_to([P, BLOCKS, 2, 64]),
                           ALU.mult).then_inc(self.normed, 1)

    def transpose(self, pe, identity, g, u):
        pe.wait_ge(self.normed, g * UNITS + u + 1)
        g1, u1 = back(g, u, 1)
        for half, copied in enumerate((self.copied_a, self.copied_b)):
            if real(g1):
                pe.wait_ge(copied, g1 * UNITS + u1 + 1)
            for k in range(4):
                last = pe.transpose(self.turned[half][:, k * P:(k + 1) * P],
                                    self.prob[u % 2][:, 4 * half + k, :], identity[:])
            last.then_inc(self.transposed, 1)


class Norm:

    def __init__(self, nc, ctx, tag):
        def sem(name):
            return nc.alloc_semaphore(f"{tag}_{name}")

        def sb(name, shape, dt=F32):
            return ctx.enter_context(nc.sbuf_tensor(f"{tag}_{name}", shape, dt))

        self.x = sb("x", [P, TILES, DIM])
        self.xr = sb("xr", [P, TILES, DIM])
        self.xo = sb("xo", [P, TILES, DIM])
        self.hat = sb("hat", [P, TILES, DIM])
        self.n = sb("n", [P, TILES, 2 * P])
        self.stats = sb("stats", [P, TILES, 6])
        self.mv = sb("mv", [P, TILES, 2])
        self.rstd = sb("rstd", [P, TILES])
        self.power = sb("power", [P, TILES])
        self.eps = sb("eps", [P, TILES])
        self.ahead = sb("ahead", [P, 1])
        self.gain, self.shift, self.bias = sb("gain", [P, DIM]), sb("shift", [P, DIM]), sb("bias", [P, DIM])
        self.hi = sb("hi", [P, 2, GROUP], F32R)
        self.lo = sb("lo", [P, GROUP], F32R)
        self.arrived = sem("arrived")
        self.again = sem("again")
        self.stored = sem("stored")
        self.set = sem("set")
        self.stat = sem("stat")
        self.var = sem("var")
        self.veps = sem("veps")
        self.root = sem("root")
        self.hatted = sem("hatted")
        self.gained = sem("gained")
        self.ready = sem("ready")
        self.turned = sem("turned")
        self.rounded = sem("rounded")
        self.split = sem("split")
        self.resid = sem("resid")
        self.multiplied = sem("multiplied")
        self.added = sem("added")

    def constants(self, pool):
        pool.memset(self.power[:], -0.5).then_inc(self.set, 1)
        pool.memset(self.eps[:], EPS).then_inc(self.set, 1)
        pool.wait_ge(self.set, 2)

    def load(self, sp, x_in, g):
        if real(g - 1):
            sp.wait_ge(self.hatted, TILES * g)
        sp.dma_start(self.x[:], x_in[g]).then_inc(self.arrived, 16)

    def load_again(self, sp, x_in, g):
        if real(g - 1):
            sp.wait_ge(self.added, TILES * g)
        sp.dma_start(self.xr[:], x_in[g]).then_inc(self.again, 16)

    def store(self, sp, x_out, g):
        sp.wait_ge(self.added, TILES * (g + 1))
        sp.dma_start(x_out[g], self.xo[:]).then_inc(self.stored, 16)

    def statistics(self, dve, g, t):
        if t == 0:
            dve.wait_ge(self.arrived, 16 * (g + 1))
            if real(g - 1):
                dve.wait_ge(self.hatted, TILES * g)
                dve.wait_ge(self.veps, g)
        dve.bn_stats(self.stats[:, t, :], self.x[:, t, :]).then_inc(self.stat, 1)
        dve.wait_ge(self.stat, TILES * g + t + 1)
        dve.memset(self.ahead[:], 0.0)
        dve.bn_aggr(self.mv[:, t, :], self.stats[:, t, :]).then_inc(self.var, 1)

    def inverse_root(self, pool, g):
        pool.wait_ge(self.var, TILES * (g + 1))
        if real(g - 1):
            pool.wait_ge(self.hatted, TILES * g)
        pool.tensor_tensor(self.rstd[:], self.mv[:, :, 1], self.eps[:], ALU.add).then_inc(self.veps, 1)
        pool.wait_ge(self.veps, g + 1)
        pool.tensor_tensor(self.rstd[:], self.rstd[:], self.power[:], ALU.pow).then_inc(self.root, 1)

    def normalise(self, dve, g, t):
        if t == 0:
            dve.wait_ge(self.root, g + 1)
            dve.wait_ge(self.var, TILES * (g + 1))
            if real(g - 1):
                dve.wait_ge(self.ready, 2 * g)
        dve.tensor_scalar(self.hat[:, t, :], self.x[:, t, :], self.mv[:, t, 0:1], self.rstd[:, t:t + 1],
                          ALU.subtract, ALU.mult).then_inc(self.hatted, 1)

    def affine(self, pool, g):
        pool.wait_ge(self.hatted, TILES * (g + 1))
        pool.tensor_tensor(self.hat[:], self.hat[:], self.gain[:].unsqueeze(1).broadcast_to([P, TILES, DIM]),
                           ALU.mult).then_inc(self.gained, 1)
        pool.wait_ge(self.gained, g + 1)
        if real(g - 1):
            pool.wait_ge(self.turned, 2 * g)
        pool.tensor_tensor(self.n[:, :, 0:P], self.hat[:, :, 0:P],
                           self.shift[:, 0:P].unsqueeze(1).broadcast_to([P, TILES, P]), ALU.add)\
            .then_inc(self.ready, 1)
        pool.tensor_tensor(self.n[:, :, P:2 * P].rearrange("p t (c r) -> p t c r", c=COPIES),
                           self.hat[:, :, P:DIM].unsqueeze(2).broadcast_to([P, TILES, COPIES, REM]),
                           self.shift[:, P:DIM].unsqueeze(1).unsqueeze(1).broadcast_to([P, TILES, COPIES, REM]),
                           ALU.add).then_inc(self.ready, 1)

    def transpose(self, pe, identity, banks, g, part):
        pe.wait_ge(self.ready, 2 * g + 2)
        for t in range(TILES):
            last = pe.transpose(banks[part][:, t * P:(t + 1) * P], self.n[:, t, part * P:(part + 1) * P], identity[:])
        last.then_inc(self.turned, 1)

    def round_hi(self, act, banks, g, part):
        act.wait_ge(self.turned, 2 * g + part + 1)
        act.activation(self.hi[:, part, :], banks[part][:], ACT.Copy).then_inc(self.rounded, 1)

    def rest_lo(self, dve, banks, g, part):
        dve.wait_ge(self.rounded, 2 * g + part + 1)
        if part == 0:
            dve.tensor_tensor(self.lo[:], banks[0][:], self.hi[:, 0, :].bitcast(F32), ALU.subtract)\
               .then_inc(self.split, 1)
        else:
            dve.tensor_tensor(self.hi[64:P, 1, :], banks[1][64:P, :], self.hi[64:P, 1, :].bitcast(F32),
                              ALU.subtract).then_inc(self.split, 1)

    def residual(self, pool, g):
        pool.wait_ge(self.again, 16 * (g + 1))
        pool.tensor_tensor(self.xr[:], self.xr[:], self.bias[:].unsqueeze(1).broadcast_to([P, TILES, DIM]),
                           ALU.add).then_inc(self.resid, 1)

    def add(self, dve, bank, g, t):
        dve.wait_ge(self.multiplied, TILES * g + t + 1)
        if t == 0:
            dve.wait_ge(self.resid, g + 1)
            if real(g - 1):
                dve.wait_ge(self.stored, 16 * g)
        dve.tensor_tensor(self.xo[:, t, :], bank[:, 0:DIM], self.xr[:, t, :], ALU.add).then_inc(self.added, 1)


def attention(nc, tag, loads, x_dram, ctx_dram, out_dram, identity, wq, wk, wv, wo, bo, gain, shift):
    cross = ctx_dram is not None
    x_in = x_dram.rearrange("(g t p) c -> g p t c", t=TILES, p=P)
    x_out = out_dram.rearrange("(g t p) c -> g p t c", t=TILES, p=P)
    with ExitStack() as ctx:
        def sem(name):
            return nc.alloc_semaphore(f"{tag}_{name}")

        def sb(name, shape, dt=F32):
            return ctx.enter_context(nc.sbuf_tensor(f"{tag}_{name}", shape, dt))

        q_hi, q_lo, q_rem = (sb(f"wq_{n}", [P, INNER], F32R) for n in ("hi", "lo", "rem"))
        jobs = [(wq[0:P, :], INNER, q_hi[:], q_lo[:]), (wq[P:DIM, :], INNER, q_rem[:], None)]
        if cross:
            k_hi, k_lo, v_hi, v_lo = (sb(f"w{n}", [P, 2, INNER], F32R) for n in ("k_hi", "k_lo", "v_hi", "v_lo"))
            for w, hi, lo in ((wk, k_hi, k_lo), (wv, v_hi, v_lo)):
                for c in range(2):
                    jobs.append((w[c * P:(c + 1) * P, :], INNER, hi[:, c, :], lo[:, c, :]))
        else:
            k_hi, k_lo, k_rem = (sb(f"wk_{n}", [P, INNER], F32R) for n in ("hi", "lo", "rem"))
            v_hi, v_lo, v_rem = (sb(f"wv_{n}", [P, INNER], F32R) for n in ("hi", "lo", "rem"))
            for w, hi, lo, rem in ((wk, k_hi, k_lo, k_rem), (wv, v_hi, v_lo, v_rem)):
                jobs += [(w[0:P, :], INNER, hi[:], lo[:]), (w[P:DIM, :], INNER, rem[:], None)]
        wo_sb = sb("wo", [P, UNITS, DIM])
        ln = Norm(nc, ctx, tag + "_ln")
        split_weights(nc, tag, loads, jobs, [
            (wo_sb[:], wo.rearrange("(u p) c -> p u c", p=P)),
            (ln.gain[:], row(gain)), (ln.shift[:], row(shift)), (ln.bias[:], row(bo))])

        sm = Softmax(nc, ctx, tag + "_sm")
        queries = [sb(f"queries{i}", [P, GROUP]) for i in range(2)]
        keys = [sb(f"keys{i}", [P, BLOCKS, P]) for i in range(2)]
        values = sb("values", [P, TILES, INNER])
        outs = sb("outs", [P, UNITS, GROUP])
        q_out = sem("q_out")
        k_out = sem("k_out")
        v_out = sem("v_out")
        q_in = sem("q_in")
        k_in_a = sem("k_in_a")
        k_in_b = sem("k_in_b")
        v_in = sem("v_in")
        o_in = sem("o_in")
        zeros = sem("zeros")
        if cross:
            c_x = sb("c_x", [P, TILES, CTX])
            c_hi, c_lo = sb("c_hi", [P, 2, GROUP], F32R), sb("c_lo", [P, 2, GROUP], F32R)
            ctx_in = ctx_dram.rearrange("(g t p) c -> g p t c", t=TILES, p=P)
            c_arrived = sem("c_arrived")
            c_turned = sem("c_turned")
            c_rounded = sem("c_rounded")
            c_split = sem("c_split")

        v_slots = [[(t, 0, 512)] for t in range(TILES)] + [[(t, 512, 512)] for t in range(TILES)] \
            + [[(t, 1024, 256), (t + 1, 1024, 256)] for t in (0, 2)]
        v_last_user = [3] * 4 + [7] * 4 + [9] * 2

        block = ctx.enter_context(nc.Block())

        @block.sync
        def _(sp):
            def load_ctx(g):
                if real(g - 1):
                    sp.wait_ge(c_turned, 2 * g)
                sp.dma_start(c_x[:], ctx_in[g]).then_inc(c_arrived, 16)

            def body(g, front, tail, ahead):
                if isinstance(g, int) and g == 0:
                    ln.load(sp, x_in, 0)
                    if cross:
                        load_ctx(0)
                if ahead:
                    ln.load(sp, x_in, g + 1)
                    if cross:
                        load_ctx(g + 1)
                if tail:
                    ln.store(sp, x_out, g - 1)
                if front:
                    ln.load_again(sp, x_in, g)

            over_groups(sp, body)
            sp.wait_ge(ln.stored, 16 * GROUPS)

        @block.gpsimd
        def _(pool):
            ln.constants(pool)
            for i in range(2):
                pool.memset(keys[i][:], 0.0).then_inc(zeros, 1)

            def body(g, front, tail, ahead):
                if isinstance(g, int) and g == 0:
                    ln.inverse_root(pool, 0)
                    ln.affine(pool, 0)
                for s in range(UNITS):
                    u1 = s - 1
                    if u1 < 0 and tail:
                        sm.normalise(pool, g - 1, UNITS - 1)
                    elif u1 >= 0 and front:
                        sm.normalise(pool, g, u1)
                    if s == 2 and tail:
                        ln.residual(pool, g - 1)
                    if s == 6 and ahead:
                        ln.inverse_root(pool, g + 1)
                    if s == 8 and ahead:
                        ln.affine(pool, g + 1)

            over_groups(pool, body)

        @block.scalar
        def _(act):
            def body(g, front, tail, ahead):
                for s in range(UNITS):
                    if s == 0 and front:
                        for part in range(2):
                            ln.round_hi(act, sm.proj, g, part)
                        if cross:
                            for c in range(2):
                                act.wait_ge(c_turned, 2 * g + c + 1)
                                act.activation(c_hi[:, c, :], sm.proj[c][:], ACT.Copy).then_inc(c_rounded, 1)
                    if front if s >= 3 else tail:
                        sm.copy_a(act, *back(g, s, 3))
                    if front if s >= 1 else tail:
                        sm.exponential(act, *back(g, s, 1), 64 ** -0.5)

                    def output():
                        g4, u4 = back(g, s, 4)
                        act.wait_ge(sm.valued, g4 * UNITS + u4 + 1)
                        act.activation(outs[:, u4, :], sm.out[:], ACT.Copy).then_inc(o_in, 1)

                    if s < 4 and tail:
                        output()
                    if s > 4 and front:
                        output()
                    if front:
                        g2, u2 = back(g, s, 2)
                        act.wait_ge(q_out, g * UNITS + s + 1)
                        if real(g2):
                            act.wait_ge(sm.scored, g2 * UNITS + u2 + 1)
                        act.activation(queries[s % 2][:], sm.proj[s % 2][:], ACT.Copy).then_inc(q_in, 1)
                        act.wait_ge(k_out, g * UNITS + s + 1)
                        if isinstance(g, int) and g == 0 and s == 0:
                            act.wait_ge(zeros, 2)
                        act.activation(keys[s % 2][0:64, :, 0:64],
                                       sm.proj[(s + 1) % 2][0:64, :].rearrange("p (b j) -> p b j", j=64),
                                       ACT.Copy).then_inc(k_in_a, 1)
                        act.wait_ge(v_out, g * UNITS + s + 1)
                        if real(g - 1):
                            act.wait_ge(sm.valued, (g - 1) * UNITS + v_last_user[s] + 1)
                        pieces = v_slots[s]
                        t0, c0, n = pieces[0]
                        act.activation(values[:, t0:t0 + len(pieces), c0:c0 + n],
                                       sm.proj[s % 2][:].rearrange("p (t c) -> p t c", c=n),
                                       ACT.Copy).then_inc(v_in, 1)
                    if s == 4 and front:
                        output()

            over_groups(act, body)

        @block.vector
        def _(dve):
            sm.constants(dve)

            def body(g, front, tail, ahead):
                if isinstance(g, int) and g == 0:
                    for t in range(TILES):
                        ln.statistics(dve, 0, t)
                    for t in range(TILES):
                        ln.normalise(dve, 0, t)
                for s in range(UNITS):
                    if s == 0 and front:
                        for part in range(2):
                            ln.rest_lo(dve, sm.proj, g, part)
                        if cross:
                            for c in range(2):
                                dve.wait_ge(c_rounded, 2 * g + c + 1)
                                dve.tensor_tensor(c_lo[:, c, :], sm.proj[c][:], c_hi[:, c, :].bitcast(F32),
                                                  ALU.subtract).then_inc(c_split, 1)
                    if front if s >= 1 else tail:
                        sm.maximum_and_shift(dve, *back(g, s, 1))
                    if front if s >= 3 else tail:
                        sm.copy_b(dve, *back(g, s, 3))
                    if s == 4 and tail:
                        for t in range(2):
                            ln.add(dve, sm.y, g - 1, t)
                    if front:
                        g2, u2 = back(g, s, 2)
                        dve.wait_ge(k_out, g * UNITS + s + 1)
                        if real(g2):
                            dve.wait_ge(sm.scored, g2 * UNITS + u2 + 1)
                        if isinstance(g, int) and g == 0 and s == 0:
                            dve.wait_ge(zeros, 2)
                        dve.tensor_copy(keys[s % 2][64:P, :, 64:P],
                                        sm.proj[(s + 1) % 2][64:P, :].rearrange("p (b j) -> p b j", j=64))\
                           .then_inc(k_in_b, 1)
                    if s == 4 and tail:
                        for t in range(2, TILES):
                            ln.add(dve, sm.y, g - 1, t)
                    if front if s >= 1 else tail:
                        sm.sum_and_invert(dve, *back(g, s, 1))
                    if ahead and s in (5, 6):
                        for t in (2 * (s - 5), 2 * (s - 5) + 1):
                            ln.statistics(dve, g + 1, t)
                    if ahead and s in (7, 8):
                        for t in (2 * (s - 7), 2 * (s - 7) + 1):
                            ln.normalise(dve, g + 1, t)

            over_groups(dve, body)

        @block.tensor
        def _(pe):
            def project_queries(g, u):
                cols, bank = slice(u * P, (u + 1) * P), sm.proj[u % 2]
                if u == 0:
                    if cross:
                        pe.wait_ge(c_split, 2 * g + 1)
                    pe.wait_ge(ln.split, 2 * g + 2)
                else:
                    pe.wait_ge(k_in_a, g * UNITS + u)
                    pe.wait_ge(k_in_b, g * UNITS + u)
                parts = [(q_hi, ln.hi[:, 0, :]), (q_lo, ln.hi[:, 0, :]), (q_hi, ln.lo[:]), (q_rem, ln.hi[:, 1, :])]
                for n, (w, moving) in enumerate(parts):
                    last = pe.matmul(bank[:], w[:, cols], moving, start=n == 0, stop=n == len(parts) - 1)
                last.then_inc(q_out, 1)

            def project_keys(g, u):
                cols, bank = slice(u * P, (u + 1) * P), sm.proj[(u + 1) % 2]
                if u == 0:
                    if cross:
                        pe.wait_ge(c_split, 2 * g + 2)
                else:
                    pe.wait_ge(v_in, g * UNITS + u)
                if cross:
                    parts = [(k_hi[:, c, cols], c_hi[:, c, :]) for c in range(2)] \
                        + [(k_lo[:, c, cols], c_hi[:, c, :]) for c in range(2)] \
                        + [(k_hi[:, c, cols], c_lo[:, c, :]) for c in range(2)]
                else:
                    parts = [(k_hi[:, cols], ln.hi[:, 0, :]), (k_lo[:, cols], ln.hi[:, 0, :]),
                             (k_hi[:, cols], ln.lo[:]), (k_rem[:, cols], ln.hi[:, 1, :])]
                for n, (w, moving) in enumerate(parts):
                    last = pe.matmul(bank[:], w, moving, start=n == 0, stop=n == len(parts) - 1)
                last.then_inc(k_out, 1)

            def project_values(g, s):
                pe.wait_ge(q_in, g * UNITS + s + 1)
                for i, (t, c0, n) in enumerate(v_slots[s]):
                    tok, cols = slice(t * P, (t + 1) * P), slice(c0, c0 + n)
                    if cross:
                        parts = [(c_hi[:, c, tok], v_hi[:, c, cols]) for c in range(2)] \
                            + [(c_lo[:, c, tok], v_hi[:, c, cols]) for c in range(2)] \
                            + [(c_hi[:, c, tok], v_lo[:, c, cols]) for c in range(2)]
                    else:
                        parts = [(ln.hi[:, 0, tok], v_hi[:, cols]), (ln.lo[:, tok], v_hi[:, cols]),
                                 (ln.hi[:, 0, tok], v_lo[:, cols]), (ln.hi[:, 1, tok], v_rem[:, cols])]
                    for k, (w, moving) in enumerate(parts):
                        last = pe.matmul(sm.proj[s % 2][:, i * n:(i + 1) * n], w, moving,
                                         start=k == 0, stop=k == len(parts) - 1)
                last.then_inc(v_out, 1)

            def score(g, u):
                g2, u2 = back(g, u, 2)
                pe.wait_ge(q_in, g * UNITS + u + 1)
                pe.wait_ge(k_in_a, g * UNITS + u + 1)
                pe.wait_ge(k_in_b, g * UNITS + u + 1)
                if real(g2):
                    pe.wait_ge(sm.shifted, g2 * UNITS + u2 + 1)
                for t in range(TILES):
                    for b in range(2):
                        seq = 2 * t + b
                        last = pe.matmul(sm.scores[u % 2][b * 64:(b + 1) * 64, t * P:(t + 1) * P],
                                         queries[u % 2][:, seq * 64:(seq + 1) * 64], keys[u % 2][:, seq, :],
                                         start=True, stop=True)
                last.then_inc(sm.scored, 1)

            def times_values(g, u):
                g1, u1 = back(g, u, 1)
                pe.wait_ge(sm.copied_a, g * UNITS + u + 1)
                pe.wait_ge(sm.copied_b, g * UNITS + u + 1)
                pe.wait_ge(v_in, g * UNITS + (4 if u < 4 else 8 if u < 8 else 10))
                if real(g1):
                    pe.wait_ge(o_in, g1 * UNITS + u1 + 1)
                for t in range(TILES):
                    for h in range(2):
                        head = 2 * u + h
                        last = pe.matmul(sm.out[h * 64:(h + 1) * 64, t * P:(t + 1) * P],
                                         values[:, t, head * 64:(head + 1) * 64], sm.probT[u % 2][:, 2 * t + h, :],
                                         start=True, stop=True)
                last.then_inc(sm.valued, 1)

            def project_out(g, t):
                pe.wait_ge(o_in, g * UNITS + UNITS)
                if t > 0:
                    pe.wait_ge(ln.added, TILES * g + t)
                elif real(g - 1):
                    pe.wait_ge(ln.added, TILES * g)
                for u in range(UNITS):
                    last = pe.matmul(sm.y[:, 0:DIM], outs[:, u, t * P:(t + 1) * P], wo_sb[:, u, :],
                                     start=u == 0, stop=u == UNITS - 1)
                last.then_inc(ln.multiplied, 1)

            def turn(g):
                if real(g - 1):
                    pe.wait_ge(v_in, g * UNITS)
                    pe.wait_ge(k_in_a, g * UNITS)
                    pe.wait_ge(k_in_b, g * UNITS)
                for part in range(2):
                    ln.transpose(pe, identity, sm.proj, g, part)
                if cross:
                    for c in range(2):
                        pe.wait_ge(c_arrived, 16 * (g + 1))
                        pe.wait_ge(ln.split, 2 * g + c + 1)
                        for t in range(TILES):
                            last = pe.transpose(sm.proj[c][:, t * P:(t + 1) * P],
                                                c_x[:, t, c * P:(c + 1) * P], identity[:])
                        last.then_inc(c_turned, 1)

            def body(g, front, tail, ahead):
                for s in range(UNITS):
                    if s == 0 and front:
                        turn(g)
                    if front if s >= 1 else tail:
                        score(*back(g, s, 1))
                    if front if s >= 3 else tail:
                        sm.transpose(pe, identity, *back(g, s, 3))
                    if s < 4 and tail:
                        times_values(*back(g, s, 4))
                    if s > 4 and front:
                        times_values(*back(g, s, 4))
                    if s == 4 and tail:
                        project_out(g - 1, 0)
                    if front:
                        project_queries(g, s)
                    if s == 4 and tail:
                        project_out(g - 1, 1)
                    if front:
                        project_keys(g, s)
                    if s == 4 and tail:
                        project_out(g - 1, 2)
                    if front:
                        project_values(g, s)
                    if s == 4 and tail:
                        project_out(g - 1, 3)
                    if s == 4 and front:
                        times_values(g, 0)

            over_groups(pe, body)


def feed_forward(nc, tag, loads, x_dram, out_dram, identity, w1, b1, w2, b2, gain, shift):
    x_in = x_dram.rearrange("(g t p) c -> g p t c", t=TILES, p=P)
    x_out = out_dram.rearrange("(g t p) c -> g p t c", t=TILES, p=P)
    with ExitStack() as ctx:
        def sem(name):
            return nc.alloc_semaphore(f"{tag}_{name}")

        def sb(name, shape, dt=F32):
            return ctx.enter_context(nc.sbuf_tensor(f"{tag}_{name}", shape, dt))

        def pb(name):
            return ctx.enter_context(nc.psum_tensor(f"{tag}_{name}", [P, 512], F32))

        w_hi, w_lo, w_rem = (sb(f"w1_{n}", [P, 2 * FF], F32R) for n in ("hi", "lo", "rem"))
        w2_sb = sb("w2", [P, FF_CHUNKS, DIM])
        b1_sb = sb("b1", [P, 2 * FF_CHUNKS])
        ln = Norm(nc, ctx, tag + "_ln")
        split_weights(nc, tag, loads, [(w1[0:P, :], 2 * FF, w_hi[:], w_lo[:]), (w1[P:DIM, :], 2 * FF, w_rem[:], None)], [
            (w2_sb[:], w2.rearrange("(c p) n -> p c n", p=P)), (b1_sb[:], b1),
            (ln.gain[:], row(gain)), (ln.shift[:], row(shift)), (ln.bias[:], row(b2))])

        gate = [sb(f"gate{i}", [P, GROUP]) for i in range(2)]
        hidden = sb("hidden", [P, FF_CHUNKS, GROUP])
        banks = [pb(f"turn{i}") for i in range(2)]
        psa, psg = [pb(f"a{i}") for i in range(2)], [pb(f"gate_p{i}") for i in range(2)]
        psy = [pb(f"y{i}") for i in range(2)]
        a_out = sem("a_out")
        g_out = sem("g_out")
        gelued = sem("gelued")
        gated = sem("gated")

        block = ctx.enter_context(nc.Block())

        @block.sync
        def _(sp):
            def body(g, front, tail, ahead):
                if isinstance(g, int) and g == 0:
                    ln.load(sp, x_in, 0)
                if ahead:
                    ln.load(sp, x_in, g + 1)
                if tail:
                    ln.store(sp, x_out, g - 1)
                if front:
                    ln.load_again(sp, x_in, g)

            over_groups(sp, body)
            sp.wait_ge(ln.stored, 16 * GROUPS)

        @block.gpsimd
        def _(pool):
            ln.constants(pool)

            def body(g, front, tail, ahead):
                if isinstance(g, int) and g == 0:
                    ln.inverse_root(pool, 0)
                    ln.affine(pool, 0)
                if ahead:
                    ln.inverse_root(pool, g + 1)
                if front:
                    ln.residual(pool, g)
                if ahead:
                    ln.affine(pool, g + 1)

            over_groups(pool, body)

        def chunk_back(g, j, n):
            return (g, j - n) if j >= n else (g - 1, j - n + FF_CHUNKS)

        @block.scalar
        def _(act):
            def body(g, front, tail, ahead):
                if front:
                    for part in range(2):
                        ln.round_hi(act, banks, g, part)
                    for j in range(FF_CHUNKS):
                        g2, j2 = chunk_back(g, j, 2) if j >= 2 else (g - 1, FF_CHUNKS - 1)
                        act.wait_ge(g_out, g * FF_CHUNKS + j + 1)
                        if real(g2):
                            act.wait_ge(gated, g2 * FF_CHUNKS + j2 + 1)
                        act.activation(gate[j % 2][:], psg[j % 2][:], ACT.Gelu,
                                       bias=b1_sb[:, FF_CHUNKS + j:FF_CHUNKS + j + 1]).then_inc(gelued, 1)

            over_groups(act, body)

        @block.vector
        def _(dve):
            def body(g, front, tail, ahead):
                if isinstance(g, int) and g == 0:
                    for t in range(TILES):
                        ln.statistics(dve, 0, t)
                    for t in range(TILES):
                        ln.normalise(dve, 0, t)
                if front:
                    for part in range(2):
                        ln.rest_lo(dve, banks, g, part)
                if tail:
                    for t in range(TILES):
                        ln.add(dve, psy[t % 2], g - 1, t)
                for j in range(FF_CHUNKS):
                    if front:
                        dve.wait_ge(gelued, g * FF_CHUNKS + j + 1)
                        dve.wait_ge(a_out, g * FF_CHUNKS + j + 1)
                        dve.scalar_tensor_tensor(hidden[:, j, :], psa[j % 2][:], b1_sb[:, j:j + 1], gate[j % 2][:],
                                                 ALU.add, ALU.mult).then_inc(gated, 1)
                    if ahead and j == 0:
                        for t in range(TILES):
                            ln.statistics(dve, g + 1, t)
                    if ahead and j == 2:
                        for t in range(TILES):
                            ln.normalise(dve, g + 1, t)

            over_groups(dve, body)

        @block.tensor
        def _(pe):
            def body(g, front, tail, ahead):
                if front:
                    if real(g - 1):
                        pe.wait_ge(ln.split, 2 * g)
                    for part in range(2):
                        ln.transpose(pe, identity, banks, g, part)
                if tail:
                    pe.wait_ge(gated, g * FF_CHUNKS)
                    for t in range(TILES):
                        if t >= 2:
                            pe.wait_ge(ln.added, TILES * (g - 1) + t - 1)
                        elif not isinstance(g, int) or g > 1:
                            pe.wait_ge(ln.added, TILES * (g - 1))
                        for j in range(FF_CHUNKS):
                            last = pe.matmul(psy[t % 2][:, 0:DIM], hidden[:, j, t * P:(t + 1) * P], w2_sb[:, j, :],
                                             start=j == 0, stop=j == FF_CHUNKS - 1)
                        last.then_inc(ln.multiplied, 1)
                if front:
                    pe.wait_ge(ln.split, 2 * g + 2)
                    for j in range(FF_CHUNKS):
                        g2, j2 = (g, j - 2) if j >= 2 else (g - 1, FF_CHUNKS - 1)
                        for bank, c, done in ((psg[j % 2], FF_CHUNKS + j, g_out), (psa[j % 2], j, a_out)):
                            if real(g2):
                                pe.wait_ge(gated, g2 * FF_CHUNKS + j2 + 1)
                            cols = slice(c * P, (c + 1) * P)
                            parts = [(w_hi, ln.hi[:, 0, :]), (w_lo, ln.hi[:, 0, :]), (w_hi, ln.lo[:]),
                                     (w_rem, ln.hi[:, 1, :])]
                            for n, (w, moving) in enumerate(parts):
                                last = pe.matmul(bank[:], w[:, cols], moving, start=n == 0, stop=n == len(parts) - 1)
                            last.then_inc(done, 1)

            over_groups(pe, body)


def ip_attention(nc, tag, loads, x_dram, ctx_dram, out_dram, identity, mask, wq, wk, wv, wo, bo):
    quads, pair = 5, 2 * P
    x_in = x_dram.rearrange("(g t p) c -> g p t c", t=TILES, p=P)
    ctx_in = ctx_dram.rearrange("(g t p) c -> g p t c", t=TILES, p=P)
    x_out = out_dram.rearrange("(g t p) c -> g p t c", t=TILES, p=P)
    with ExitStack() as ctx:
        def sem(name):
            return nc.alloc_semaphore(f"{tag}_{name}")

        def sb(name, shape, dt=F32):
            return ctx.enter_context(nc.sbuf_tensor(f"{tag}_{name}", shape, dt))

        q_hi, q_lo, q_rem = (sb(f"wq_{n}", [P, 2 * P], F32R) for n in ("hi", "lo", "rem"))
        k_hi, k_lo = sb("wk_hi", [P, 2, 2 * P], F32R), sb("wk_lo", [P, 2, 2 * P], F32R)
        wv_sb = sb("wv", [P, 2, DIM])
        wo_sb = sb("wo", [P, 2, DIM])
        mask_sb = sb("mask", [P, 4, 4])
        bias = sb("bias", [P, DIM])
        jobs = [(wq[0:P, :], 2 * P, q_hi[:], q_lo[:]), (wq[P:DIM, :], 2 * P, q_rem[:], None)] \
            + [(wk[c * P:(c + 1) * P, :], 2 * P, k_hi[:, c, :], k_lo[:, c, :]) for c in range(2)]
        split_weights(nc, tag, loads, jobs, [
            (wv_sb[:], wv.rearrange("(c p) n -> p c n", p=P)), (wo_sb[:], wo.rearrange("(c p) n -> p c n", p=P)),
            (mask_sb[:], mask), (bias[:], row(bo))])

        sm = Softmax(nc, ctx, tag + "_sm")
        x = sb("x", [P, TILES, DIM])
        xn = sb("xn", [P, TILES, 2 * P])
        xr = sb("xr", [P, TILES, DIM])
        xo = sb("xo", [P, TILES, DIM])
        hi, lo = sb("hi", [P, 2, GROUP], F32R), sb("lo", [P, GROUP], F32R)
        c_x = sb("c_x", [P, TILES, CTX])
        c_t = sb("c_t", [P, 2, GROUP])
        c_hi, c_lo = sb("c_hi", [P, 2, GROUP], F32R), sb("c_lo", [P, 2, GROUP], F32R)
        queries = sb("queries", [P, 2, GROUP])
        keys = sb("keys", [P, 2, GROUP])
        diagonal = [sb(f"diagonal{i}", [P, 4, 4, 64]) for i in range(2)]
        values = sb("values", [P, TILES, HEADS, 32])
        outs = sb("outs", [P, 2, GROUP])
        arrived, again, stored, c_arrived = sem("arrived"), sem("again"), sem("stored"), sem("c_arrived")
        spread = sem("spread")
        turned = sem("turned")
        rounded = sem("rounded")
        split = sem("split")
        c_kept = sem("c_kept")
        q_out, q_in = sem("q_out"), sem("q_in")
        k_out, k_in = sem("k_out"), sem("k_in")
        v_out, v_in = sem("v_out"), sem("v_in")
        masked = sem("masked")
        zeros = sem("zeros")
        o_in = sem("o_in")
        resid = sem("resid")
        multiplied, added = sem("multiplied"), sem("added")

        block = ctx.enter_context(nc.Block())

        @block.sync
        def _(sp):
            def load(g):
                if real(g - 1):
                    sp.wait_ge(spread, 2 * g)
                sp.dma_start(x[:], x_in[g]).then_inc(arrived, 16)
                if real(g - 1):
                    sp.wait_ge(turned, 4 * g)
                sp.dma_start(c_x[:], ctx_in[g]).then_inc(c_arrived, 16)

            def body(g, front, tail, ahead):
                if isinstance(g, int) and g == 0:
                    load(0)
                if ahead:
                    load(g + 1)
                if tail:
                    sp.wait_ge(added, TILES * g)
                    sp.dma_start(x_out[g - 1], xo[:]).then_inc(stored, 16)
                if front:
                    if real(g - 1):
                        sp.wait_ge(added, TILES * g)
                    sp.dma_start(xr[:], x_in[g]).then_inc(again, 16)

            over_groups(sp, body)
            sp.wait_ge(stored, 16 * GROUPS)

        @block.gpsimd
        def _(pool):
            pool.memset(values[:], 0.0).then_inc(zeros, 1)
            pool.memset(outs[:], 0.0).then_inc(zeros, 1)

            def body(g, front, tail, ahead):
                for s in range(UNITS):
                    if front if s >= 1 else tail:
                        sm.normalise(pool, *back(g, s, 1))
                    if s == 2 and tail:
                        pool.wait_ge(again, 16 * g)
                        pool.tensor_tensor(xr[:], xr[:], bias[:].unsqueeze(1).broadcast_to([P, TILES, DIM]),
                                           ALU.add).then_inc(resid, 1)

            over_groups(pool, body)

        @block.scalar
        def _(act):
            def spread_x(g):
                act.wait_ge(arrived, 16 * (g + 1))
                if real(g - 1):
                    act.wait_ge(turned, 4 * (g - 1) + 2)
                act.activation(xn[:, :, 0:P], x[:, :, 0:P], ACT.Copy).then_inc(spread, 1)
                act.activation(xn[:, :, P:2 * P].rearrange("p t (c r) -> p t c r", c=COPIES),
                                 x[:, :, P:DIM].unsqueeze(2).broadcast_to([P, TILES, COPIES, REM]), ACT.Copy).then_inc(spread, 1)

            def body(g, front, tail, ahead):
                if isinstance(g, int) and g == 0:
                    spread_x(0)
                for s in range(UNITS):
                    if s == 5 and ahead:
                        spread_x(g + 1)
                    if s == 0 and front:
                        for part in range(2):
                            act.wait_ge(turned, 4 * g + part + 1)
                            act.activation(hi[:, part, :], sm.proj[part][:], ACT.Copy).then_inc(rounded, 1)
                        for c in range(2):
                            act.wait_ge(turned, 4 * g + 2 + c + 1)
                            act.activation(c_hi[:, c, :], sm.proj[c][:], ACT.Copy).then_inc(rounded, 1)
                            act.activation(c_t[:, c, :], sm.proj[c][:], ACT.Copy).then_inc(c_kept, 1)
                    if front if s >= 3 else tail:
                        sm.copy_a(act, *back(g, s, 3))
                    if front if s >= 1 else tail:
                        sm.exponential(act, *back(g, s, 1), 8 ** -0.5)
                    if s == 0 and front:
                        for c in range(2):
                            act.wait_ge(q_out, 2 * g + c + 1)
                            if real(g - 1):
                                act.wait_ge(sm.scored, g * UNITS)
                            act.activation(queries[:, c, :], sm.proj[c][:], ACT.Copy).then_inc(q_in, 1)
                        for c in range(2):
                            act.wait_ge(k_out, 2 * g + c + 1)
                            if real(g - 1):
                                act.wait_ge(masked, g * UNITS)
                            act.activation(keys[:, c, :], sm.proj[c][:], ACT.Copy).then_inc(k_in, 1)
                    for at, there, tp in ((8, front, 0), (3, tail, 1)):
                        if s == at and there:
                            go = g if tp == 0 else g - 1
                            act.wait_ge(sm.valued, go * UNITS + 5 * tp + 5)
                            if isinstance(g, int) and g == 0:
                                act.wait_ge(zeros, 2)
                            if tp == 0 and real(g - 1):
                                act.wait_ge(multiplied, TILES * g)
                            toks = slice(tp * pair, (tp + 1) * pair)
                            act.activation(outs[:, 0, toks], sm.out[:, 0:pair], ACT.Copy).then_inc(o_in, 1)
                            act.activation(outs[0:REM, 1, toks], sm.out[0:REM, pair:2 * pair], ACT.Copy)\
                               .then_inc(o_in, 1)

            over_groups(act, body)

        @block.vector
        def _(dve):
            sm.constants(dve)

            def diagonal_keys(g, u):
                tp, q = divmod(u, quads)
                g2, u2 = back(g, u, 2)
                if u == 0:
                    dve.wait_ge(k_in, 2 * g + 2)
                if real(g2):
                    dve.wait_ge(sm.scored, g2 * UNITS + u2 + 1)
                seqs = keys[:, q // 4, tp * pair:(tp + 1) * pair].rearrange("p (b j) -> p b j", j=64)
                dve.tensor_tensor(diagonal[u % 2][:], seqs.unsqueeze(2).broadcast_to([P, 4, 4, 64]),
                                  mask_sb[:, q % 4, :].unsqueeze(1).unsqueeze(3).broadcast_to([P, 4, 4, 64]),
                                  ALU.mult).then_inc(masked, 1)

            def body(g, front, tail, ahead):
                for s in range(UNITS):
                    if s == 0 and front:
                        for part in range(4):
                            dve.wait_ge(rounded, 4 * g + part + 1)
                            if part == 0:
                                dve.tensor_tensor(lo[:], sm.proj[0][:], hi[:, 0, :].bitcast(F32), ALU.subtract)\
                                   .then_inc(split, 1)
                            elif part == 1:
                                dve.tensor_tensor(hi[64:P, 1, :], sm.proj[1][64:P, :], hi[64:P, 1, :].bitcast(F32),
                                                  ALU.subtract).then_inc(split, 1)
                            else:
                                dve.wait_ge(c_kept, 2 * g + part - 1)
                                dve.tensor_tensor(c_lo[:, part - 2, :], sm.proj[part - 2][:],
                                                  c_hi[:, part - 2, :].bitcast(F32), ALU.subtract).then_inc(split, 1)
                    if s == 0 and tail:
                        sm.maximum_and_shift(dve, g - 1, UNITS - 1)
                    if front:
                        diagonal_keys(g, s)
                    if front and s >= 1:
                        sm.maximum_and_shift(dve, g, s - 1)
                    if front if s >= 3 else tail:
                        sm.copy_b(dve, *back(g, s, 3))
                    if s == 3 and front:
                        for tp in range(2):
                            dve.wait_ge(v_out, 2 * g + tp + 1)
                            if isinstance(g, int) and g == 0:
                                dve.wait_ge(zeros, 2)
                            else:
                                dve.wait_ge(sm.valued, g * UNITS)
                            for h in range(4):
                                last = dve.tensor_copy(
                                    values[:, 2 * tp:2 * tp + 2, h::4, 8 * h:8 * h + 8],
                                    sm.proj[tp][:, 0:2 * DIM].rearrange("p (t q h d) -> p t q h d", t=2, h=4, d=8)
                                    [:, :, :, h, :])
                                last.then_inc(v_in, 1)
                    if s == 4 and tail:
                        for t in range(TILES):
                            dve.wait_ge(multiplied, TILES * (g - 1) + t + 1)
                            if t == 0:
                                dve.wait_ge(resid, g)
                                if not isinstance(g, int) or g > 1:
                                    dve.wait_ge(stored, 16 * (g - 1))
                            dve.tensor_tensor(xo[:, t, :], sm.y[:, 0:DIM], xr[:, t, :], ALU.add).then_inc(added, 1)
                    if front if s >= 1 else tail:
                        sm.sum_and_invert(dve, *back(g, s, 1))

            over_groups(dve, body)

        @block.tensor
        def _(pe):
            def turn(g):
                for part in range(4):
                    bank = sm.proj[part % 2]
                    if part < 2:
                        pe.wait_ge(spread, 2 * g + 2)
                        if real(g - 1):
                            pe.wait_ge(v_in, 8 * g)
                    else:
                        pe.wait_ge(c_arrived, 16 * (g + 1))
                        pe.wait_ge(split, 4 * g + part - 1)
                    for t in range(TILES):
                        cols = slice((part % 2) * P, (part % 2 + 1) * P)
                        source = xn[:, t, cols] if part < 2 else c_x[:, t, cols]
                        last = pe.transpose(bank[:, t * P:(t + 1) * P], source, identity[:])
                    last.then_inc(turned, 1)

            def project_queries_and_keys(g):
                for c in range(2):
                    cols = slice(c * P, (c + 1) * P)
                    pe.wait_ge(split, 4 * g + 3 + c)
                    parts = [(q_hi, hi[:, 0, :]), (q_lo, hi[:, 0, :]), (q_hi, lo[:]), (q_rem, hi[:, 1, :])]
                    for n, (w, moving) in enumerate(parts):
                        last = pe.matmul(sm.proj[c][:], w[:, cols], moving, start=n == 0, stop=n == len(parts) - 1)
                    last.then_inc(q_out, 1)
                for c in range(2):
                    cols = slice(c * P, (c + 1) * P)
                    pe.wait_ge(q_in, 2 * g + c + 1)
                    parts = [(w[:, k, cols], m[:, k, :]) for w, m in ((k_hi, c_hi), (k_lo, c_hi), (k_hi, c_lo))
                             for k in range(2)]
                    for n, (w, moving) in enumerate(parts):
                        last = pe.matmul(sm.proj[c][:], w, moving, start=n == 0, stop=n == len(parts) - 1)
                    last.then_inc(k_out, 1)

            def project_values(g):
                for tp in range(2):
                    pe.wait_ge(k_in, 2 * g + tp + 1)
                    for i in range(2):
                        t = 2 * tp + i
                        for c in range(2):
                            last = pe.matmul(sm.proj[tp][:, i * DIM:(i + 1) * DIM], c_t[:, c, t * P:(t + 1) * P],
                                             wv_sb[:, c, :], start=c == 0, stop=c == 1)
                    last.then_inc(v_out, 1)

            def score(g, u):
                tp, q = divmod(u, quads)
                g2, u2 = back(g, u, 2)
                pe.wait_ge(q_in, 2 * g + 2)
                pe.wait_ge(masked, g * UNITS + u + 1)
                if real(g2):
                    pe.wait_ge(sm.shifted, g2 * UNITS + u2 + 1)
                for i in range(2):
                    for b in range(2):
                        first = (2 * tp + i) * P + b * 64
                        last = pe.matmul(sm.scores[u % 2][b * 64:(b + 1) * 64, i * 256:(i + 1) * 256],
                                         queries[:, q // 4, first:first + 64],
                                         diagonal[u % 2][:, 2 * i + b, :, :], start=True, stop=True)
                last.then_inc(sm.scored, 1)

            def times_values(g, u):
                tp, q = divmod(u, quads)
                pe.wait_ge(sm.copied_a, g * UNITS + u + 1)
                pe.wait_ge(sm.copied_b, g * UNITS + u + 1)
                if u == 0:
                    pe.wait_ge(v_in, 8 * (g + 1))
                if q == 0 and (tp == 1 or real(g - 1)):
                    pe.wait_ge(o_in, 4 * g + 2 * tp)
                rows, col = (slice(32 * q, 32 * q + 32), 0) if q < 4 else (slice(0, 32), pair)
                for i in range(2):
                    for h in range(4):
                        last = pe.matmul(sm.out[rows, col + i * P:col + (i + 1) * P],
                                         values[:, 2 * tp + i, 4 * q + h, :], sm.probT[u % 2][:, 4 * i + h, :],
                                         start=h == 0, stop=h == 3)
                last.then_inc(sm.valued, 1)

            def project_out(g):
                pe.wait_ge(o_in, 4 * g + 4)
                for t in range(TILES):
                    if t > 0 or real(g - 1):
                        pe.wait_ge(added, TILES * g + t)
                    for c in range(2):
                        last = pe.matmul(sm.y[:, 0:DIM], outs[:, c, t * P:(t + 1) * P], wo_sb[:, c, :],
                                         start=c == 0, stop=c == 1)
                    last.then_inc(multiplied, 1)

            def body(g, front, tail, ahead):
                for s in range(UNITS):
                    if s == 0 and front:
                        turn(g)
                    if s == 0 and tail:
                        score(g - 1, UNITS - 1)
                    if front if s >= 3 else tail:
                        sm.transpose(pe, identity, *back(g, s, 3))
                    if front if s >= 4 else tail:
                        times_values(*back(g, s, 4))
                    if s == 0 and front:
                        project_queries_and_keys(g)
                    if s >= 1 and front:
                        score(g, s - 1)
                    if s == 3 and front:
                        project_values(g)
                    if s == 4 and tail:
                        project_out(g - 1)

            over_groups(pe, body)


def build(nc, a, out):
    with ExitStack() as ctx:
        identity = ctx.enter_context(nc.sbuf_tensor("identity_sb", [P, P], F32))
        ready = nc.alloc_semaphore("identity_ready")
        loads = Loads(nc)
        x1, x2, x3 = (nc.dram_tensor(f"x{n}", [TOKENS, DIM], F32).ap() for n in (1, 2, 3))
        with nc.Block() as block:
            @block.sync
            def _(sp):
                sp.dma_start(identity[:], a["identity"]).then_inc(ready, 16)
                sp.wait_ge(ready, 16)
        ip_attention(nc, "ip", loads, a["x"], a["ctx"], x1, identity, a["mask"],
                     a["ip_wq"], a["ip_wk"], a["ip_wv"], a["ip_wo"], a["ip_bo"])
        attention(nc, "self", loads, x1, None, x2, identity, a["a1_wq"], a["a1_wk"], a["a1_wv"], a["a1_wo"], a["a1_bo"],
                  a["ln1_g"], a["ln1_b"])
        attention(nc, "cross", loads, x2, a["ctx"], x3, identity, a["a2_wq"], a["a2_wk"], a["a2_wv"], a["a2_wo"], a["a2_bo"],
                  a["ln2_g"], a["ln2_b"])
        feed_forward(nc, "ff", loads, x3, out, identity, a["ff_w1"], a["ff_b1"], a["ff_w2"], a["ff_b2"],
                     a["ln3_g"], a["ln3_b"])


def layout(inputs):
    def padded(w, rows, cols):
        out = np.zeros((rows, cols), w.dtype)
        out[:w.shape[0], :w.shape[1]] = w
        return out

    get = {k: np.asarray(v) for k, v in inputs.items()}
    a = {"x": get["x"].reshape(TOKENS, DIM), "ctx": get["ctx_2048"].reshape(TOKENS, CTX)}
    a["ip_wq"] = padded(get["L0_xattn_Wq"].T, DIM, 2 * P)
    a["ip_wk"] = padded(get["L0_xattn_Wk"].T, CTX, 2 * P)
    a["ip_wv"] = get["L0_xattn_Wv"].T
    a["ip_wo"] = padded(get["L0_xattn_Wo"].T, 2 * P, DIM)
    a["ip_bo"] = get["L0_xattn_bo"]
    for n in ("a1_wq", "a1_wk", "a1_wv", "a1_wo", "a1_bo", "a2_wq", "a2_wk", "a2_wv", "a2_wo", "a2_bo",
              "ff_w1", "ff_w2", "ff_b2", "ln1_g", "ln1_b", "ln2_g", "ln2_b", "ln3_g", "ln3_b"):
        a[n] = get["L1_xattn_" + n]
    a["ff_b1"] = get["L1_xattn_ff_b1"].reshape(2 * FF_CHUNKS, P).T
    a["identity"] = np.eye(P, dtype=np.float32)
    heads = np.arange(P)[:, None] // 8 == np.arange(16)[None, :]
    a["mask"] = heads.reshape(P, 4, 4).astype(np.float32)
    return {k: np.ascontiguousarray(v) for k, v in a.items()}


def kernel(**inputs):
    import concourse.bacc as bacc
    from concourse.bass_utils import run_bass_kernel_spmd

    nc = bacc.Bacc("TRN2", target_bir_lowering=False, num_devices=1)
    arrays = {f"in_{k}": v for k, v in layout(inputs).items()}
    a = {k[3:]: nc.dram_tensor(k, v.shape, mybir.dt.from_np(v.dtype), kind="ExternalInput").ap()
         for k, v in arrays.items()}
    out = nc.dram_tensor("out", [TOKENS, DIM], F32, kind="ExternalOutput").ap()
    build(nc, a, out)
    got = run_bass_kernel_spmd(nc, [arrays], core_ids=[0])
    return got.results[0]["out"].reshape(SEQS, SEQ, DIM)
```

```python
from contextlib import ExitStack

import numpy as np
from concourse import mybir
import concourse.bass as bass

F32 = mybir.dt.float32
F32R = mybir.dt.float32r
ALU = mybir.AluOpType
ACT = mybir.ActivationFunctionType
AX = mybir.AxisListType

P = 128
SEQS, SEQ, DIM, CTX = 128, 64, 160, 256
TOKENS = SEQS * SEQ
TILES = 4
GROUP = TILES * P
GROUPS = TOKENS // GROUP
REM = DIM - P
COPIES = P // REM
HEADS = 20
INNER = HEADS * 64
UNITS = 10
BLOCKS = 8
EPS = 1e-5
FF = 640
FF_CHUNKS = FF // P
PIECE = 320


def back(g, u, n):
    return (g, u - n) if u >= n else (g - 1, u - n + UNITS)


def real(g):
    return not (isinstance(g, int) and g < 0)


def over_groups(engine, body):
    body(0, True, False, True)
    body(1, True, True, True)
    with engine.Fori(2, GROUPS - 1) as g:
        body(g, True, True, True)
    body(GROUPS - 1, True, True, False)
    body(GROUPS, False, True, False)


class Loads:

    def __init__(self, nc):
        self.staged = [nc.alloc_semaphore(f"w_staged{i}") for i in range(2)]
        self.rounded = nc.alloc_semaphore("w_rounded")
        self.split = nc.alloc_semaphore("w_split")
        self.loaded = nc.alloc_semaphore("w_loaded")
        self.arrivals, self.jobs, self.plain = [0, 0], 0, 0

    def plain_loads(self, sp, tiles):
        for tile, source in tiles:
            sp.dma_start(tile, source).then_inc(self.loaded, 16)


class Weights:

    def __init__(self, nc, ctx, tag, side, matrices):
        self.parts, self.jobs = [], []
        for n, (source, stacked) in enumerate(matrices):
            tiles, cols = source.shape[0] // P, source.shape[1]
            full = tiles - stacked
            hi, lo = (ctx.enter_context(nc.sbuf_tensor(f"{tag}_w{n}_{part}", [P, full, cols], F32R, side=side))
                      for part in ("hi", "lo"))
            rem = ctx.enter_context(nc.sbuf_tensor(f"{tag}_w{n}_rem", [P, cols], F32R, side=side)) if stacked else None
            self.parts.append((hi, lo, rem))
            for k in range(tiles):
                for c in range(0, cols, PIECE):
                    span = slice(c, min(c + PIECE, cols))
                    self.jobs.append((source[k * P:(k + 1) * P, span], hi[:, k, span] if k < full else rem[:, span],
                                      lo[:, k, span] if k < full else None))


class Splitter:

    TIMES = [(0, s) for s in range(4, UNITS)] + [(g, s) for g in (1, GROUPS - 1) for s in range(UNITS)]

    def __init__(self, nc, ctx, tag, loads, jobs):
        self.loads, self.jobs, self.first = loads, jobs, loads.jobs
        self.stage = [ctx.enter_context(nc.sbuf_tensor(f"{tag}_stage{i}", [P, PIECE], F32)) for i in range(2)]
        self.arrived = []
        for n in range(len(jobs)):
            loads.arrivals[n % 2] += 16
            self.arrived.append(loads.arrivals[n % 2])
        loads.jobs += len(jobs)
        assert len(jobs) <= len(self.TIMES)

    def load(self, act, n):
        if n < len(self.jobs):
            source, hi, lo = self.jobs[n]
            if n >= 2:
                act.wait_ge(self.loads.split, self.first + n - 1)
            act.dma_start(self.stage[n % 2][:, 0:source.shape[1]], source).then_inc(self.loads.staged[n % 2], 16)

    def round_hi(self, act, n):
        if n == 0:
            self.load(act, 0)
        self.load(act, n + 1)
        source, hi, lo = self.jobs[n]
        act.wait_ge(self.loads.staged[n % 2], self.arrived[n])
        act.activation(hi, self.stage[n % 2][:, 0:source.shape[1]], ACT.Copy).then_inc(self.loads.rounded, 1)

    def rest_lo(self, dve, n):
        source, hi, lo = self.jobs[n]
        stage, w = self.stage[n % 2], source.shape[1]
        dve.wait_ge(self.loads.rounded, self.first + n + 1)
        if lo is None:
            for r in (REM, 3 * REM):
                part = dve.tensor_tensor(hi[r:r + REM, :], stage[r:r + REM, 0:w], hi[r:r + REM, :].bitcast(F32),
                                         ALU.subtract)
        else:
            part = dve.tensor_tensor(lo, stage[:, 0:w], hi.bitcast(F32), ALU.subtract)
        part.then_inc(self.loads.split, 1)

    def at(self, body, step, split):
        if isinstance(body, int) and (body, step) in self.TIMES:
            n = self.TIMES.index((body, step))
            if n < len(self.jobs):
                split(n)


def row(v):
    return v.rearrange("(a n) -> a n", a=1).broadcast_to([P, v.shape[0]])


class Softmax:

    def __init__(self, nc, ctx, tag):
        def sem(name):
            return nc.alloc_semaphore(f"{tag}_{name}")

        def sb(name, shape):
            return ctx.enter_context(nc.sbuf_tensor(f"{tag}_{name}", shape, F32))

        def pb(name):
            return ctx.enter_context(nc.psum_tensor(f"{tag}_{name}", [P, 512], F32))

        self.scores = [pb(f"scores{i}") for i in range(2)]
        self.turned = [pb(f"turned{i}") for i in range(2)]
        self.out = pb("out")
        self.y = pb("y")
        self.proj = [pb(f"proj{i}") for i in range(2)]
        self.top = sb("top", [P, 2, BLOCKS])
        self.total = sb("total", [P, 2, BLOCKS])
        self.inverse = sb("inverse", [P, 2, BLOCKS])
        self.own = sb("own", [P, 2])
        self.factor = sb("factor", [P, 2, BLOCKS, 2])
        self.e = [sb(f"e{i}", [P, BLOCKS, 64]) for i in range(2)]
        self.prob = [sb(f"prob{i}", [P, BLOCKS, P]) for i in range(2)]
        self.probT = [sb(f"probT{i}", [P, BLOCKS, P]) for i in range(2)]
        self.scored = sem("scored")
        self.topped = sem("topped")
        self.shifted = sem("shifted")
        self.exped = sem("exped")
        self.summed = sem("summed")
        self.inverted = sem("inverted")
        self.factored = sem("factored")
        self.normed = sem("normed")
        self.transposed = sem("transposed")
        self.copied_a = sem("copied_a")
        self.copied_b = sem("copied_b")
        self.valued = sem("valued")
        self.set = sem("set")

    def constants(self, dve):
        for b in range(2):
            for c in range(2):
                dve.memset(self.own[b * 64:(b + 1) * 64, c:c + 1], float(b == c)).then_inc(self.set, 1)
        dve.wait_ge(self.set, 4)

    def maximum_and_shift(self, dve, g, u):
        r, s = u % 2, self.scores[u % 2][:].rearrange("p (k j) -> p k j", j=64)
        g2, u2 = back(g, u, 2)
        dve.wait_ge(self.scored, g * UNITS + u + 1)
        if real(g2):
            dve.wait_ge(self.shifted, g2 * UNITS + u2 + 1)
        dve.tensor_reduce(self.top[:, r, :], s, axis=AX.X, op=ALU.max).then_inc(self.topped, 1)
        dve.wait_ge(self.topped, g * UNITS + u + 1)
        if real(g2):
            dve.wait_ge(self.normed, g2 * UNITS + u2 + 1)
        dve.tensor_tensor(self.e[r][:], s, self.top[:, r, :].unsqueeze(2).broadcast_to([P, BLOCKS, 64]),
                          ALU.subtract).then_inc(self.shifted, 1)

    def sum_and_invert(self, dve, g, u):
        r = u % 2
        g2, u2 = back(g, u, 2)
        dve.wait_ge(self.exped, g * UNITS + u + 1)
        dve.tensor_reduce(self.total[:, r, :], self.e[r][:], axis=AX.X, op=ALU.add).then_inc(self.summed, 1)
        dve.wait_ge(self.summed, g * UNITS + u + 1)
        dve.reciprocal(self.inverse[:, r, :], self.total[:, r, :]).then_inc(self.inverted, 1)
        dve.wait_ge(self.inverted, g * UNITS + u + 1)
        if real(g2):
            dve.wait_ge(self.normed, g2 * UNITS + u2 + 1)
        dve.tensor_tensor(self.factor[:, r, :, :], self.inverse[:, r, :].unsqueeze(2).broadcast_to([P, BLOCKS, 2]),
                          self.own[:].unsqueeze(1).broadcast_to([P, BLOCKS, 2]), ALU.mult).then_inc(self.factored, 1)

    def copy_b(self, dve, g, u):
        g2, u2 = back(g, u, 2)
        dve.wait_ge(self.transposed, 2 * (g * UNITS + u) + 2)
        if real(g2):
            dve.wait_ge(self.valued, g2 * UNITS + u2 + 1)
        dve.tensor_copy(self.probT[u % 2][:, 4:8, :], self.turned[1][:].rearrange("p (k i) -> p k i", i=P))\
           .then_inc(self.copied_b, 1)

    def exponential(self, act, g, u, scale):
        act.wait_ge(self.shifted, g * UNITS + u + 1)
        act.activation(self.e[u % 2][:], self.e[u % 2][:], ACT.Exp, scale=scale).then_inc(self.exped, 1)

    def copy_a(self, act, g, u):
        g2, u2 = back(g, u, 2)
        act.wait_ge(self.transposed, 2 * (g * UNITS + u) + 1)
        if real(g2):
            act.wait_ge(self.valued, g2 * UNITS + u2 + 1)
        act.activation(self.probT[u % 2][:, 0:4, :], self.turned[0][:].rearrange("p (k i) -> p k i", i=P),
                       ACT.Copy).then_inc(self.copied_a, 1)

    def copy_both(self, act, g, u):
        self.copy_a(act, g, u)
        act.wait_ge(self.transposed, 2 * (g * UNITS + u) + 2)
        act.activation(self.probT[u % 2][:, 4:8, :], self.turned[1][:].rearrange("p (k i) -> p k i", i=P),
                       ACT.Copy).then_inc(self.copied_b, 1)

    def normalise(self, pool, g, u):
        r = u % 2
        g2, u2 = back(g, u, 2)
        pool.wait_ge(self.factored, g * UNITS + u + 1)
        if real(g2):
            pool.wait_ge(self.transposed, 2 * (g2 * UNITS + u2 + 1))
        pool.tensor_tensor(self.prob[r][:].rearrange("p k (b j) -> p k b j", b=2),
                           self.e[r][:].unsqueeze(2).broadcast_to([P, BLOCKS, 2, 64]),
                           self.factor[:, r, :, :].unsqueeze(3).broadcast_to([P, BLOCKS, 2, 64]),
                           ALU.mult).then_inc(self.normed, 1)

    def transpose(self, pe, identity, g, u):
        pe.wait_ge(self.normed, g * UNITS + u + 1)
        g1, u1 = back(g, u, 1)
        for half, copied in enumerate((self.copied_a, self.copied_b)):
            if real(g1):
                pe.wait_ge(copied, g1 * UNITS + u1 + 1)
            for k in range(4):
                last = pe.transpose(self.turned[half][:, k * P:(k + 1) * P],
                                    self.prob[u % 2][:, 4 * half + k, :], identity[:])
            last.then_inc(self.transposed, 1)


class Norm:

    def __init__(self, nc, ctx, tag):
        def sem(name):
            return nc.alloc_semaphore(f"{tag}_{name}")

        def sb(name, shape, dt=F32):
            return ctx.enter_context(nc.sbuf_tensor(f"{tag}_{name}", shape, dt))

        self.x = sb("x", [P, TILES, DIM])
        self.xr = sb("xr", [P, TILES, DIM])
        self.xo = sb("xo", [P, TILES, DIM])
        self.hat = sb("hat", [P, TILES, DIM])
        self.n = sb("n", [P, TILES, 2 * P])
        self.stats = sb("stats", [P, TILES, 6])
        self.mv = sb("mv", [P, TILES, 2])
        self.rstd = sb("rstd", [P, TILES])
        self.power = sb("power", [P, TILES])
        self.eps = sb("eps", [P, TILES])
        self.ahead = sb("ahead", [P, 1])
        self.gain, self.shift, self.bias = sb("gain", [P, DIM]), sb("shift", [P, DIM]), sb("bias", [P, DIM])
        self.hi = sb("hi", [P, 2, GROUP], F32R)
        self.lo = sb("lo", [P, GROUP], F32R)
        self.arrived = sem("arrived")
        self.again = sem("again")
        self.stored = sem("stored")
        self.set = sem("set")
        self.stat = sem("stat")
        self.var = sem("var")
        self.veps = sem("veps")
        self.root = sem("root")
        self.hatted = sem("hatted")
        self.gained = sem("gained")
        self.ready = sem("ready")
        self.turned = sem("turned")
        self.rounded = sem("rounded")
        self.split = sem("split")
        self.resid = sem("resid")
        self.multiplied = sem("multiplied")
        self.added = sem("added")

    def constants(self, pool):
        pool.memset(self.power[:], -0.5).then_inc(self.set, 1)
        pool.memset(self.eps[:], EPS).then_inc(self.set, 1)
        pool.wait_ge(self.set, 2)

    def load(self, sp, x_in, g):
        if real(g - 1):
            sp.wait_ge(self.hatted, TILES * g)
        sp.dma_start(self.x[:], x_in[g]).then_inc(self.arrived, 16)

    def load_again(self, sp, x_in, g):
        if real(g - 1):
            sp.wait_ge(self.added, TILES * g)
        sp.dma_start(self.xr[:], x_in[g]).then_inc(self.again, 16)

    def store(self, sp, x_out, g):
        sp.wait_ge(self.added, TILES * (g + 1))
        sp.dma_start(x_out[g], self.xo[:]).then_inc(self.stored, 16)

    def statistics(self, dve, g, t):
        if t == 0:
            dve.wait_ge(self.arrived, 16 * (g + 1))
            if real(g - 1):
                dve.wait_ge(self.hatted, TILES * g)
                dve.wait_ge(self.veps, g)
        dve.bn_stats(self.stats[:, t, :], self.x[:, t, :]).then_inc(self.stat, 1)
        dve.wait_ge(self.stat, TILES * g + t + 1)
        dve.memset(self.ahead[:], 0.0)
        dve.bn_aggr(self.mv[:, t, :], self.stats[:, t, :]).then_inc(self.var, 1)

    def inverse_root(self, pool, g):
        pool.wait_ge(self.var, TILES * (g + 1))
        if real(g - 1):
            pool.wait_ge(self.hatted, TILES * g)
        pool.tensor_tensor(self.rstd[:], self.mv[:, :, 1], self.eps[:], ALU.add).then_inc(self.veps, 1)
        pool.wait_ge(self.veps, g + 1)
        pool.tensor_tensor(self.rstd[:], self.rstd[:], self.power[:], ALU.pow).then_inc(self.root, 1)

    def normalise(self, dve, g, t):
        if t == 0:
            dve.wait_ge(self.root, g + 1)
            dve.wait_ge(self.var, TILES * (g + 1))
            if real(g - 1):
                dve.wait_ge(self.ready, 2 * g)
        dve.tensor_scalar(self.hat[:, t, :], self.x[:, t, :], self.mv[:, t, 0:1], self.rstd[:, t:t + 1],
                          ALU.subtract, ALU.mult).then_inc(self.hatted, 1)

    def affine(self, pool, g):
        pool.wait_ge(self.hatted, TILES * (g + 1))
        pool.tensor_tensor(self.hat[:], self.hat[:], self.gain[:].unsqueeze(1).broadcast_to([P, TILES, DIM]),
                           ALU.mult).then_inc(self.gained, 1)
        pool.wait_ge(self.gained, g + 1)
        if real(g - 1):
            pool.wait_ge(self.turned, 2 * g)
        pool.tensor_tensor(self.n[:, :, 0:P], self.hat[:, :, 0:P],
                           self.shift[:, 0:P].unsqueeze(1).broadcast_to([P, TILES, P]), ALU.add)\
            .then_inc(self.ready, 1)
        pool.tensor_tensor(self.n[:, :, P:2 * P].rearrange("p t (c r) -> p t c r", c=COPIES),
                           self.hat[:, :, P:DIM].unsqueeze(2).broadcast_to([P, TILES, COPIES, REM]),
                           self.shift[:, P:DIM].unsqueeze(1).unsqueeze(1).broadcast_to([P, TILES, COPIES, REM]),
                           ALU.add).then_inc(self.ready, 1)

    def transpose(self, pe, identity, banks, g, part):
        pe.wait_ge(self.ready, 2 * g + 2)
        for t in range(TILES):
            last = pe.transpose(banks[part][:, t * P:(t + 1) * P], self.n[:, t, part * P:(part + 1) * P], identity[:])
        last.then_inc(self.turned, 1)

    def round_hi(self, act, banks, g, part):
        act.wait_ge(self.turned, 2 * g + part + 1)
        act.activation(self.hi[:, part, :], banks[part][:], ACT.Copy).then_inc(self.rounded, 1)

    def rest_lo(self, dve, banks, g, part):
        dve.wait_ge(self.rounded, 2 * g + part + 1)
        if part == 0:
            dve.tensor_tensor(self.lo[:], banks[0][:], self.hi[:, 0, :].bitcast(F32), ALU.subtract)\
               .then_inc(self.split, 1)
        else:
            dve.tensor_tensor(self.hi[64:P, 1, :], banks[1][64:P, :], self.hi[64:P, 1, :].bitcast(F32),
                              ALU.subtract).then_inc(self.split, 1)

    def residual(self, pool, g):
        pool.wait_ge(self.again, 16 * (g + 1))
        pool.tensor_tensor(self.xr[:], self.xr[:], self.bias[:].unsqueeze(1).broadcast_to([P, TILES, DIM]),
                           ALU.add).then_inc(self.resid, 1)

    def add(self, dve, bank, g, t):
        dve.wait_ge(self.multiplied, TILES * g + t + 1)
        if t == 0:
            dve.wait_ge(self.resid, g + 1)
            if real(g - 1):
                dve.wait_ge(self.stored, 16 * g)
        dve.tensor_tensor(self.xo[:, t, :], bank[:, 0:DIM], self.xr[:, t, :], ALU.add).then_inc(self.added, 1)


def attention(nc, tag, loads, weights, following, x_dram, ctx_dram, out_dram, identity, wo, bo, gain, shift):
    cross = ctx_dram is not None
    x_in = x_dram.rearrange("(g t p) c -> g p t c", t=TILES, p=P)
    x_out = out_dram.rearrange("(g t p) c -> g p t c", t=TILES, p=P)
    with ExitStack() as ctx:
        def sem(name):
            return nc.alloc_semaphore(f"{tag}_{name}")

        def sb(name, shape, dt=F32):
            return ctx.enter_context(nc.sbuf_tensor(f"{tag}_{name}", shape, dt))

        (q_hi, q_lo, q_rem), (k_hi, k_lo, k_rem), (v_hi, v_lo, v_rem) = weights.parts
        wo_sb = sb("wo", [P, UNITS, DIM])
        ln = Norm(nc, ctx, tag + "_ln")
        plain = [(ln.gain[:], row(gain)), (ln.shift[:], row(shift)), (ln.bias[:], row(bo)),
                 (wo_sb[:], wo.rearrange("(u p) c -> p u c", p=P))]
        loads.plain += 16 * len(plain)
        loaded = loads.plain
        splitter = Splitter(nc, ctx, tag, loads, following.jobs)

        sm = Softmax(nc, ctx, tag + "_sm")
        queries = [sb(f"queries{i}", [P, GROUP]) for i in range(2)]
        keys = [sb(f"keys{i}", [P, BLOCKS, P]) for i in range(2)]
        values = sb("values", [P, TILES, INNER])
        outs = sb("outs", [P, UNITS, GROUP])
        q_out = sem("q_out")
        k_out = sem("k_out")
        v_out = sem("v_out")
        q_in = sem("q_in")
        k_in_a = sem("k_in_a")
        k_in_b = sem("k_in_b")
        v_in = sem("v_in")
        o_in = sem("o_in")
        zeros = sem("zeros")
        if cross:
            c_x = sb("c_x", [P, TILES, CTX])
            c_hi, c_lo = sb("c_hi", [P, 2, GROUP], F32R), sb("c_lo", [P, 2, GROUP], F32R)
            ctx_in = ctx_dram.rearrange("(g t p) c -> g p t c", t=TILES, p=P)
            c_arrived = sem("c_arrived")
            c_turned = sem("c_turned")
            c_rounded = sem("c_rounded")
            c_split = sem("c_split")
            c_bank = [sm.y, sm.proj[1]]

        v_slots = [[(t, 0, 512)] for t in range(TILES)] + [[(t, 512, 512)] for t in range(TILES)] \
            + [[(t, 1024, 256), (t + 1, 1024, 256)] for t in (0, 2)]
        v_last_user = [3] * 4 + [7] * 4 + [9] * 2

        block = ctx.enter_context(nc.Block())

        @block.sync
        def _(sp):
            def load_ctx(g):
                if real(g - 1):
                    sp.wait_ge(c_turned, 2 * g)
                sp.dma_start(c_x[:], ctx_in[g]).then_inc(c_arrived, 16)

            def body(g, front, tail, ahead):
                if isinstance(g, int) and g == 0:
                    ln.load(sp, x_in, 0)
                    if cross:
                        load_ctx(0)
                    loads.plain_loads(sp, plain)
                if ahead:
                    ln.load(sp, x_in, g + 1)
                    if cross:
                        load_ctx(g + 1)
                if tail:
                    ln.store(sp, x_out, g - 1)
                if front:
                    ln.load_again(sp, x_in, g)

            over_groups(sp, body)
            sp.wait_ge(ln.stored, 16 * GROUPS)

        @block.gpsimd
        def _(pool):
            ln.constants(pool)
            pool.wait_ge(loads.loaded, loaded)
            for i in range(2):
                pool.memset(keys[i][:], 0.0).then_inc(zeros, 1)

            def body(g, front, tail, ahead):
                if isinstance(g, int) and g == 0:
                    ln.inverse_root(pool, 0)
                    ln.affine(pool, 0)
                for s in range(UNITS):
                    u1 = s - 1
                    if u1 < 0 and tail:
                        sm.normalise(pool, g - 1, UNITS - 1)
                    elif u1 >= 0 and front:
                        sm.normalise(pool, g, u1)
                    if s == 2 and tail:
                        ln.residual(pool, g - 1)
                    if s == 6 and ahead:
                        ln.inverse_root(pool, g + 1)
                    if s == 8 and ahead:
                        ln.affine(pool, g + 1)

            over_groups(pool, body)

        @block.scalar
        def _(act):
            def queries_in(g, s):
                g2, u2 = back(g, s, 2)
                act.wait_ge(q_out, g * UNITS + s + 1)
                if real(g2):
                    act.wait_ge(sm.scored, g2 * UNITS + u2 + 1)
                act.activation(queries[s % 2][:], sm.proj[s % 2][:], ACT.Copy).then_inc(q_in, 1)

            def output(g, u):
                act.wait_ge(sm.valued, g * UNITS + u + 1)
                act.activation(outs[:, u, :], sm.out[:], ACT.Copy).then_inc(o_in, 1)

            def body(g, front, tail, ahead):
                for s in range(UNITS):
                    if s == 0 and front:
                        for part in range(2):
                            ln.round_hi(act, sm.proj, g, part)
                    elif front:
                        queries_in(g, s)
                    if s < 4 and tail:
                        output(*back(g, s, 4))
                    if s > 4 and front:
                        output(*back(g, s, 4))
                    if front if s >= 1 else tail:
                        sm.exponential(act, *back(g, s, 1), 64 ** -0.5)
                    if s == 0:
                        if tail:
                            sm.copy_a(act, *back(g, s, 3))
                        if front and cross:
                            for c in range(2):
                                act.wait_ge(c_turned, 2 * g + c + 1)
                                act.activation(c_hi[:, c, :], c_bank[c][:], ACT.Copy).then_inc(c_rounded, 1)
                        if front:
                            queries_in(g, s)
                    if front:
                        act.wait_ge(k_out, g * UNITS + s + 1)
                        if isinstance(g, int) and g == 0 and s == 0:
                            act.wait_ge(zeros, 2)
                        act.activation(keys[s % 2][0:64, :, 0:64],
                                       sm.proj[(s + 1) % 2][0:64, :].rearrange("p (b j) -> p b j", j=64),
                                       ACT.Copy).then_inc(k_in_a, 1)
                    if s > 0 and (front if s >= 3 else tail):
                        sm.copy_a(act, *back(g, s, 3))
                    if front:
                        act.wait_ge(v_out, g * UNITS + s + 1)
                        if real(g - 1):
                            act.wait_ge(sm.valued, (g - 1) * UNITS + v_last_user[s] + 1)
                        pieces = v_slots[s]
                        t0, c0, n = pieces[0]
                        act.activation(values[:, t0:t0 + len(pieces), c0:c0 + n],
                                       sm.proj[s % 2][:].rearrange("p (t c) -> p t c", c=n),
                                       ACT.Copy).then_inc(v_in, 1)
                    if s == 4 and front:
                        output(g, 0)
                    splitter.at(g, s, lambda n: splitter.round_hi(act, n))

            over_groups(act, body)

        @block.vector
        def _(dve):
            sm.constants(dve)

            def body(g, front, tail, ahead):
                if isinstance(g, int) and g == 0:
                    for t in range(TILES):
                        ln.statistics(dve, 0, t)
                    for t in range(TILES):
                        ln.normalise(dve, 0, t)
                for s in range(UNITS):
                    if front if s >= 1 else tail:
                        sm.maximum_and_shift(dve, *back(g, s, 1))
                    if s == 0 and front:
                        for part in range(2):
                            ln.rest_lo(dve, sm.proj, g, part)
                    if s == 0 and tail:
                        sm.copy_b(dve, *back(g, s, 3))
                    if s == 0 and front and cross:
                        for c in range(2):
                            dve.wait_ge(c_rounded, 2 * g + c + 1)
                            dve.tensor_tensor(c_lo[:, c, :], c_bank[c][:], c_hi[:, c, :].bitcast(F32),
                                              ALU.subtract).then_inc(c_split, 1)
                    if s == 4 and tail:
                        ln.add(dve, sm.y, g - 1, 0)
                    if front:
                        g2, u2 = back(g, s, 2)
                        dve.wait_ge(k_out, g * UNITS + s + 1)
                        if real(g2):
                            dve.wait_ge(sm.scored, g2 * UNITS + u2 + 1)
                        if isinstance(g, int) and g == 0 and s == 0:
                            dve.wait_ge(zeros, 2)
                        dve.tensor_copy(keys[s % 2][64:P, :, 64:P],
                                        sm.proj[(s + 1) % 2][64:P, :].rearrange("p (b j) -> p b j", j=64))\
                           .then_inc(k_in_b, 1)
                    if s == 4 and tail:
                        ln.add(dve, sm.y, g - 1, 1)
                        ln.add(dve, sm.y, g - 1, 2)
                    if front if s >= 1 else tail:
                        sm.sum_and_invert(dve, *back(g, s, 1))
                    if s > 0 and (front if s >= 3 else tail):
                        sm.copy_b(dve, *back(g, s, 3))
                    if s == 4 and tail:
                        ln.add(dve, sm.y, g - 1, 3)
                    if ahead and s in (5, 6):
                        for t in (2 * (s - 5), 2 * (s - 5) + 1):
                            ln.statistics(dve, g + 1, t)
                    if ahead and s in (7, 8):
                        for t in (2 * (s - 7), 2 * (s - 7) + 1):
                            ln.normalise(dve, g + 1, t)
                    splitter.at(g, s, lambda n: splitter.rest_lo(dve, n))

            over_groups(dve, body)

        @block.tensor
        def _(pe):
            def project_queries(g, u):
                cols, bank = slice(u * P, (u + 1) * P), sm.proj[u % 2]
                if u == 0:
                    pe.wait_ge(ln.split, 2 * g + 2)
                else:
                    pe.wait_ge(k_in_a, g * UNITS + u)
                    pe.wait_ge(k_in_b, g * UNITS + u)
                parts = [(q_hi[:, 0, cols], ln.hi[:, 0, :]), (q_lo[:, 0, cols], ln.hi[:, 0, :]),
                         (q_hi[:, 0, cols], ln.lo[:]), (q_rem[:, cols], ln.hi[:, 1, :])]
                for n, (w, moving) in enumerate(parts):
                    last = pe.matmul(bank[:], w, moving, start=n == 0, stop=n == len(parts) - 1)
                last.then_inc(q_out, 1)

            def project_keys(g, u):
                cols, bank = slice(u * P, (u + 1) * P), sm.proj[(u + 1) % 2]
                if u == 0:
                    if cross:
                        pe.wait_ge(c_split, 2 * g + 2)
                else:
                    pe.wait_ge(v_in, g * UNITS + u)
                if cross:
                    parts = [(k_hi[:, c, cols], c_hi[:, c, :]) for c in range(2)] \
                        + [(k_lo[:, c, cols], c_hi[:, c, :]) for c in range(2)] \
                        + [(k_hi[:, c, cols], c_lo[:, c, :]) for c in range(2)]
                else:
                    parts = [(k_hi[:, 0, cols], ln.hi[:, 0, :]), (k_lo[:, 0, cols], ln.hi[:, 0, :]),
                             (k_hi[:, 0, cols], ln.lo[:]), (k_rem[:, cols], ln.hi[:, 1, :])]
                for n, (w, moving) in enumerate(parts):
                    last = pe.matmul(bank[:], w, moving, start=n == 0, stop=n == len(parts) - 1)
                last.then_inc(k_out, 1)

            def project_values(g, s):
                pe.wait_ge(q_in, g * UNITS + s + 1)
                for i, (t, c0, n) in enumerate(v_slots[s]):
                    tok, cols = slice(t * P, (t + 1) * P), slice(c0, c0 + n)
                    if cross:
                        parts = [(c_hi[:, c, tok], v_hi[:, c, cols]) for c in range(2)] \
                            + [(c_lo[:, c, tok], v_hi[:, c, cols]) for c in range(2)] \
                            + [(c_hi[:, c, tok], v_lo[:, c, cols]) for c in range(2)]
                    else:
                        parts = [(ln.hi[:, 0, tok], v_hi[:, 0, cols]), (ln.lo[:, tok], v_hi[:, 0, cols]),
                                 (ln.hi[:, 0, tok], v_lo[:, 0, cols]), (ln.hi[:, 1, tok], v_rem[:, cols])]
                    for k, (w, moving) in enumerate(parts):
                        last = pe.matmul(sm.proj[s % 2][:, i * n:(i + 1) * n], w, moving,
                                         start=k == 0, stop=k == len(parts) - 1)
                last.then_inc(v_out, 1)

            def score(g, u):
                g2, u2 = back(g, u, 2)
                pe.wait_ge(q_in, g * UNITS + u + 1)
                pe.wait_ge(k_in_a, g * UNITS + u + 1)
                pe.wait_ge(k_in_b, g * UNITS + u + 1)
                if real(g2):
                    pe.wait_ge(sm.shifted, g2 * UNITS + u2 + 1)
                for t in range(TILES):
                    for b in range(2):
                        seq = 2 * t + b
                        last = pe.matmul(sm.scores[u % 2][b * 64:(b + 1) * 64, t * P:(t + 1) * P],
                                         queries[u % 2][:, seq * 64:(seq + 1) * 64], keys[u % 2][:, seq, :],
                                         start=True, stop=True)
                last.then_inc(sm.scored, 1)

            def times_values(g, u):
                g1, u1 = back(g, u, 1)
                pe.wait_ge(sm.copied_a, g * UNITS + u + 1)
                pe.wait_ge(sm.copied_b, g * UNITS + u + 1)
                pe.wait_ge(v_in, g * UNITS + (4 if u < 4 else 8 if u < 8 else 10))
                if real(g1):
                    pe.wait_ge(o_in, g1 * UNITS + u1 + 1)
                for t in range(TILES):
                    for h in range(2):
                        head = 2 * u + h
                        last = pe.matmul(sm.out[h * 64:(h + 1) * 64, t * P:(t + 1) * P],
                                         values[:, t, head * 64:(head + 1) * 64], sm.probT[u % 2][:, 2 * t + h, :],
                                         start=True, stop=True)
                last.then_inc(sm.valued, 1)

            def project_out(g, t):
                pe.wait_ge(o_in, g * UNITS + UNITS)
                if t > 0:
                    pe.wait_ge(ln.added, TILES * g + t)
                elif real(g - 2):
                    pe.wait_ge(ln.added, TILES * g)
                for u in range(UNITS):
                    last = pe.matmul(sm.y[:, 0:DIM], outs[:, u, t * P:(t + 1) * P], wo_sb[:, u, :],
                                     start=u == 0, stop=u == UNITS - 1)
                last.then_inc(ln.multiplied, 1)

            def turn(g, part):
                if real(g - 1):
                    if part == 0:
                        pe.wait_ge(k_in_a, g * UNITS)
                        pe.wait_ge(k_in_b, g * UNITS)
                    else:
                        pe.wait_ge(v_in, g * UNITS)
                ln.transpose(pe, identity, sm.proj, g, part)

            def turn_context(g, c):
                pe.wait_ge(c_arrived, 16 * (g + 1))
                if c == 1:
                    pe.wait_ge(ln.split, 2 * g + 2)
                elif real(g - 2):
                    pe.wait_ge(ln.added, TILES * (g - 1))
                for t in range(TILES):
                    last = pe.transpose(c_bank[c][:, t * P:(t + 1) * P], c_x[:, t, c * P:(c + 1) * P], identity[:])
                last.then_inc(c_turned, 1)

            def body(g, front, tail, ahead):
                for s in range(UNITS):
                    if s > 0 and front:
                        project_queries(g, s)
                    if s == 4 and tail:
                        project_out(g - 1, 0)
                    if front if s >= 1 else tail:
                        score(*back(g, s, 1))
                    if s == 0 and front:
                        for part in range(2):
                            turn(g, part)
                        if cross:
                            turn_context(g, 0)
                    if s < 4 and tail:
                        times_values(*back(g, s, 4))
                    if s > 4 and front:
                        times_values(*back(g, s, 4))
                    if s == 0:
                        if tail:
                            sm.transpose(pe, identity, *back(g, s, 3))
                        if front and cross:
                            turn_context(g, 1)
                        if front:
                            project_queries(g, s)
                    if front:
                        project_keys(g, s)
                    if s == 4 and tail:
                        project_out(g - 1, 1)
                    if s > 0 and (front if s >= 3 else tail):
                        sm.transpose(pe, identity, *back(g, s, 3))
                    if s == 4 and tail:
                        project_out(g - 1, 2)
                    if front:
                        project_values(g, s)
                    if s == 4 and tail:
                        project_out(g - 1, 3)
                    if s == 4 and front:
                        times_values(g, 0)

            pe.wait_ge(loads.loaded, loaded)
            over_groups(pe, body)


def feed_forward(nc, tag, loads, weights, x_dram, out_dram, identity, b1, w2, b2, gain, shift):
    x_in = x_dram.rearrange("(g t p) c -> g p t c", t=TILES, p=P)
    x_out = out_dram.rearrange("(g t p) c -> g p t c", t=TILES, p=P)
    with ExitStack() as ctx:
        def sem(name):
            return nc.alloc_semaphore(f"{tag}_{name}")

        def sb(name, shape, dt=F32):
            return ctx.enter_context(nc.sbuf_tensor(f"{tag}_{name}", shape, dt))

        def pb(name):
            return ctx.enter_context(nc.psum_tensor(f"{tag}_{name}", [P, 512], F32))

        w_hi, w_lo, w_rem = weights.parts[0]
        w2_sb = sb("w2", [P, FF_CHUNKS, DIM])
        b1_sb = sb("b1", [P, 2 * FF_CHUNKS])
        ln = Norm(nc, ctx, tag + "_ln")
        plain = [(ln.gain[:], row(gain)), (ln.shift[:], row(shift)), (ln.bias[:], row(b2)), (b1_sb[:], b1),
                 (w2_sb[:], w2.rearrange("(c p) n -> p c n", p=P))]
        loads.plain += 16 * len(plain)
        loaded = loads.plain

        gate = [sb(f"gate{i}", [P, GROUP]) for i in range(2)]
        hidden = sb("hidden", [P, FF_CHUNKS, GROUP])
        banks = [pb(f"turn{i}") for i in range(2)]
        psa, psg = [pb(f"a{i}") for i in range(2)], [pb(f"gate_p{i}") for i in range(2)]
        psy = [pb(f"y{i}") for i in range(2)]
        a_out = sem("a_out")
        g_out = sem("g_out")
        gelued = sem("gelued")
        gated = sem("gated")

        block = ctx.enter_context(nc.Block())

        @block.sync
        def _(sp):
            def body(g, front, tail, ahead):
                if isinstance(g, int) and g == 0:
                    ln.load(sp, x_in, 0)
                    loads.plain_loads(sp, plain)
                if ahead:
                    ln.load(sp, x_in, g + 1)
                if tail:
                    ln.store(sp, x_out, g - 1)
                if front:
                    ln.load_again(sp, x_in, g)

            over_groups(sp, body)
            sp.wait_ge(ln.stored, 16 * GROUPS)

        @block.gpsimd
        def _(pool):
            ln.constants(pool)
            pool.wait_ge(loads.loaded, loaded)

            def body(g, front, tail, ahead):
                if isinstance(g, int) and g == 0:
                    ln.inverse_root(pool, 0)
                    ln.affine(pool, 0)
                if ahead:
                    ln.inverse_root(pool, g + 1)
                if ahead:
                    ln.affine(pool, g + 1)
                if front:
                    ln.residual(pool, g)

            over_groups(pool, body)

        def chunk_back(g, j, n):
            return (g, j - n) if j >= n else (g - 1, j - n + FF_CHUNKS)

        @block.scalar
        def _(act):
            def body(g, front, tail, ahead):
                if front:
                    for part in range(2):
                        ln.round_hi(act, banks, g, part)
                    for j in range(FF_CHUNKS):
                        g2, j2 = chunk_back(g, j, 2) if j >= 2 else (g - 1, FF_CHUNKS - 1)
                        act.wait_ge(g_out, g * FF_CHUNKS + j + 1)
                        if real(g2):
                            act.wait_ge(gated, g2 * FF_CHUNKS + j2 + 1)
                        act.activation(gate[j % 2][:], psg[j % 2][:], ACT.Gelu,
                                       bias=b1_sb[:, FF_CHUNKS + j:FF_CHUNKS + j + 1]).then_inc(gelued, 1)

            act.wait_ge(loads.loaded, loaded)
            over_groups(act, body)

        @block.vector
        def _(dve):
            def body(g, front, tail, ahead):
                if isinstance(g, int) and g == 0:
                    for t in range(TILES):
                        ln.statistics(dve, 0, t)
                    for t in range(TILES):
                        ln.normalise(dve, 0, t)
                if front:
                    for part in range(2):
                        ln.rest_lo(dve, banks, g, part)
                if ahead:
                    for t in range(TILES):
                        ln.statistics(dve, g + 1, t)
                if tail:
                    for t in range(TILES):
                        ln.add(dve, psy[t % 2], g - 1, t)
                for j in range(FF_CHUNKS):
                    if front:
                        dve.wait_ge(gelued, g * FF_CHUNKS + j + 1)
                        dve.wait_ge(a_out, g * FF_CHUNKS + j + 1)
                        dve.scalar_tensor_tensor(hidden[:, j, :], psa[j % 2][:], b1_sb[:, j:j + 1], gate[j % 2][:],
                                                 ALU.add, ALU.mult).then_inc(gated, 1)
                    if ahead and j == 0:
                        for t in range(TILES):
                            ln.normalise(dve, g + 1, t)

            dve.wait_ge(loads.loaded, loaded)
            over_groups(dve, body)

        @block.tensor
        def _(pe):
            def body(g, front, tail, ahead):
                if front:
                    if real(g - 1):
                        pe.wait_ge(ln.split, 2 * g)
                    for part in range(2):
                        ln.transpose(pe, identity, banks, g, part)
                if tail:
                    pe.wait_ge(gated, g * FF_CHUNKS)
                    for t in range(TILES):
                        if t >= 2:
                            pe.wait_ge(ln.added, TILES * (g - 1) + t - 1)
                        elif not isinstance(g, int) or g > 1:
                            pe.wait_ge(ln.added, TILES * (g - 1))
                        for j in range(FF_CHUNKS):
                            last = pe.matmul(psy[t % 2][:, 0:DIM], hidden[:, j, t * P:(t + 1) * P], w2_sb[:, j, :],
                                             start=j == 0, stop=j == FF_CHUNKS - 1)
                        last.then_inc(ln.multiplied, 1)
                if front:
                    pe.wait_ge(ln.split, 2 * g + 2)
                    for j in range(FF_CHUNKS):
                        g2, j2 = (g, j - 2) if j >= 2 else (g - 1, FF_CHUNKS - 1)
                        for bank, c, done in ((psg[j % 2], FF_CHUNKS + j, g_out), (psa[j % 2], j, a_out)):
                            if real(g2):
                                pe.wait_ge(gated, g2 * FF_CHUNKS + j2 + 1)
                            cols = slice(c * P, (c + 1) * P)
                            parts = [(w_hi[:, 0, cols], ln.hi[:, 0, :]), (w_lo[:, 0, cols], ln.hi[:, 0, :]),
                                     (w_hi[:, 0, cols], ln.lo[:]), (w_rem[:, cols], ln.hi[:, 1, :])]
                            for n, (w, moving) in enumerate(parts):
                                last = pe.matmul(bank[:], w, moving, start=n == 0, stop=n == len(parts) - 1)
                            last.then_inc(done, 1)

            pe.wait_ge(loads.loaded, loaded)
            over_groups(pe, body)


def ip_attention(nc, tag, loads, weights, following, x_dram, ctx_dram, out_dram, identity, eye, mask, wv, wo, bo):
    quads, pair = 5, 2 * P
    pools = (1, 4, 7, 8)

    def masked_before(g, u, by_pool):
        mine = [v for v in range(UNITS) if (v in pools) == by_pool]
        return g * len(mine) + sum(v < u for v in mine)

    x_in = x_dram.rearrange("(g t p) c -> g p t c", t=TILES, p=P)
    ctx_in = ctx_dram.rearrange("(g t p) c -> g p t c", t=TILES, p=P)
    x_out = out_dram.rearrange("(g t p) c -> g p t c", t=TILES, p=P)
    with ExitStack() as ctx:
        def sem(name):
            return nc.alloc_semaphore(f"{tag}_{name}")

        def sb(name, shape, dt=F32):
            return ctx.enter_context(nc.sbuf_tensor(f"{tag}_{name}", shape, dt))

        (q_hi, q_lo, q_rem), (k_hi, k_lo, _) = weights.parts
        wv_sb = sb("wv", [P, 2, DIM])
        wo_sb = sb("wo", [P, 2, DIM])
        mask_sb = sb("mask", [P, quads, 4])
        bias = sb("bias", [P, DIM])
        plain = [(identity[:], eye), (mask_sb[:], mask), (bias[:], row(bo)),
                 (wv_sb[:], wv.rearrange("(c p) n -> p c n", p=P)), (wo_sb[:], wo.rearrange("(c p) n -> p c n", p=P))]
        loads.plain += 16 * len(plain)
        loaded = loads.plain
        own = Splitter(nc, ctx, tag + "_own", loads, weights.jobs)
        splitter = Splitter(nc, ctx, tag, loads, following.jobs)

        sm = Softmax(nc, ctx, tag + "_sm")
        x = sb("x", [P, TILES, DIM])
        xn = sb("xn", [P, TILES, 2 * P])
        xr = sb("xr", [P, TILES, DIM])
        xo = sb("xo", [P, TILES, DIM])
        hi, lo = sb("hi", [P, 2, GROUP], F32R), sb("lo", [P, GROUP], F32R)
        c_x = sb("c_x", [P, TILES, CTX])
        c_t = sb("c_t", [P, 2, GROUP])
        c_hi, c_lo = sb("c_hi", [P, 2, GROUP], F32R), sb("c_lo", [P, 2, GROUP], F32R)
        queries = sb("queries", [P, 2, GROUP])
        keys = sb("keys", [P, 2, GROUP])
        diagonal = [sb(f"diagonal{i}", [P, 4, 4, 64]) for i in range(2)]
        values = sb("values", [P, TILES, HEADS, 32])
        outs = sb("outs", [P, 2, GROUP])
        arrived, again, stored, c_arrived = sem("arrived"), sem("again"), sem("stored"), sem("c_arrived")
        spread = sem("spread")
        turned = sem("turned")
        rounded = sem("rounded")
        split = sem("split")
        c_kept = sem("c_kept")
        q_out, q_in = sem("q_out"), sem("q_in")
        k_out, k_in = sem("k_out"), sem("k_in")
        v_out, v_in = sem("v_out"), sem("v_in")
        masked_v, masked_g = sem("masked_v"), sem("masked_g")
        zeros = sem("zeros")
        o_in = sem("o_in")
        resid = sem("resid")
        multiplied, added = sem("multiplied"), sem("added")

        def diagonal_keys(engine, g, u):
            tp, q = divmod(u, quads)
            g2, u2 = back(g, u, 2)
            if u in (0, 1, 4):
                engine.wait_ge(k_in, 2 * g + (2 if u == 4 else 1))
            elif u in pools:
                engine.wait_ge(k_in, 2 * g + 2)
            if real(g2):
                engine.wait_ge(sm.scored, g2 * UNITS + u2 + 1)
            seqs = keys[:, q // 4, tp * pair:(tp + 1) * pair].rearrange("p (b j) -> p b j", j=64)
            engine.tensor_tensor(diagonal[u % 2][:], seqs.unsqueeze(2).broadcast_to([P, 4, 4, 64]),
                                 mask_sb[:, q, :].unsqueeze(1).unsqueeze(3).broadcast_to([P, 4, 4, 64]),
                                 ALU.mult).then_inc(masked_g if u in pools else masked_v, 1)

        block = ctx.enter_context(nc.Block())

        @block.sync
        def _(sp):
            def load(g):
                if real(g - 1):
                    sp.wait_ge(spread, 2 * g)
                sp.dma_start(x[:], x_in[g]).then_inc(arrived, 16)
                if real(g - 1):
                    sp.wait_ge(turned, 4 * g)
                sp.dma_start(c_x[:], ctx_in[g]).then_inc(c_arrived, 16)

            def body(g, front, tail, ahead):
                if isinstance(g, int) and g == 0:
                    load(0)
                    loads.plain_loads(sp, plain)
                if ahead:
                    load(g + 1)
                if tail:
                    sp.wait_ge(added, TILES * g)
                    sp.dma_start(x_out[g - 1], xo[:]).then_inc(stored, 16)
                if front:
                    if real(g - 1):
                        sp.wait_ge(added, TILES * g)
                    sp.dma_start(xr[:], x_in[g]).then_inc(again, 16)

            over_groups(sp, body)
            sp.wait_ge(stored, 16 * GROUPS)

        @block.gpsimd
        def _(pool):
            pool.memset(values[:], 0.0).then_inc(zeros, 1)
            pool.wait_ge(loads.loaded, loaded)

            def body(g, front, tail, ahead):
                for s in range(UNITS):
                    if front and s + 1 in pools:
                        diagonal_keys(pool, g, s + 1)
                    if front if s >= 1 else tail:
                        sm.normalise(pool, *back(g, s, 1))
                    if s == 2 and tail:
                        pool.wait_ge(again, 16 * g)
                        pool.tensor_tensor(xr[:], xr[:], bias[:].unsqueeze(1).broadcast_to([P, TILES, DIM]),
                                           ALU.add).then_inc(resid, 1)

            over_groups(pool, body)

        @block.scalar
        def _(act):
            def spread_x(g):
                act.wait_ge(arrived, 16 * (g + 1))
                if real(g - 1):
                    act.wait_ge(turned, 4 * (g - 1) + 2)
                act.activation(xn[:, :, 0:P], x[:, :, 0:P], ACT.Copy).then_inc(spread, 1)
                act.activation(xn[:, :, P:2 * P].rearrange("p t (c r) -> p t c r", c=COPIES),
                                 x[:, :, P:DIM].unsqueeze(2).broadcast_to([P, TILES, COPIES, REM]), ACT.Copy).then_inc(spread, 1)

            def round_hi(g, part):
                act.wait_ge(turned, 4 * g + part + 1)
                if part < 2:
                    act.activation(hi[:, part, :], sm.proj[part][:], ACT.Copy).then_inc(rounded, 1)
                else:
                    act.activation(c_hi[:, part - 2, :], sm.proj[part - 2][:], ACT.Copy).then_inc(rounded, 1)
                    act.activation(c_t[:, part - 2, :], sm.proj[part - 2][:], ACT.Copy).then_inc(c_kept, 1)

            def queries_and_keys_in(g, c):
                act.wait_ge(q_out, 2 * g + c + 1)
                if real(g - 1):
                    act.wait_ge(sm.scored, (g - 1) * UNITS + 9 + c)
                act.activation(queries[:, c, :], sm.proj[0][:], ACT.Copy).then_inc(q_in, 1)
                act.wait_ge(k_out, 2 * g + c + 1)
                if real(g - 1):
                    act.wait_ge(masked_v, masked_before(g - 1, 9 + c, False))
                    act.wait_ge(masked_g, masked_before(g - 1, 9 + c, True))
                act.activation(keys[:, c, :], sm.proj[1][:], ACT.Copy).then_inc(k_in, 1)

            def body(g, front, tail, ahead):
                if isinstance(g, int) and g == 0:
                    for n in range(len(own.jobs)):
                        own.round_hi(act, n)
                    spread_x(0)
                    for part in range(4):
                        round_hi(0, part)
                    queries_and_keys_in(0, 0)
                for s in range(UNITS):
                    if s == 4 and ahead:
                        spread_x(g + 1)
                    if front if s >= 1 else tail:
                        sm.exponential(act, *back(g, s, 1), 8 ** -0.5)
                    if s in (6, 7) and ahead:
                        round_hi(g + 1, 2 * (s - 6))
                        round_hi(g + 1, 2 * (s - 6) + 1)
                    if front if s >= 3 else tail:
                        sm.copy_both(act, *back(g, s, 3))
                    if s == 1 and front:
                        queries_and_keys_in(g, 1)
                    if s == 9 and ahead:
                        queries_and_keys_in(g + 1, 0)
                    for at, there, tp in ((8, front, 0), (3, tail, 1)):
                        if s == at and there:
                            go = g if tp == 0 else g - 1
                            act.wait_ge(sm.valued, go * UNITS + 5 * tp + 5)
                            if tp == 0 and real(g - 1):
                                act.wait_ge(multiplied, TILES * g)
                            act.activation(outs[:, :, tp * pair:(tp + 1) * pair],
                                           sm.out[:].rearrange("p (c n) -> p c n", c=2), ACT.Copy).then_inc(o_in, 1)
                    splitter.at(g, s, lambda n: splitter.round_hi(act, n))

            over_groups(act, body)

        @block.vector
        def _(dve):
            sm.constants(dve)
            dve.wait_ge(loads.loaded, loaded)

            def rest_lo(g, part):
                dve.wait_ge(rounded, 4 * g + part + 1)
                if part == 0:
                    dve.tensor_tensor(lo[:], sm.proj[0][:], hi[:, 0, :].bitcast(F32), ALU.subtract).then_inc(split, 1)
                elif part == 1:
                    dve.tensor_tensor(hi[64:P, 1, :], sm.proj[1][64:P, :], hi[64:P, 1, :].bitcast(F32),
                                      ALU.subtract).then_inc(split, 1)
                else:
                    dve.wait_ge(c_kept, 2 * g + part - 1)
                    dve.tensor_tensor(c_lo[:, part - 2, :], sm.proj[part - 2][:],
                                      c_hi[:, part - 2, :].bitcast(F32), ALU.subtract).then_inc(split, 1)

            def values_in(g, tp):
                dve.wait_ge(v_out, 2 * g + tp + 1)
                if isinstance(g, int) and g == 0:
                    dve.wait_ge(zeros, 1)
                else:
                    dve.wait_ge(sm.valued, g * UNITS)
                for h in range(4):
                    last = dve.tensor_copy(
                        values[:, 2 * tp:2 * tp + 2, h::4, 8 * h:8 * h + 8],
                        sm.proj[tp][:, 0:2 * DIM].rearrange("p (t q h d) -> p t q h d", t=2, h=4, d=8)[:, :, :, h, :])
                    last.then_inc(v_in, 1)

            def add(g, t):
                dve.wait_ge(multiplied, TILES * g + t + 1)
                if t == 0:
                    dve.wait_ge(resid, g + 1)
                    if real(g - 1):
                        dve.wait_ge(stored, 16 * g)
                dve.tensor_tensor(xo[:, t, :], sm.y[:, 0:DIM], xr[:, t, :], ALU.add).then_inc(added, 1)

            def body(g, front, tail, ahead):
                if isinstance(g, int) and g == 0:
                    for n in range(len(own.jobs)):
                        own.rest_lo(dve, n)
                    for part in range(4):
                        rest_lo(0, part)
                for s in range(UNITS):
                    if front if s >= 1 else tail:
                        sm.maximum_and_shift(dve, *back(g, s, 1))
                    if s in (4, 5) and tail:
                        add(g - 1, 2 * (s - 4))
                    if front and s < 9 and (s == 0 or s + 1 not in pools):
                        diagonal_keys(dve, g, s + 1 if s else 0)
                    if front if s >= 1 else tail:
                        sm.sum_and_invert(dve, *back(g, s, 1))
                    if s in (6, 7) and ahead:
                        rest_lo(g + 1, 2 * (s - 6))
                        rest_lo(g + 1, 2 * (s - 6) + 1)
                    if s == 3 and front:
                        values_in(g, 0)
                        values_in(g, 1)
                    if s in (4, 5) and tail:
                        add(g - 1, 2 * (s - 4) + 1)
                    splitter.at(g, s, lambda n: splitter.rest_lo(dve, n))

            over_groups(dve, body)

        @block.tensor
        def _(pe):
            def turn(g, part):
                bank = sm.proj[part % 2]
                if part < 2:
                    pe.wait_ge(spread, 2 * g + 2)
                    if real(g - 1):
                        pe.wait_ge(v_in, 8 * g)
                else:
                    pe.wait_ge(c_arrived, 16 * (g + 1))
                    pe.wait_ge(split, 4 * g + part - 1)
                for t in range(TILES):
                    cols = slice((part % 2) * P, (part % 2 + 1) * P)
                    source = xn[:, t, cols] if part < 2 else c_x[:, t, cols]
                    last = pe.transpose(bank[:, t * P:(t + 1) * P], source, identity[:])
                last.then_inc(turned, 1)

            def project_queries(g, c):
                cols = slice(c * P, (c + 1) * P)
                if c == 0:
                    pe.wait_ge(split, 4 * g + 3)
                else:
                    pe.wait_ge(q_in, 2 * g + 1)
                parts = [(q_hi[:, 0, cols], hi[:, 0, :]), (q_lo[:, 0, cols], hi[:, 0, :]),
                         (q_hi[:, 0, cols], lo[:]), (q_rem[:, cols], hi[:, 1, :])]
                for n, (w, moving) in enumerate(parts):
                    last = pe.matmul(sm.proj[0][:], w, moving, start=n == 0, stop=n == len(parts) - 1)
                last.then_inc(q_out, 1)

            def project_keys(g, c):
                cols = slice(c * P, (c + 1) * P)
                if c == 0:
                    pe.wait_ge(split, 4 * g + 4)
                else:
                    pe.wait_ge(k_in, 2 * g + 1)
                parts = [(w[:, k, cols], m[:, k, :]) for w, m in ((k_hi, c_hi), (k_lo, c_hi), (k_hi, c_lo))
                         for k in range(2)]
                for n, (w, moving) in enumerate(parts):
                    last = pe.matmul(sm.proj[1][:], w, moving, start=n == 0, stop=n == len(parts) - 1)
                last.then_inc(k_out, 1)

            def project_values(g):
                for tp in range(2):
                    pe.wait_ge(k_in if tp else q_in, 2 * g + 2)
                    for i in range(2):
                        t = 2 * tp + i
                        for c in range(2):
                            last = pe.matmul(sm.proj[tp][:, i * DIM:(i + 1) * DIM], c_t[:, c, t * P:(t + 1) * P],
                                             wv_sb[:, c, :], start=c == 0, stop=c == 1)
                    last.then_inc(v_out, 1)

            def score(g, u):
                tp, q = divmod(u, quads)
                g2, u2 = back(g, u, 2)
                if u in (0, 4):
                    pe.wait_ge(q_in, 2 * g + (1 if u == 0 else 2))
                pe.wait_ge(masked_g if u in pools else masked_v, masked_before(g, u + 1, u in pools))
                if real(g2):
                    pe.wait_ge(sm.shifted, g2 * UNITS + u2 + 1)
                for i in range(2):
                    for b in range(2):
                        first = (2 * tp + i) * P + b * 64
                        last = pe.matmul(sm.scores[u % 2][b * 64:(b + 1) * 64, i * 256:(i + 1) * 256],
                                         queries[:, q // 4, first:first + 64],
                                         diagonal[u % 2][:, 2 * i + b, :, :], start=True, stop=True)
                last.then_inc(sm.scored, 1)

            def times_values(g, u):
                tp, q = divmod(u, quads)
                pe.wait_ge(sm.copied_a, g * UNITS + u + 1)
                pe.wait_ge(sm.copied_b, g * UNITS + u + 1)
                if u == 0:
                    pe.wait_ge(v_in, 8 * (g + 1))
                if q == 0 and (tp == 1 or real(g - 1)):
                    pe.wait_ge(o_in, 2 * g + tp)
                col = 0 if q < 4 else pair
                for i in range(2):
                    for h in range(4):
                        head = 4 * h + q if q < 4 else 16 + h
                        last = pe.matmul(sm.out[32 * h:32 * h + 32, col + i * P:col + (i + 1) * P],
                                         values[:, 2 * tp + i, head, :], sm.probT[u % 2][:, 4 * i + h, :],
                                         start=q in (0, 4) and i == 0, stop=q >= 3, skip_group_check=True)
                last.then_inc(sm.valued, 1)

            def project_out(g, t):
                pe.wait_ge(o_in, 2 * g + 2)
                if t > 0 or real(g - 1):
                    pe.wait_ge(added, TILES * g + t)
                for c in range(2):
                    last = pe.matmul(sm.y[:, 0:DIM], outs[:, c, t * P:(t + 1) * P], wo_sb[:, c, :],
                                     start=c == 0, stop=c == 1)
                last.then_inc(multiplied, 1)

            def body(g, front, tail, ahead):
                if isinstance(g, int) and g == 0:
                    pe.wait_ge(loads.loaded, loaded)
                    for part in range(4):
                        turn(0, part)
                    pe.wait_ge(loads.split, own.first + len(own.jobs))
                    project_queries(0, 0)
                    project_keys(0, 0)
                for s in range(UNITS):
                    if front if s >= 1 else tail:
                        score(*back(g, s, 1))
                    if s in (4, 5) and tail:
                        project_out(g - 1, 2 * (s - 4))
                    if front if s >= 3 else tail:
                        sm.transpose(pe, identity, *back(g, s, 3))
                    if s in (6, 7) and ahead:
                        turn(g + 1, 2 * (s - 6))
                        turn(g + 1, 2 * (s - 6) + 1)
                    if front if s >= 4 else tail:
                        times_values(*back(g, s, 4))
                    if s in (4, 5) and tail:
                        project_out(g - 1, 2 * (s - 4) + 1)
                    if s == 1 and front:
                        project_queries(g, 1)
                        project_keys(g, 1)
                    if s == 3 and front:
                        project_values(g)
                    if s == 9 and ahead:
                        project_queries(g + 1, 0)
                        project_keys(g + 1, 0)

            over_groups(pe, body)


def build(nc, a, out):
    with ExitStack() as ctx, ExitStack() as self_ctx, ExitStack() as ff_ctx, ExitStack() as cross_ctx:
        identity = ctx.enter_context(nc.sbuf_tensor("identity_sb", [P, P], F32))
        loads = Loads(nc)
        x1, x2, x3 = (nc.dram_tensor(f"x{n}", [TOKENS, DIM], F32).ap() for n in (1, 2, 3))
        self_w = Weights(nc, self_ctx, "self", "right", [(a["a1_wq"], 1), (a["a1_wk"], 1), (a["a1_wv"], 1)])
        with ExitStack() as ip_ctx:
            ip_w = Weights(nc, ip_ctx, "ip", "left", [(a["ip_wq"], 1), (a["ip_wk"], 0)])
            ip_attention(nc, "ip", loads, ip_w, self_w, a["x"], a["ctx"], x1, identity, a["identity"], a["mask"],
                         a["ip_wv"], a["ip_wo"], a["ip_bo"])
        cross_w = Weights(nc, cross_ctx, "cross", "left", [(a["a2_wq"], 1), (a["a2_wk"], 0), (a["a2_wv"], 0)])
        attention(nc, "self", loads, self_w, cross_w, x1, None, x2, identity, a["a1_wo"], a["a1_bo"],
                  a["ln1_g"], a["ln1_b"])
        self_ctx.close()
        ff_w = Weights(nc, ff_ctx, "ff", "right", [(a["ff_w1"], 1)])
        attention(nc, "cross", loads, cross_w, ff_w, x2, a["ctx"], x3, identity, a["a2_wo"], a["a2_bo"],
                  a["ln2_g"], a["ln2_b"])
        cross_ctx.close()
        feed_forward(nc, "ff", loads, ff_w, x3, out, identity, a["ff_b1"], a["ff_w2"], a["ff_b2"],
                     a["ln3_g"], a["ln3_b"])


def layout(inputs):
    def padded(w, rows, cols):
        out = np.zeros((rows, cols), w.dtype)
        out[:w.shape[0], :w.shape[1]] = w
        return out

    def stacked(w):
        return np.concatenate([w[:P]] + [w[P:]] * COPIES)

    get = {k: np.asarray(v) for k, v in inputs.items()}
    a = {"x": get["x"].reshape(TOKENS, DIM), "ctx": get["ctx_2048"].reshape(TOKENS, CTX)}
    a["ip_wq"] = stacked(padded(get["L0_xattn_Wq"].T, DIM, 2 * P))
    a["ip_wk"] = padded(get["L0_xattn_Wk"].T, CTX, 2 * P)
    a["ip_wv"] = get["L0_xattn_Wv"].T
    wo = get["L0_xattn_Wo"].T
    a["ip_wo"] = padded(wo[:P], 2 * P, DIM)
    for h in range(4):
        a["ip_wo"][P + 40 * h:P + 40 * h + 8] = wo[P + 8 * h:P + 8 * h + 8]
    a["ip_bo"] = get["L0_xattn_bo"]
    for n in ("a1_wq", "a1_wk", "a1_wv", "a2_wq", "ff_w1"):
        a[n] = stacked(get["L1_xattn_" + n])
    for n in ("a1_wo", "a1_bo", "a2_wk", "a2_wv", "a2_wo", "a2_bo", "ff_w2", "ff_b2", "ln1_g", "ln1_b", "ln2_g", "ln2_b", "ln3_g", "ln3_b"):
        a[n] = get["L1_xattn_" + n]
    a["ff_b1"] = get["L1_xattn_ff_b1"].reshape(2 * FF_CHUNKS, P).T
    a["identity"] = np.eye(P, dtype=np.float32)
    head = np.stack([4 * np.arange(4) + q for q in range(4)] + [np.arange(4)])
    a["mask"] = (np.arange(P)[:, None, None] // 8 == head).astype(np.float32)
    return {k: np.ascontiguousarray(v) for k, v in a.items()}


def kernel(**inputs):
    import concourse.bacc as bacc
    from concourse.bass_utils import run_bass_kernel_spmd

    nc = bacc.Bacc("TRN2", target_bir_lowering=False, num_devices=1)
    arrays = {f"in_{k}": v for k, v in layout(inputs).items()}
    a = {k[3:]: nc.dram_tensor(k, v.shape, mybir.dt.from_np(v.dtype), kind="ExternalInput").ap()
         for k, v in arrays.items()}
    out = nc.dram_tensor("out", [TOKENS, DIM], F32, kind="ExternalOutput").ap()
    build(nc, a, out)
    got = run_bass_kernel_spmd(nc, [arrays], core_ids=[0])
    return got.results[0]["out"].reshape(SEQS, SEQ, DIM)
```

```python
from contextlib import ExitStack

import numpy as np
from concourse import mybir
import concourse.bass as bass

F32 = mybir.dt.float32
F32R = mybir.dt.float32r
ALU = mybir.AluOpType
ACT = mybir.ActivationFunctionType
AX = mybir.AxisListType

P = 128
SEQS, SEQ, DIM, CTX = 128, 64, 160, 256
TOKENS = SEQS * SEQ
TILES = 4
GROUP = TILES * P
GROUPS = TOKENS // GROUP
REM = DIM - P
COPIES = P // REM
HEADS = 20
INNER = HEADS * 64
UNITS = 10
BLOCKS = 8
EPS = 1e-5
FF = 640
FF_CHUNKS = FF // P
PIECE = 320


def back(g, u, n):
    return (g, u - n) if u >= n else (g - 1, u - n + UNITS)


def real(g):
    return not (isinstance(g, int) and g < 0)


def over_groups(engine, body):
    body(0, True, False, True)
    body(1, True, True, True)
    with engine.Fori(2, GROUPS - 1) as g:
        body(g, True, True, True)
    body(GROUPS - 1, True, True, False)
    body(GROUPS, False, True, False)


class Loads:

    def __init__(self, nc):
        self.staged = [nc.alloc_semaphore(f"w_staged{i}") for i in range(2)]
        self.rounded = nc.alloc_semaphore("w_rounded")
        self.split = nc.alloc_semaphore("w_split")
        self.loaded = nc.alloc_semaphore("w_loaded")
        self.arrivals, self.jobs, self.plain = [0, 0], 0, 0

    def plain_loads(self, sp, tiles):
        for tile, source in tiles:
            sp.dma_start(tile, source).then_inc(self.loaded, 16)


class Weights:

    def __init__(self, nc, ctx, tag, side, matrices):
        self.parts, self.jobs = [], []
        for n, (source, stacked) in enumerate(matrices):
            tiles, cols = source.shape[0] // P, source.shape[1]
            full = tiles - stacked
            hi, lo = (ctx.enter_context(nc.sbuf_tensor(f"{tag}_w{n}_{part}", [P, full, cols], F32R, side=side))
                      for part in ("hi", "lo"))
            rem = ctx.enter_context(nc.sbuf_tensor(f"{tag}_w{n}_rem", [P, cols], F32R, side=side)) if stacked else None
            self.parts.append((hi, lo, rem))
            for k in range(tiles):
                for c in range(0, cols, PIECE):
                    span = slice(c, min(c + PIECE, cols))
                    self.jobs.append((source[k * P:(k + 1) * P, span], hi[:, k, span] if k < full else rem[:, span],
                                      lo[:, k, span] if k < full else None))


class Splitter:

    TIMES = [(0, s) for s in range(4, UNITS)] + [(g, s) for g in (1, GROUPS - 1) for s in range(UNITS)]

    def __init__(self, nc, ctx, tag, loads, jobs):
        self.loads, self.jobs, self.first = loads, jobs, loads.jobs
        self.stage = [ctx.enter_context(nc.sbuf_tensor(f"{tag}_stage{i}", [P, PIECE], F32)) for i in range(2)]
        self.arrived = []
        for n in range(len(jobs)):
            loads.arrivals[n % 2] += 16
            self.arrived.append(loads.arrivals[n % 2])
        loads.jobs += len(jobs)
        assert len(jobs) < len(self.TIMES)

    def load(self, act, n):
        if n < len(self.jobs):
            source, hi, lo = self.jobs[n]
            if n >= 2:
                act.wait_ge(self.loads.split, self.first + n - 1)
            act.dma_start(self.stage[n % 2][:, 0:source.shape[1]], source).then_inc(self.loads.staged[n % 2], 16)

    def round_hi(self, act, n):
        if n == 0:
            self.load(act, 0)
        self.load(act, n + 1)
        source, hi, lo = self.jobs[n]
        act.wait_ge(self.loads.staged[n % 2], self.arrived[n])
        act.activation(hi, self.stage[n % 2][:, 0:source.shape[1]], ACT.Copy).then_inc(self.loads.rounded, 1)

    def rest_lo(self, dve, n):
        source, hi, lo = self.jobs[n]
        stage, w = self.stage[n % 2], source.shape[1]
        dve.wait_ge(self.loads.rounded, self.first + n + 1)
        if lo is None:
            for r in (REM, 3 * REM):
                part = dve.tensor_tensor(hi[r:r + REM, :], stage[r:r + REM, 0:w], hi[r:r + REM, :].bitcast(F32),
                                         ALU.subtract)
        else:
            part = dve.tensor_tensor(lo, stage[:, 0:w], hi.bitcast(F32), ALU.subtract)
        part.then_inc(self.loads.split, 1)

    def at(self, body, step, split, behind=0):
        if isinstance(body, int) and (body, step) in self.TIMES:
            n = self.TIMES.index((body, step)) - behind
            if 0 <= n < len(self.jobs):
                split(n)


def row(v):
    return v.rearrange("(a n) -> a n", a=1).broadcast_to([P, v.shape[0]])


class Softmax:

    def __init__(self, nc, ctx, tag):
        def sem(name):
            return nc.alloc_semaphore(f"{tag}_{name}")

        def sb(name, shape):
            return ctx.enter_context(nc.sbuf_tensor(f"{tag}_{name}", shape, F32))

        def pb(name):
            return ctx.enter_context(nc.psum_tensor(f"{tag}_{name}", [P, 512], F32))

        self.scores = [pb(f"scores{i}") for i in range(2)]
        self.turned = [pb(f"turned{i}") for i in range(2)]
        self.out = pb("out")
        self.y = pb("y")
        self.proj = [pb(f"proj{i}") for i in range(2)]
        self.top = sb("top", [P, 2, BLOCKS])
        self.total = sb("total", [P, 2, BLOCKS])
        self.inverse = sb("inverse", [P, 2, BLOCKS])
        self.own = sb("own", [P, 2])
        self.factor = sb("factor", [P, 2, BLOCKS, 2])
        self.e = [sb(f"e{i}", [P, BLOCKS, 64]) for i in range(2)]
        self.prob = [sb(f"prob{i}", [P, BLOCKS, P]) for i in range(2)]
        self.probT = [sb(f"probT{i}", [P, BLOCKS, P]) for i in range(2)]
        self.scored = sem("scored")
        self.topped = sem("topped")
        self.shifted = sem("shifted")
        self.exped = sem("exped")
        self.summed = sem("summed")
        self.inverted = sem("inverted")
        self.factored = sem("factored")
        self.normed = sem("normed")
        self.transposed = sem("transposed")
        self.copied_a = sem("copied_a")
        self.copied_b = sem("copied_b")
        self.valued = sem("valued")
        self.set = sem("set")

    def constants(self, dve):
        for b in range(2):
            for c in range(2):
                dve.memset(self.own[b * 64:(b + 1) * 64, c:c + 1], float(b == c)).then_inc(self.set, 1)
        dve.wait_ge(self.set, 4)

    def maximum(self, dve, g, u):
        r, s = u % 2, self.scores[u % 2][:].rearrange("p (k j) -> p k j", j=64)
        g2, u2 = back(g, u, 2)
        dve.wait_ge(self.scored, g * UNITS + u + 1)
        if real(g2):
            dve.wait_ge(self.shifted, g2 * UNITS + u2 + 1)
        dve.tensor_reduce(self.top[:, r, :], s, axis=AX.X, op=ALU.max).then_inc(self.topped, 1)

    def shift(self, dve, g, u):
        r, s = u % 2, self.scores[u % 2][:].rearrange("p (k j) -> p k j", j=64)
        g2, u2 = back(g, u, 2)
        dve.wait_ge(self.topped, g * UNITS + u + 1)
        if real(g2):
            dve.wait_ge(self.normed, g2 * UNITS + u2 + 1)
        dve.tensor_tensor(self.e[r][:], s, self.top[:, r, :].unsqueeze(2).broadcast_to([P, BLOCKS, 64]),
                          ALU.subtract).then_inc(self.shifted, 1)

    def add_up(self, dve, g, u):
        dve.wait_ge(self.exped, g * UNITS + u + 1)
        dve.tensor_reduce(self.total[:, u % 2, :], self.e[u % 2][:], axis=AX.X, op=ALU.add).then_inc(self.summed, 1)

    def invert(self, dve, g, u):
        dve.wait_ge(self.summed, g * UNITS + u + 1)
        dve.reciprocal(self.inverse[:, u % 2, :], self.total[:, u % 2, :]).then_inc(self.inverted, 1)

    def make_factor(self, dve, g, u):
        r = u % 2
        g2, u2 = back(g, u, 2)
        dve.wait_ge(self.inverted, g * UNITS + u + 1)
        if real(g2):
            dve.wait_ge(self.normed, g2 * UNITS + u2 + 1)
        dve.tensor_tensor(self.factor[:, r, :, :], self.inverse[:, r, :].unsqueeze(2).broadcast_to([P, BLOCKS, 2]),
                          self.own[:].unsqueeze(1).broadcast_to([P, BLOCKS, 2]), ALU.mult).then_inc(self.factored, 1)

    def copy_b(self, dve, g, u):
        g2, u2 = back(g, u, 2)
        dve.wait_ge(self.transposed, 2 * (g * UNITS + u) + 2)
        if real(g2):
            dve.wait_ge(self.valued, g2 * UNITS + u2 + 1)
        dve.tensor_copy(self.probT[u % 2][:, 4:8, :], self.turned[1][:].rearrange("p (k i) -> p k i", i=P))\
           .then_inc(self.copied_b, 1)

    def exponential(self, act, g, u, scale):
        act.wait_ge(self.shifted, g * UNITS + u + 1)
        act.activation(self.e[u % 2][:], self.e[u % 2][:], ACT.Exp, scale=scale).then_inc(self.exped, 1)

    def copy_a(self, act, g, u):
        g2, u2 = back(g, u, 2)
        act.wait_ge(self.transposed, 2 * (g * UNITS + u) + 1)
        if real(g2):
            act.wait_ge(self.valued, g2 * UNITS + u2 + 1)
        act.activation(self.probT[u % 2][:, 0:4, :], self.turned[0][:].rearrange("p (k i) -> p k i", i=P),
                       ACT.Copy).then_inc(self.copied_a, 1)

    def copy_both(self, act, g, u):
        self.copy_a(act, g, u)
        act.wait_ge(self.transposed, 2 * (g * UNITS + u) + 2)
        act.activation(self.probT[u % 2][:, 4:8, :], self.turned[1][:].rearrange("p (k i) -> p k i", i=P),
                       ACT.Copy).then_inc(self.copied_b, 1)

    def normalise(self, pool, g, u):
        r = u % 2
        g2, u2 = back(g, u, 2)
        pool.wait_ge(self.factored, g * UNITS + u + 1)
        if real(g2):
            pool.wait_ge(self.transposed, 2 * (g2 * UNITS + u2 + 1))
        pool.tensor_tensor(self.prob[r][:].rearrange("p k (b j) -> p k b j", b=2),
                           self.e[r][:].unsqueeze(2).broadcast_to([P, BLOCKS, 2, 64]),
                           self.factor[:, r, :, :].unsqueeze(3).broadcast_to([P, BLOCKS, 2, 64]),
                           ALU.mult).then_inc(self.normed, 1)

    def transpose(self, pe, identity, g, u):
        pe.wait_ge(self.normed, g * UNITS + u + 1)
        g1, u1 = back(g, u, 1)
        for half, copied in enumerate((self.copied_a, self.copied_b)):
            if real(g1):
                pe.wait_ge(copied, g1 * UNITS + u1 + 1)
            for k in range(4):
                last = pe.transpose(self.turned[half][:, k * P:(k + 1) * P],
                                    self.prob[u % 2][:, 4 * half + k, :], identity[:])
            last.then_inc(self.transposed, 1)


class Norm:

    def __init__(self, nc, ctx, tag):
        def sem(name):
            return nc.alloc_semaphore(f"{tag}_{name}")

        def sb(name, shape, dt=F32):
            return ctx.enter_context(nc.sbuf_tensor(f"{tag}_{name}", shape, dt))

        self.x = sb("x", [P, TILES, DIM])
        self.xr = sb("xr", [P, TILES, DIM])
        self.xo = sb("xo", [P, TILES, DIM])
        self.hat = sb("hat", [P, TILES, DIM])
        self.n = sb("n", [P, TILES, 2 * P])
        self.stats = sb("stats", [P, TILES, 6])
        self.mv = sb("mv", [P, TILES, 2])
        self.rstd = sb("rstd", [P, TILES])
        self.power = sb("power", [P, TILES])
        self.eps = sb("eps", [P, TILES])
        self.ahead = sb("ahead", [P, 1])
        self.gains = [sb(f"gain{i}", [P, DIM]) for i in range(2)]
        self.shifts = [sb(f"shift{i}", [P, DIM]) for i in range(2)]
        self.bias = sb("bias", [P, DIM])
        self.phase, self.normed, self.done = 0, -GROUPS, 0
        self.hi = sb("hi", [P, 2, GROUP], F32R)
        self.lo = sb("lo", [P, GROUP], F32R)
        self.arrived = sem("arrived")
        self.again = sem("again")
        self.stored = sem("stored")
        self.set = sem("set")
        self.stat = sem("stat")
        self.var = sem("var")
        self.veps = sem("veps")
        self.root = sem("root")
        self.hatted = sem("hatted")
        self.gained = sem("gained")
        self.ready = sem("ready")
        self.turned = sem("turned")
        self.rounded = sem("rounded")
        self.split = sem("split")
        self.resid = sem("resid")
        self.multiplied = sem("multiplied")
        self.added = sem("added")

    def constants(self, pool):
        pool.memset(self.power[:], -0.5).then_inc(self.set, 1)
        pool.memset(self.eps[:], EPS).then_inc(self.set, 1)
        pool.wait_ge(self.set, 2)

    def next_phase(self):
        self.phase, self.normed, self.done = self.phase + 1, self.normed + GROUPS, self.done + GROUPS

    def vectors(self, phase, gain, shift):
        return [(self.gains[phase % 2][:], row(gain)), (self.shifts[phase % 2][:], row(shift))]

    def load(self, sp, x_in, g, n):
        g = g + self.normed
        sp.wait_ge(self.stored, 16 * (g + 1))
        if real(g - 1):
            sp.wait_ge(self.hatted, TILES * g)
        sp.dma_start(self.x[:], x_in[n]).then_inc(self.arrived, 16)

    def load_again(self, sp, x_in, g):
        if self.normed >= 0:
            sp.wait_ge(self.stored, 16 * (g + self.normed + 1))
        if real(g + self.done - 1):
            sp.wait_ge(self.added, TILES * (g + self.done))
        sp.dma_start(self.xr[:], x_in[g]).then_inc(self.again, 16)

    def store(self, sp, x_out, g):
        sp.wait_ge(self.added, TILES * (g + self.done + 1))
        sp.dma_start(x_out[g], self.xo[:]).then_inc(self.stored, 16)

    def statistics(self, dve, g, t):
        g = g + self.normed
        if t == 0:
            dve.wait_ge(self.arrived, 16 * (g + 1))
            if real(g - 1):
                dve.wait_ge(self.hatted, TILES * g)
                dve.wait_ge(self.veps, g)
        dve.bn_stats(self.stats[:, t, :], self.x[:, t, :]).then_inc(self.stat, 1)
        dve.wait_ge(self.stat, TILES * g + t + 1)
        dve.memset(self.ahead[:], 0.0)
        dve.bn_aggr(self.mv[:, t, :], self.stats[:, t, :]).then_inc(self.var, 1)

    def inverse_root(self, pool, g):
        g = g + self.normed
        pool.wait_ge(self.var, TILES * (g + 1))
        if real(g - 1):
            pool.wait_ge(self.hatted, TILES * g)
        pool.tensor_tensor(self.rstd[:], self.mv[:, :, 1], self.eps[:], ALU.add).then_inc(self.veps, 1)
        pool.wait_ge(self.veps, g + 1)
        pool.tensor_tensor(self.rstd[:], self.rstd[:], self.power[:], ALU.pow).then_inc(self.root, 1)

    def normalise(self, dve, g, t):
        g = g + self.normed
        if t == 0:
            dve.wait_ge(self.root, g + 1)
            dve.wait_ge(self.var, TILES * (g + 1))
            if real(g - 1):
                dve.wait_ge(self.ready, 2 * g)
        dve.tensor_scalar(self.hat[:, t, :], self.x[:, t, :], self.mv[:, t, 0:1], self.rstd[:, t:t + 1],
                          ALU.subtract, ALU.mult).then_inc(self.hatted, 1)

    def affine(self, pool, g):
        which = (self.phase + (isinstance(g, int) and g == GROUPS)) % 2
        gain, shift = self.gains[which], self.shifts[which]
        g = g + self.normed
        pool.wait_ge(self.hatted, TILES * (g + 1))
        pool.tensor_tensor(self.hat[:], self.hat[:], gain[:].unsqueeze(1).broadcast_to([P, TILES, DIM]),
                           ALU.mult).then_inc(self.gained, 1)
        pool.wait_ge(self.gained, g + 1)
        if real(g - 1):
            pool.wait_ge(self.turned, 2 * g)
        pool.tensor_tensor(self.n[:, :, 0:P], self.hat[:, :, 0:P],
                           shift[:, 0:P].unsqueeze(1).broadcast_to([P, TILES, P]), ALU.add)\
            .then_inc(self.ready, 1)
        pool.tensor_tensor(self.n[:, :, P:2 * P].rearrange("p t (c r) -> p t c r", c=COPIES),
                           self.hat[:, :, P:DIM].unsqueeze(2).broadcast_to([P, TILES, COPIES, REM]),
                           shift[:, P:DIM].unsqueeze(1).unsqueeze(1).broadcast_to([P, TILES, COPIES, REM]),
                           ALU.add).then_inc(self.ready, 1)

    def transpose(self, pe, identity, banks, g, part):
        g = g + self.normed
        pe.wait_ge(self.ready, 2 * g + 2)
        for t in range(TILES):
            last = pe.transpose(banks[part][:, t * P:(t + 1) * P], self.n[:, t, part * P:(part + 1) * P], identity[:])
        last.then_inc(self.turned, 1)

    def round_hi(self, act, banks, g, part):
        g = g + self.normed
        act.wait_ge(self.turned, 2 * g + part + 1)
        act.activation(self.hi[:, part, :], banks[part][:], ACT.Copy).then_inc(self.rounded, 1)

    def rest_lo(self, dve, banks, g, part):
        g = g + self.normed
        dve.wait_ge(self.rounded, 2 * g + part + 1)
        if part == 0:
            dve.tensor_tensor(self.lo[:], banks[0][:], self.hi[:, 0, :].bitcast(F32), ALU.subtract)\
               .then_inc(self.split, 1)
        else:
            dve.tensor_tensor(self.hi[64:P, 1, :], banks[1][64:P, :], self.hi[64:P, 1, :].bitcast(F32),
                              ALU.subtract).then_inc(self.split, 1)

    def residual(self, pool, g):
        g = g + self.done
        pool.wait_ge(self.again, 16 * (g + 1))
        pool.tensor_tensor(self.xr[:], self.xr[:], self.bias[:].unsqueeze(1).broadcast_to([P, TILES, DIM]),
                           ALU.add).then_inc(self.resid, 1)

    def add(self, dve, bank, g, t):
        g = g + self.done
        dve.wait_ge(self.multiplied, TILES * g + t + 1)
        if t == 0:
            dve.wait_ge(self.resid, g + 1)
            if real(g - 1):
                dve.wait_ge(self.stored, 16 * g)
        dve.tensor_tensor(self.xo[:, t, :], bank[:, 0:DIM], self.xr[:, t, :], ALU.add).then_inc(self.added, 1)


def attention(nc, tag, loads, ln, weights, following, x_dram, ctx_dram, out_dram, identity, wo, bo, early):
    cross = ctx_dram is not None
    x_in = x_dram.rearrange("(g t p) c -> g p t c", t=TILES, p=P)
    x_out = out_dram.rearrange("(g t p) c -> g p t c", t=TILES, p=P)
    ln.next_phase()
    with ExitStack() as ctx:
        def sem(name):
            return nc.alloc_semaphore(f"{tag}_{name}")

        def sb(name, shape, dt=F32):
            return ctx.enter_context(nc.sbuf_tensor(f"{tag}_{name}", shape, dt))

        (q_hi, q_lo, q_rem), (k_hi, k_lo, k_rem), (v_hi, v_lo, v_rem) = weights.parts
        wo_sb = sb("wo", [P, UNITS, DIM])
        plain = early + [(ln.bias[:], row(bo)), (wo_sb[:], wo.rearrange("(u p) c -> p u c", p=P))]
        loads.plain += 16 * len(plain)
        loaded = loads.plain
        splitter = Splitter(nc, ctx, tag, loads, following.jobs)

        sm = Softmax(nc, ctx, tag + "_sm")
        queries = [sb(f"queries{i}", [P, GROUP]) for i in range(2)]
        keys = [sb(f"keys{i}", [P, BLOCKS, P]) for i in range(2)]
        values = sb("values", [P, TILES, INNER])
        outs = sb("outs", [P, UNITS, GROUP])
        q_out = sem("q_out")
        k_out = sem("k_out")
        v_out = sem("v_out")
        q_in = sem("q_in")
        k_in_a = sem("k_in_a")
        k_in_b = sem("k_in_b")
        v_in = sem("v_in")
        o_in = sem("o_in")
        zeros = sem("zeros")
        if cross:
            c_x = sb("c_x", [P, TILES, CTX])
            c_hi, c_lo = sb("c_hi", [P, 2, GROUP], F32R), sb("c_lo", [P, 2, GROUP], F32R)
            ctx_in = ctx_dram.rearrange("(g t p) c -> g p t c", t=TILES, p=P)
            c_arrived = sem("c_arrived")
            c_turned = sem("c_turned")
            c_rounded = sem("c_rounded")
            c_split = sem("c_split")
            c_bank = [sm.y, sm.proj[1]]

        v_slots = [[(t, 0, 512)] for t in range(TILES)] + [[(t, 512, 512)] for t in range(TILES)] \
            + [[(t, 1024, 256), (t + 1, 1024, 256)] for t in (0, 2)]
        v_last_user = [3] * 4 + [7] * 4 + [9] * 2

        block = ctx.enter_context(nc.Block())

        @block.sync
        def _(sp):
            def load_ctx(g):
                if real(g - 1):
                    sp.wait_ge(c_turned, 2 * g)
                sp.dma_start(c_x[:], ctx_in[g]).then_inc(c_arrived, 16)

            def body(g, front, tail, ahead):
                if isinstance(g, int) and g == 0:
                    if cross:
                        load_ctx(0)
                    loads.plain_loads(sp, plain)
                if ahead:
                    ln.load(sp, x_in, g + 1, g + 1)
                    if cross:
                        load_ctx(g + 1)
                if isinstance(g, int) and g == GROUPS - 1:
                    ln.load(sp, x_out, GROUPS, 0)
                if tail:
                    ln.store(sp, x_out, g - 1)
                if front:
                    ln.load_again(sp, x_in, g)

            over_groups(sp, body)

        @block.gpsimd
        def _(pool):
            pool.wait_ge(loads.loaded, loaded)
            for i in range(2):
                pool.memset(keys[i][:], 0.0).then_inc(zeros, 1)

            def body(g, front, tail, ahead):
                for s in range(UNITS):
                    u1 = s - 1
                    if u1 < 0 and tail:
                        sm.normalise(pool, g - 1, UNITS - 1)
                    elif u1 >= 0 and front:
                        sm.normalise(pool, g, u1)
                    if s == 2 and tail:
                        ln.residual(pool, g - 1)
                    if s == 6 and front:
                        ln.inverse_root(pool, g + 1)
                    if s == 8 and front:
                        ln.affine(pool, g + 1)

            over_groups(pool, body)

        @block.scalar
        def _(act):
            def queries_in(g, s):
                g2, u2 = back(g, s, 2)
                act.wait_ge(q_out, g * UNITS + s + 1)
                if real(g2):
                    act.wait_ge(sm.scored, g2 * UNITS + u2 + 1)
                act.activation(queries[s % 2][:], sm.proj[s % 2][:], ACT.Copy).then_inc(q_in, 1)

            def context_hi(g, c):
                act.wait_ge(c_turned, 2 * g + c + 1)
                act.activation(c_hi[:, c, :], c_bank[c][:], ACT.Copy).then_inc(c_rounded, 1)

            def output(g, u):
                act.wait_ge(sm.valued, g * UNITS + u + 1)
                act.activation(outs[:, u, :], sm.out[:], ACT.Copy).then_inc(o_in, 1)

            def body(g, front, tail, ahead):
                for s in range(UNITS):
                    if s == 0 and front:
                        for part in range(2):
                            ln.round_hi(act, sm.proj, g, part)
                        if cross:
                            context_hi(g, 0)
                    elif front:
                        queries_in(g, s)
                    if s < 4 and tail:
                        output(*back(g, s, 4))
                    if s > 4 and front:
                        output(*back(g, s, 4))
                    if front if s >= 1 else tail:
                        sm.exponential(act, *back(g, s, 1), 64 ** -0.5)
                    if s == 0:
                        if tail and not cross:
                            sm.copy_a(act, *back(g, s, 3))
                        if front and cross:
                            context_hi(g, 1)
                        if front:
                            queries_in(g, s)
                        if tail and cross:
                            sm.copy_a(act, *back(g, s, 3))
                    if front:
                        act.wait_ge(k_out, g * UNITS + s + 1)
                        if isinstance(g, int) and g == 0 and s == 0:
                            act.wait_ge(zeros, 2)
                        act.activation(keys[s % 2][0:64, :, 0:64],
                                       sm.proj[(s + 1) % 2][0:64, :].rearrange("p (b j) -> p b j", j=64),
                                       ACT.Copy).then_inc(k_in_a, 1)
                    if s > 0 and (front if s >= 3 else tail):
                        sm.copy_a(act, *back(g, s, 3))
                    if front:
                        act.wait_ge(v_out, g * UNITS + s + 1)
                        if real(g - 1):
                            act.wait_ge(sm.valued, (g - 1) * UNITS + v_last_user[s] + 1)
                        pieces = v_slots[s]
                        t0, c0, n = pieces[0]
                        act.activation(values[:, t0:t0 + len(pieces), c0:c0 + n],
                                       sm.proj[s % 2][:].rearrange("p (t c) -> p t c", c=n),
                                       ACT.Copy).then_inc(v_in, 1)
                    if s == 4 and front:
                        output(g, 0)
                    splitter.at(g, s, lambda n: splitter.round_hi(act, n))

            over_groups(act, body)

        @block.vector
        def _(dve):
            sm.constants(dve)

            def body(g, front, tail, ahead):
                for s in range(UNITS):
                    splitter.at(g, s, lambda n: splitter.rest_lo(dve, n), behind=1)
                    if s == 4 and tail:
                        ln.add(dve, sm.y, g - 1, 0)
                    if front if s >= 1 else tail:
                        sm.maximum(dve, *back(g, s, 1))
                        sm.shift(dve, *back(g, s, 1))
                    if s == 0 and front:
                        for part in range(2):
                            ln.rest_lo(dve, sm.proj, g, part)
                    if s == 0 and tail and not cross:
                        sm.copy_b(dve, *back(g, s, 3))
                    if s == 0 and front and cross:
                        for c in range(2):
                            dve.wait_ge(c_rounded, 2 * g + c + 1)
                            dve.tensor_tensor(c_lo[:, c, :], c_bank[c][:], c_hi[:, c, :].bitcast(F32),
                                              ALU.subtract).then_inc(c_split, 1)
                    if s == 0 and tail and cross:
                        sm.copy_b(dve, *back(g, s, 3))
                    if front:
                        g2, u2 = back(g, s, 2)
                        dve.wait_ge(k_out, g * UNITS + s + 1)
                        if real(g2):
                            dve.wait_ge(sm.scored, g2 * UNITS + u2 + 1)
                        if isinstance(g, int) and g == 0 and s == 0:
                            dve.wait_ge(zeros, 2)
                        dve.tensor_copy(keys[s % 2][64:P, :, 64:P],
                                        sm.proj[(s + 1) % 2][64:P, :].rearrange("p (b j) -> p b j", j=64))\
                           .then_inc(k_in_b, 1)
                    if s == 4 and tail:
                        ln.add(dve, sm.y, g - 1, 1)
                        ln.add(dve, sm.y, g - 1, 2)
                    if front if s >= 1 else tail:
                        sm.add_up(dve, *back(g, s, 1))
                        sm.invert(dve, *back(g, s, 1))
                        sm.make_factor(dve, *back(g, s, 1))
                    if s > 0 and (front if s >= 3 else tail):
                        sm.copy_b(dve, *back(g, s, 3))
                    if s == 4 and tail:
                        ln.add(dve, sm.y, g - 1, 3)
                    if front and s in (5, 6):
                        for t in (2 * (s - 5), 2 * (s - 5) + 1):
                            ln.statistics(dve, g + 1, t)
                    if front and s in (7, 8):
                        for t in (2 * (s - 7), 2 * (s - 7) + 1):
                            ln.normalise(dve, g + 1, t)

            over_groups(dve, body)

        @block.tensor
        def _(pe):
            def project_queries(g, u):
                cols, bank = slice(u * P, (u + 1) * P), sm.proj[u % 2]
                if u == 0:
                    pe.wait_ge(ln.split, 2 * (g + ln.normed) + 2)
                else:
                    pe.wait_ge(k_in_a, g * UNITS + u)
                    pe.wait_ge(k_in_b, g * UNITS + u)
                parts = [(q_hi[:, 0, cols], ln.hi[:, 0, :]), (q_lo[:, 0, cols], ln.hi[:, 0, :]),
                         (q_hi[:, 0, cols], ln.lo[:]), (q_rem[:, cols], ln.hi[:, 1, :])]
                for n, (w, moving) in enumerate(parts):
                    last = pe.matmul(bank[:], w, moving, start=n == 0, stop=n == len(parts) - 1)
                last.then_inc(q_out, 1)

            def project_keys(g, u):
                cols, bank = slice(u * P, (u + 1) * P), sm.proj[(u + 1) % 2]
                if u == 0:
                    if cross:
                        pe.wait_ge(c_split, 2 * g + 2)
                else:
                    pe.wait_ge(v_in, g * UNITS + u)
                if cross:
                    parts = [(k_hi[:, c, cols], c_hi[:, c, :]) for c in range(2)] \
                        + [(k_lo[:, c, cols], c_hi[:, c, :]) for c in range(2)] \
                        + [(k_hi[:, c, cols], c_lo[:, c, :]) for c in range(2)]
                else:
                    parts = [(k_hi[:, 0, cols], ln.hi[:, 0, :]), (k_lo[:, 0, cols], ln.hi[:, 0, :]),
                             (k_hi[:, 0, cols], ln.lo[:]), (k_rem[:, cols], ln.hi[:, 1, :])]
                for n, (w, moving) in enumerate(parts):
                    last = pe.matmul(bank[:], w, moving, start=n == 0, stop=n == len(parts) - 1)
                last.then_inc(k_out, 1)

            def project_values(g, s):
                pe.wait_ge(q_in, g * UNITS + s + 1)
                for i, (t, c0, n) in enumerate(v_slots[s]):
                    tok, cols = slice(t * P, (t + 1) * P), slice(c0, c0 + n)
                    if cross:
                        parts = [(c_hi[:, c, tok], v_hi[:, c, cols]) for c in range(2)] \
                            + [(c_lo[:, c, tok], v_hi[:, c, cols]) for c in range(2)] \
                            + [(c_hi[:, c, tok], v_lo[:, c, cols]) for c in range(2)]
                    else:
                        parts = [(ln.hi[:, 0, tok], v_hi[:, 0, cols]), (ln.lo[:, tok], v_hi[:, 0, cols]),
                                 (ln.hi[:, 0, tok], v_lo[:, 0, cols]), (ln.hi[:, 1, tok], v_rem[:, cols])]
                    for k, (w, moving) in enumerate(parts):
                        last = pe.matmul(sm.proj[s % 2][:, i * n:(i + 1) * n], w, moving,
                                         start=k == 0, stop=k == len(parts) - 1)
                last.then_inc(v_out, 1)

            def score(g, u):
                g2, u2 = back(g, u, 2)
                pe.wait_ge(q_in, g * UNITS + u + 1)
                pe.wait_ge(k_in_a, g * UNITS + u + 1)
                pe.wait_ge(k_in_b, g * UNITS + u + 1)
                if real(g2):
                    pe.wait_ge(sm.shifted, g2 * UNITS + u2 + 1)
                for t in range(TILES):
                    for b in range(2):
                        seq = 2 * t + b
                        last = pe.matmul(sm.scores[u % 2][b * 64:(b + 1) * 64, t * P:(t + 1) * P],
                                         queries[u % 2][:, seq * 64:(seq + 1) * 64], keys[u % 2][:, seq, :],
                                         start=True, stop=True)
                last.then_inc(sm.scored, 1)

            def times_values(g, u):
                g1, u1 = back(g, u, 1)
                pe.wait_ge(sm.copied_a, g * UNITS + u + 1)
                pe.wait_ge(sm.copied_b, g * UNITS + u + 1)
                pe.wait_ge(v_in, g * UNITS + (4 if u < 4 else 8 if u < 8 else 10))
                if real(g1):
                    pe.wait_ge(o_in, g1 * UNITS + u1 + 1)
                for t in range(TILES):
                    for h in range(2):
                        head = 2 * u + h
                        last = pe.matmul(sm.out[h * 64:(h + 1) * 64, t * P:(t + 1) * P],
                                         values[:, t, head * 64:(head + 1) * 64], sm.probT[u % 2][:, 2 * t + h, :],
                                         start=True, stop=True)
                last.then_inc(sm.valued, 1)

            def project_out(g, t):
                pe.wait_ge(o_in, g * UNITS + UNITS)
                pe.wait_ge(ln.added, TILES * (g + ln.done) + t)
                for u in range(UNITS):
                    last = pe.matmul(sm.y[:, 0:DIM], outs[:, u, t * P:(t + 1) * P], wo_sb[:, u, :],
                                     start=u == 0, stop=u == UNITS - 1)
                last.then_inc(ln.multiplied, 1)

            def turn(g, part):
                if real(g - 1):
                    if part == 0:
                        pe.wait_ge(k_in_a, g * UNITS)
                        pe.wait_ge(k_in_b, g * UNITS)
                    else:
                        pe.wait_ge(v_in, g * UNITS)
                ln.transpose(pe, identity, sm.proj, g, part)

            def turn_context(g, c):
                pe.wait_ge(c_arrived, 16 * (g + 1))
                if c == 1:
                    pe.wait_ge(ln.split, 2 * (g + ln.normed) + 2)
                else:
                    pe.wait_ge(ln.added, TILES * (g + ln.done - 1))
                for t in range(TILES):
                    last = pe.transpose(c_bank[c][:, t * P:(t + 1) * P], c_x[:, t, c * P:(c + 1) * P], identity[:])
                last.then_inc(c_turned, 1)

            def body(g, front, tail, ahead):
                for s in range(UNITS):
                    if s > 0 and front:
                        project_queries(g, s)
                    if s == 4 and isinstance(g, int) and g == 1:
                        pe.wait_ge(loads.loaded, loaded)
                    if s == 4 and tail:
                        project_out(g - 1, 0)
                    if front if s >= 1 else tail:
                        score(*back(g, s, 1))
                    if s == 0 and front:
                        for part in range(2):
                            turn(g, part)
                        if cross:
                            turn_context(g, 0)
                    if s < 4 and tail:
                        times_values(*back(g, s, 4))
                    if s > 4 and front:
                        times_values(*back(g, s, 4))
                    if s == 0:
                        if tail and not cross:
                            sm.transpose(pe, identity, *back(g, s, 3))
                        if front and cross:
                            turn_context(g, 1)
                        if front:
                            project_queries(g, s)
                        if tail and cross:
                            sm.transpose(pe, identity, *back(g, s, 3))
                    if front:
                        project_keys(g, s)
                    if s == 4 and tail:
                        project_out(g - 1, 1)
                    if s > 0 and (front if s >= 3 else tail):
                        sm.transpose(pe, identity, *back(g, s, 3))
                    if s == 4 and tail:
                        project_out(g - 1, 2)
                    if front:
                        project_values(g, s)
                    if s == 4 and tail:
                        project_out(g - 1, 3)
                    if s == 4 and front:
                        times_values(g, 0)

            over_groups(pe, body)


def feed_forward(nc, tag, loads, ln, weights, x_dram, out_dram, identity, b1_sb, w2_sb, b2):
    x_in = x_dram.rearrange("(g t p) c -> g p t c", t=TILES, p=P)
    x_out = out_dram.rearrange("(g t p) c -> g p t c", t=TILES, p=P)
    ln.next_phase()
    with ExitStack() as ctx:
        def sem(name):
            return nc.alloc_semaphore(f"{tag}_{name}")

        def sb(name, shape, dt=F32):
            return ctx.enter_context(nc.sbuf_tensor(f"{tag}_{name}", shape, dt))

        def pb(name):
            return ctx.enter_context(nc.psum_tensor(f"{tag}_{name}", [P, 512], F32))

        w_hi, w_lo, w_rem = weights.parts[0]
        plain = [(ln.bias[:], row(b2))]
        loads.plain += 16 * len(plain)
        loaded = loads.plain

        gate = [sb(f"gate{i}", [P, GROUP]) for i in range(2)]
        hidden = sb("hidden", [P, FF_CHUNKS, GROUP])
        banks = [pb(f"turn{i}") for i in range(2)]
        psa, psg = [pb(f"a{i}") for i in range(2)], [pb(f"gate_p{i}") for i in range(2)]
        psy = [pb(f"y{i}") for i in range(2)]
        a_out = sem("a_out")
        g_out = sem("g_out")
        gelued = sem("gelued")
        gated = sem("gated")

        block = ctx.enter_context(nc.Block())

        @block.sync
        def _(sp):
            def body(g, front, tail, ahead):
                if isinstance(g, int) and g == 0:
                    loads.plain_loads(sp, plain)
                if ahead:
                    ln.load(sp, x_in, g + 1, g + 1)
                if tail:
                    ln.store(sp, x_out, g - 1)
                if front:
                    ln.load_again(sp, x_in, g)

            over_groups(sp, body)
            sp.wait_ge(ln.stored, 16 * (GROUPS + ln.done))

        @block.gpsimd
        def _(pool):
            pool.wait_ge(loads.loaded, loaded)

            def body(g, front, tail, ahead):
                if ahead:
                    ln.inverse_root(pool, g + 1)
                if ahead:
                    ln.affine(pool, g + 1)
                if front:
                    ln.residual(pool, g)

            over_groups(pool, body)

        def chunk_back(g, j, n):
            return (g, j - n) if j >= n else (g - 1, j - n + FF_CHUNKS)

        @block.scalar
        def _(act):
            def body(g, front, tail, ahead):
                if front:
                    for part in range(2):
                        ln.round_hi(act, banks, g, part)
                    for j in range(FF_CHUNKS):
                        g2, j2 = chunk_back(g, j, 2) if j >= 2 else (g - 1, FF_CHUNKS - 1)
                        act.wait_ge(g_out, g * FF_CHUNKS + j + 1)
                        if real(g2):
                            act.wait_ge(gated, g2 * FF_CHUNKS + j2 + 1)
                        act.activation(gate[j % 2][:], psg[j % 2][:], ACT.Gelu,
                                       bias=b1_sb[:, FF_CHUNKS + j:FF_CHUNKS + j + 1]).then_inc(gelued, 1)

            over_groups(act, body)

        @block.vector
        def _(dve):
            def body(g, front, tail, ahead):
                if front:
                    for part in range(2):
                        ln.rest_lo(dve, banks, g, part)
                for t in range(2):
                    if ahead:
                        ln.statistics(dve, g + 1, t)
                for t in range(TILES):
                    if tail:
                        ln.add(dve, psy[t % 2], g - 1, t)
                    if ahead and t < 2:
                        ln.statistics(dve, g + 1, t + 2)
                for j in range(FF_CHUNKS):
                    if front:
                        dve.wait_ge(gelued, g * FF_CHUNKS + j + 1)
                        dve.wait_ge(a_out, g * FF_CHUNKS + j + 1)
                        dve.scalar_tensor_tensor(hidden[:, j, :], psa[j % 2][:], b1_sb[:, j:j + 1], gate[j % 2][:],
                                                 ALU.add, ALU.mult).then_inc(gated, 1)
                    if ahead and j == 0:
                        for t in range(TILES):
                            ln.normalise(dve, g + 1, t)

            over_groups(dve, body)

        @block.tensor
        def _(pe):
            def body(g, front, tail, ahead):
                if front:
                    if real(g - 1):
                        pe.wait_ge(ln.split, 2 * (g + ln.normed))
                    for part in range(2):
                        ln.transpose(pe, identity, banks, g, part)
                if tail:
                    pe.wait_ge(gated, g * FF_CHUNKS)
                    for t in range(TILES):
                        pe.wait_ge(ln.added, TILES * (g - 1 + ln.done) + max(t - 1, 0))
                        for j in range(FF_CHUNKS):
                            last = pe.matmul(psy[t % 2][:, 0:DIM], hidden[:, j, t * P:(t + 1) * P], w2_sb[:, j, :],
                                             start=j == 0, stop=j == FF_CHUNKS - 1)
                        last.then_inc(ln.multiplied, 1)
                if front:
                    pe.wait_ge(ln.split, 2 * (g + ln.normed) + 2)
                    for j in range(FF_CHUNKS):
                        g2, j2 = (g, j - 2) if j >= 2 else (g - 1, FF_CHUNKS - 1)
                        for bank, c, done in ((psg[j % 2], FF_CHUNKS + j, g_out), (psa[j % 2], j, a_out)):
                            if real(g2):
                                pe.wait_ge(gated, g2 * FF_CHUNKS + j2 + 1)
                            cols = slice(c * P, (c + 1) * P)
                            parts = [(w_hi[:, 0, cols], ln.hi[:, 0, :]), (w_lo[:, 0, cols], ln.hi[:, 0, :]),
                                     (w_hi[:, 0, cols], ln.lo[:]), (w_rem[:, cols], ln.hi[:, 1, :])]
                            for n, (w, moving) in enumerate(parts):
                                last = pe.matmul(bank[:], w, moving, start=n == 0, stop=n == len(parts) - 1)
                            last.then_inc(done, 1)

            over_groups(pe, body)


def ip_attention(nc, tag, loads, ln, weights, following, x_dram, ctx_dram, out_dram, identity, eye, mask, wv, wo, bo,
                 early):
    quads, pair = 5, 2 * P
    pools = (3,)
    out_steps = (5, 6, 7, 9)

    def pair_and_quad(u):
        return divmod(u, 4) if u < 8 else (u - 8, 4)

    def masked_before(g, u, by_pool):
        mine = [v for v in range(UNITS) if (v in pools) == by_pool]
        return g * len(mine) + sum(v < u for v in mine)

    x_in = x_dram.rearrange("(g t p) c -> g p t c", t=TILES, p=P)
    ctx_in = ctx_dram.rearrange("(g t p) c -> g p t c", t=TILES, p=P)
    x_out = out_dram.rearrange("(g t p) c -> g p t c", t=TILES, p=P)
    with ExitStack() as ctx:
        def sem(name):
            return nc.alloc_semaphore(f"{tag}_{name}")

        def sb(name, shape, dt=F32):
            return ctx.enter_context(nc.sbuf_tensor(f"{tag}_{name}", shape, dt))

        (q_hi, q_lo, q_rem), (k_hi, k_lo, _) = weights.parts
        wv_sb = sb("wv", [P, 2, DIM])
        wo_sb = sb("wo", [P, 2, DIM])
        mask_sb = sb("mask", [P, quads, 4])
        plain = [(identity[:], eye), (mask_sb[:], mask), (ln.bias[:], row(bo)),
                 (wv_sb[:], wv.rearrange("(c p) n -> p c n", p=P)), (wo_sb[:], wo.rearrange("(c p) n -> p c n", p=P))] + early
        loads.plain += 16 * len(plain)
        loaded = loads.plain
        own = Splitter(nc, ctx, tag + "_own", loads, weights.jobs)
        splitter = Splitter(nc, ctx, tag, loads, following.jobs)

        sm = Softmax(nc, ctx, tag + "_sm")
        x = sb("x", [P, TILES, DIM])
        xn = sb("xn", [P, TILES, 2 * P])
        hi, lo = sb("hi", [P, 2, GROUP], F32R), sb("lo", [P, GROUP], F32R)
        c_x = sb("c_x", [P, TILES, CTX])
        c_t = sb("c_t", [P, 2, GROUP])
        c_hi, c_lo = sb("c_hi", [P, 2, GROUP], F32R), sb("c_lo", [P, 2, GROUP], F32R)
        queries = sb("queries", [P, 2, GROUP])
        keys = sb("keys", [P, 2, GROUP])
        diagonal = [sb(f"diagonal{i}", [P, 4, 4, 64]) for i in range(2)]
        values = sb("values", [P, TILES, HEADS, 32])
        outs = sb("outs", [P, 2, GROUP])
        arrived, c_arrived = sem("arrived"), sem("c_arrived")
        spread = sem("spread")
        turned = sem("turned")
        rounded = sem("rounded")
        split = sem("split")
        c_split = sem("c_split")
        c_kept = sem("c_kept")
        q_out, q_in = sem("q_out"), sem("q_in")
        k_out, k_in = sem("k_out"), sem("k_in")
        v_out, v_in = sem("v_out"), sem("v_in")
        masked_v, masked_g = sem("masked_v"), sem("masked_g")
        zeros = sem("zeros")
        o_in = sem("o_in")

        def diagonal_keys(engine, g, u):
            tp, q = pair_and_quad(u)
            g2, u2 = back(g, u, 2)
            engine.wait_ge(k_in, 2 * g + (1 if u < 8 else 2))
            if real(g2):
                engine.wait_ge(sm.scored, g2 * UNITS + u2 + 1)
            seqs = keys[:, q // 4, tp * pair:(tp + 1) * pair].rearrange("p (b j) -> p b j", j=64)
            engine.tensor_tensor(diagonal[u % 2][:], seqs.unsqueeze(2).broadcast_to([P, 4, 4, 64]),
                                 mask_sb[:, q, :].unsqueeze(1).unsqueeze(3).broadcast_to([P, 4, 4, 64]),
                                 ALU.mult).then_inc(masked_g if u in pools else masked_v, 1)

        block = ctx.enter_context(nc.Block())

        @block.sync
        def _(sp):
            def load(g):
                if real(g - 1):
                    sp.wait_ge(spread, 2 * g)
                sp.dma_start(x[:], x_in[g]).then_inc(arrived, 16)
                if real(g - 1):
                    sp.wait_ge(turned, 4 * g)
                sp.dma_start(c_x[:], ctx_in[g]).then_inc(c_arrived, 16)

            def body(g, front, tail, ahead):
                if isinstance(g, int) and g == 0:
                    load(0)
                    loads.plain_loads(sp, plain)
                if ahead:
                    load(g + 1)
                if isinstance(g, int) and g == GROUPS - 1:
                    ln.load(sp, x_out, GROUPS, 0)
                if tail:
                    ln.store(sp, x_out, g - 1)
                if front:
                    ln.load_again(sp, x_in, g)

            over_groups(sp, body)

        @block.gpsimd
        def _(pool):
            ln.constants(pool)
            pool.memset(values[:], 0.0).then_inc(zeros, 1)
            pool.wait_ge(loads.loaded, loaded)

            def context_lo(g, c):
                pool.wait_ge(rounded, 4 * g + 3 + c)
                pool.wait_ge(c_kept, 2 * g + 1 + c)
                pool.tensor_tensor(c_lo[:, c, :], c_t[:, c, :], c_hi[:, c, :].bitcast(F32), ALU.subtract)\
                    .then_inc(c_split, 1)

            def body(g, front, tail, ahead):
                if isinstance(g, int) and g == 0:
                    context_lo(0, 0)
                    context_lo(0, 1)
                for s in range(UNITS):
                    if s in (7, 8) and ahead:
                        context_lo(g + 1, s - 7)
                    if front and s + 1 in pools:
                        diagonal_keys(pool, g, s + 1)
                    if front if s >= 2 else tail:
                        sm.normalise(pool, *back(g, s, 2))
                    if s == 2 and tail:
                        ln.residual(pool, g - 1)
                    if isinstance(g, int) and g == GROUPS - 1 and s == 4:
                        ln.inverse_root(pool, GROUPS)
                    if isinstance(g, int) and g == GROUPS - 1 and s == 7:
                        ln.affine(pool, GROUPS)

            over_groups(pool, body)

        @block.scalar
        def _(act):
            def spread_x(g):
                act.wait_ge(arrived, 16 * (g + 1))
                if real(g - 1):
                    act.wait_ge(turned, 4 * (g - 1) + 2)
                act.activation(xn[:, :, 0:P], x[:, :, 0:P], ACT.Copy).then_inc(spread, 1)
                act.activation(xn[:, :, P:2 * P].rearrange("p t (c r) -> p t c r", c=COPIES),
                                 x[:, :, P:DIM].unsqueeze(2).broadcast_to([P, TILES, COPIES, REM]), ACT.Copy).then_inc(spread, 1)

            def round_hi(g, part):
                act.wait_ge(turned, 4 * g + part + 1)
                if part < 2:
                    act.activation(hi[:, part, :], sm.proj[part][:], ACT.Copy).then_inc(rounded, 1)
                else:
                    act.activation(c_hi[:, part - 2, :], sm.proj[part - 2][:], ACT.Copy).then_inc(rounded, 1)
                    act.activation(c_t[:, part - 2, :], sm.proj[part - 2][:], ACT.Copy).then_inc(c_kept, 1)

            def values_in(g, tp):
                act.wait_ge(v_out, 2 * g + tp + 1)
                if isinstance(g, int) and g == 0:
                    act.wait_ge(zeros, 1)
                else:
                    act.wait_ge(sm.valued, g * UNITS)
                for h in range(4):
                    last = act.activation(
                        values[:, 2 * tp:2 * tp + 2, h::4, 8 * h:8 * h + 8],
                        sm.proj[tp][:, 0:2 * DIM].rearrange("p (t q h d) -> p t q h d", t=2, h=4, d=8)[:, :, :, h, :],
                        ACT.Copy)
                    last.then_inc(v_in, 1)

            def queries_in(g, c):
                act.wait_ge(q_out, 2 * g + c + 1)
                if real(g - 1):
                    act.wait_ge(sm.scored, (g - 1) * UNITS + 8 + 2 * c)
                act.activation(queries[:, c, :], sm.proj[0][:], ACT.Copy).then_inc(q_in, 1)

            def keys_in(g, c):
                act.wait_ge(k_out, 2 * g + c + 1)
                if real(g - 1):
                    act.wait_ge(masked_v, masked_before(g - 1, 8 + 2 * c, False))
                    act.wait_ge(masked_g, masked_before(g - 1, 8 + 2 * c, True))
                act.activation(keys[:, c, :], sm.proj[1][:], ACT.Copy).then_inc(k_in, 1)

            def body(g, front, tail, ahead):
                if isinstance(g, int) and g == 0:
                    own.round_hi(act, 0)
                    spread_x(0)
                    round_hi(0, 0)
                    round_hi(0, 1)
                    own.round_hi(act, 1)
                    round_hi(0, 2)
                    round_hi(0, 3)
                    for n in range(2, len(own.jobs)):
                        own.round_hi(act, n)
                    queries_in(0, 0)
                    keys_in(0, 0)
                for s in range(UNITS):
                    if s == 4 and ahead:
                        spread_x(g + 1)
                    if s == 5 and front:
                        values_in(g, 1)
                    if front if s >= 4 else tail:
                        sm.copy_both(act, *back(g, s, 4))
                    if front if s >= 1 else tail:
                        sm.exponential(act, *back(g, s, 1), 8 ** -0.5)
                    if s in (5, 6) and ahead:
                        round_hi(g + 1, 2 * (s - 5))
                        round_hi(g + 1, 2 * (s - 5) + 1)
                    if s == 1 and front:
                        queries_in(g, 1)
                    if s == 2 and front:
                        keys_in(g, 1)
                    if s == 8 and ahead:
                        queries_in(g + 1, 0)
                        keys_in(g + 1, 0)
                    if s == 4 and front:
                        values_in(g, 0)
                    for at, c in ((2, 0), (4, 1)):
                        if s == at and tail:
                            act.wait_ge(sm.valued, (g - 1) * UNITS + 8 + 2 * c)
                            if c == 0 and real(g - 2):
                                act.wait_ge(ln.multiplied, TILES * (g - 1))
                            act.activation(outs[:, c, :], sm.out[:], ACT.Copy).then_inc(o_in, 1)
                    splitter.at(g, s, lambda n: splitter.round_hi(act, n))

            over_groups(act, body)

        @block.vector
        def _(dve):
            sm.constants(dve)
            dve.wait_ge(loads.loaded, loaded)

            def rest_lo(g, part):
                dve.wait_ge(rounded, 4 * g + part + 1)
                if part == 0:
                    dve.tensor_tensor(lo[:], sm.proj[0][:], hi[:, 0, :].bitcast(F32), ALU.subtract).then_inc(split, 1)
                else:
                    dve.tensor_tensor(hi[64:P, 1, :], sm.proj[1][64:P, :], hi[64:P, 1, :].bitcast(F32),
                                      ALU.subtract).then_inc(split, 1)

            def body(g, front, tail, ahead):
                if isinstance(g, int) and g == 0:
                    own.rest_lo(dve, 0)
                    rest_lo(0, 0)
                    rest_lo(0, 1)
                    for n in range(1, len(own.jobs)):
                        own.rest_lo(dve, n)
                    diagonal_keys(dve, 0, 0)
                for s in range(UNITS):
                    if s == 6 and ahead:
                        rest_lo(g + 1, 1)
                    behind = front if s >= 2 else tail
                    if behind:
                        sm.add_up(dve, *back(g, s, 2))
                    if front if s >= 1 else tail:
                        sm.maximum(dve, *back(g, s, 1))
                    if behind:
                        sm.invert(dve, *back(g, s, 2))
                    if front if s >= 1 else tail:
                        sm.shift(dve, *back(g, s, 1))
                    if behind:
                        sm.make_factor(dve, *back(g, s, 2))
                    if s in out_steps and tail:
                        ln.add(dve, sm.y, g - 1, out_steps.index(s))
                    if isinstance(g, int) and g == GROUPS - 1 and s in (2, 3):
                        for t in (2 * (s - 2), 2 * (s - 2) + 1):
                            ln.statistics(dve, GROUPS, t)
                    if isinstance(g, int) and g == GROUPS - 1 and s in (5, 6):
                        for t in (2 * (s - 5), 2 * (s - 5) + 1):
                            ln.normalise(dve, GROUPS, t)
                    if front and s < 9 and s + 1 not in pools:
                        diagonal_keys(dve, g, s + 1)
                    if s == 5 and ahead:
                        rest_lo(g + 1, 0)
                    if s == 9 and ahead:
                        diagonal_keys(dve, g + 1, 0)
                    splitter.at(g, s, lambda n: splitter.rest_lo(dve, n), behind=1)

            over_groups(dve, body)

        @block.tensor
        def _(pe):
            def turn(g, part):
                bank = sm.proj[part % 2]
                if part < 2:
                    pe.wait_ge(spread, 2 * g + 2)
                    if real(g - 1):
                        pe.wait_ge(v_in, 8 * g)
                else:
                    pe.wait_ge(c_arrived, 16 * (g + 1))
                    pe.wait_ge(split, 2 * g + part - 1)
                for t in range(TILES):
                    cols = slice((part % 2) * P, (part % 2 + 1) * P)
                    source = xn[:, t, cols] if part < 2 else c_x[:, t, cols]
                    last = pe.transpose(bank[:, t * P:(t + 1) * P], source, identity[:])
                last.then_inc(turned, 1)

            def project_queries(g, c):
                cols = slice(c * P, (c + 1) * P)
                if c == 0:
                    pe.wait_ge(split, 2 * g + 2)
                    pe.wait_ge(c_kept, 2 * g + 1)
                else:
                    pe.wait_ge(q_in, 2 * g + 1)
                parts = [(q_hi[:, 0, cols], hi[:, 0, :]), (q_lo[:, 0, cols], hi[:, 0, :]),
                         (q_hi[:, 0, cols], lo[:]), (q_rem[:, cols], hi[:, 1, :])]
                for n, (w, moving) in enumerate(parts):
                    last = pe.matmul(sm.proj[0][:], w, moving, start=n == 0, stop=n == len(parts) - 1)
                last.then_inc(q_out, 1)

            def project_keys(g, c):
                cols = slice(c * P, (c + 1) * P)
                if c == 0:
                    pe.wait_ge(c_split, 2 * g + 2)
                    pe.wait_ge(c_kept, 2 * g + 2)
                else:
                    pe.wait_ge(k_in, 2 * g + 1)
                parts = [(w[:, k, cols], m[:, k, :]) for w, m in ((k_hi, c_hi), (k_lo, c_hi), (k_hi, c_lo))
                         for k in range(2)]
                for n, (w, moving) in enumerate(parts):
                    last = pe.matmul(sm.proj[1][:], w, moving, start=n == 0, stop=n == len(parts) - 1)
                last.then_inc(k_out, 1)

            def project_values(g, tp):
                pe.wait_ge(k_in if tp else q_in, 2 * g + 2)
                for i in range(2):
                    t = 2 * tp + i
                    for c in range(2):
                        last = pe.matmul(sm.proj[tp][:, i * DIM:(i + 1) * DIM], c_t[:, c, t * P:(t + 1) * P],
                                         wv_sb[:, c, :], start=c == 0, stop=c == 1)
                last.then_inc(v_out, 1)

            def score(g, u):
                tp, q = pair_and_quad(u)
                g2, u2 = back(g, u, 2)
                if u in (0, 8):
                    pe.wait_ge(q_in, 2 * g + (1 if u == 0 else 2))
                pe.wait_ge(masked_g if u in pools else masked_v, masked_before(g, u + 1, u in pools))
                if real(g2):
                    pe.wait_ge(sm.shifted, g2 * UNITS + u2 + 1)
                for i in range(2):
                    for b in range(2):
                        first = (2 * tp + i) * P + b * 64
                        last = pe.matmul(sm.scores[u % 2][b * 64:(b + 1) * 64, i * 256:(i + 1) * 256],
                                         queries[:, q // 4, first:first + 64],
                                         diagonal[u % 2][:, 2 * i + b, :, :], start=True, stop=True)
                last.then_inc(sm.scored, 1)

            def times_values(g, u):
                tp, q = pair_and_quad(u)
                pe.wait_ge(sm.copied_a, g * UNITS + u + 1)
                pe.wait_ge(sm.copied_b, g * UNITS + u + 1)
                if u in (0, 4):
                    pe.wait_ge(v_in, 8 * g + 4 + u)
                if u == 8 or (u == 0 and real(g - 1)):
                    pe.wait_ge(o_in, 2 * g + u // 8)
                col = tp * pair
                for i in range(2):
                    for h in range(4):
                        head = 4 * h + q if q < 4 else 16 + h
                        last = pe.matmul(sm.out[32 * h:32 * h + 32, col + i * P:col + (i + 1) * P],
                                         values[:, 2 * tp + i, head, :], sm.probT[u % 2][:, 4 * i + h, :],
                                         start=u in (0, 8) and i == 0, stop=q >= 3, skip_group_check=True)
                last.then_inc(sm.valued, 1)

            def project_out(g, t):
                pe.wait_ge(o_in, 2 * g + 2)
                if t > 0 or real(g - 1):
                    pe.wait_ge(ln.added, TILES * g + t)
                for c in range(2):
                    last = pe.matmul(sm.y[:, 0:DIM], outs[:, c, t * P:(t + 1) * P], wo_sb[:, c, :],
                                     start=c == 0, stop=c == 1)
                last.then_inc(ln.multiplied, 1)

            def body(g, front, tail, ahead):
                if isinstance(g, int) and g == 0:
                    pe.wait_ge(loads.loaded, loaded)
                    for part in range(4):
                        turn(0, part)
                    pe.wait_ge(loads.split, own.first + 2)
                    project_queries(0, 0)
                    pe.wait_ge(loads.split, own.first + len(own.jobs))
                    project_keys(0, 0)
                for s in range(UNITS):
                    if front if s >= 1 else tail:
                        score(*back(g, s, 1))
                    if front if s >= 4 else tail:
                        sm.transpose(pe, identity, *back(g, s, 4))
                    if s in out_steps and tail:
                        project_out(g - 1, out_steps.index(s))
                    if s in (5, 6) and ahead:
                        turn(g + 1, 2 * (s - 5))
                        turn(g + 1, 2 * (s - 5) + 1)
                    if front if s >= 5 else tail:
                        times_values(*back(g, s, 5))
                    if s == 1 and front:
                        project_queries(g, 1)
                    if s == 2 and front:
                        project_keys(g, 1)
                    if s in (3, 4) and front:
                        project_values(g, s - 3)
                    if s == 7 and ahead:
                        project_queries(g + 1, 0)
                    if s == 8 and ahead:
                        project_keys(g + 1, 0)

            over_groups(pe, body)


def build(nc, a, out):
    with ExitStack() as ctx, ExitStack() as self_ctx, ExitStack() as ff_ctx, ExitStack() as cross_ctx:
        identity = ctx.enter_context(nc.sbuf_tensor("identity_sb", [P, P], F32))
        loads = Loads(nc)
        x1, x2, x3 = (nc.dram_tensor(f"x{n}", [TOKENS, DIM], F32).ap() for n in (1, 2, 3))
        ln = Norm(nc, ctx, "ln")
        self_w = Weights(nc, self_ctx, "self", "right", [(a["a1_wq"], 1), (a["a1_wk"], 1), (a["a1_wv"], 1)])
        with ExitStack() as ip_ctx:
            ip_w = Weights(nc, ip_ctx, "ip", "left", [(a["ip_wq"], 1), (a["ip_wk"], 0)])
            ip_attention(nc, "ip", loads, ln, ip_w, self_w, a["x"], a["ctx"], x1, identity, a["identity"], a["mask"],
                         a["ip_wv"], a["ip_wo"], a["ip_bo"], ln.vectors(1, a["ln1_g"], a["ln1_b"]))
        cross_w = Weights(nc, cross_ctx, "cross", "left", [(a["a2_wq"], 1), (a["a2_wk"], 0), (a["a2_wv"], 0)])
        attention(nc, "self", loads, ln, self_w, cross_w, x1, None, x2, identity, a["a1_wo"], a["a1_bo"],
                  ln.vectors(2, a["ln2_g"], a["ln2_b"]))
        self_ctx.close()
        ff_w = Weights(nc, ff_ctx, "ff", "right", [(a["ff_w1"], 1)])
        w2 = ff_ctx.enter_context(nc.sbuf_tensor("ff_w2_sb", [P, FF_CHUNKS, DIM], F32, side="right"))
        b1 = ff_ctx.enter_context(nc.sbuf_tensor("ff_b1_sb", [P, 2 * FF_CHUNKS], F32, side="right"))
        ff_loads = [(b1[:], a["ff_b1"]), (w2[:], a["ff_w2"].rearrange("(c p) n -> p c n", p=P))]
        attention(nc, "cross", loads, ln, cross_w, ff_w, x2, a["ctx"], x3, identity, a["a2_wo"], a["a2_bo"],
                  ln.vectors(3, a["ln3_g"], a["ln3_b"]) + ff_loads)
        cross_ctx.close()
        feed_forward(nc, "ff", loads, ln, ff_w, x3, out, identity, b1, w2, a["ff_b2"])


def layout(inputs):
    def padded(w, rows, cols):
        out = np.zeros((rows, cols), w.dtype)
        out[:w.shape[0], :w.shape[1]] = w
        return out

    def stacked(w):
        return np.concatenate([w[:P]] + [w[P:]] * COPIES)

    get = {k: np.asarray(v) for k, v in inputs.items()}
    a = {"x": get["x"].reshape(TOKENS, DIM), "ctx": get["ctx_2048"].reshape(TOKENS, CTX)}
    a["ip_wq"] = stacked(padded(get["L0_xattn_Wq"].T, DIM, 2 * P))
    a["ip_wk"] = padded(get["L0_xattn_Wk"].T, CTX, 2 * P)
    a["ip_wv"] = get["L0_xattn_Wv"].T
    wo = get["L0_xattn_Wo"].T
    a["ip_wo"] = padded(wo[:P], 2 * P, DIM)
    for h in range(4):
        a["ip_wo"][P + 40 * h:P + 40 * h + 8] = wo[P + 8 * h:P + 8 * h + 8]
    a["ip_bo"] = get["L0_xattn_bo"]
    for n in ("a1_wq", "a1_wk", "a1_wv", "a2_wq", "ff_w1"):
        a[n] = stacked(get["L1_xattn_" + n])
    for n in ("a1_wo", "a1_bo", "a2_wk", "a2_wv", "a2_wo", "a2_bo", "ff_w2", "ff_b2", "ln1_g", "ln1_b", "ln2_g", "ln2_b", "ln3_g", "ln3_b"):
        a[n] = get["L1_xattn_" + n]
    a["ff_b1"] = get["L1_xattn_ff_b1"].reshape(2 * FF_CHUNKS, P).T
    a["identity"] = np.eye(P, dtype=np.float32)
    head = np.stack([4 * np.arange(4) + q for q in range(4)] + [np.arange(4)])
    a["mask"] = (np.arange(P)[:, None, None] // 8 == head).astype(np.float32)
    return {k: np.ascontiguousarray(v) for k, v in a.items()}


def kernel(**inputs):
    import concourse.bacc as bacc
    from concourse.bass_utils import run_bass_kernel_spmd

    nc = bacc.Bacc("TRN2", target_bir_lowering=False, num_devices=1)
    arrays = {f"in_{k}": v for k, v in layout(inputs).items()}
    a = {k[3:]: nc.dram_tensor(k, v.shape, mybir.dt.from_np(v.dtype), kind="ExternalInput").ap()
         for k, v in arrays.items()}
    out = nc.dram_tensor("out", [TOKENS, DIM], F32, kind="ExternalOutput").ap()
    build(nc, a, out)
    got = run_bass_kernel_spmd(nc, [arrays], core_ids=[0])
    return got.results[0]["out"].reshape(SEQS, SEQ, DIM)
```
